# Optimizing a Trainium2 kernel written in Bass

```python
import numpy as np
import jax
import jax.numpy as jnp

def _softmax(x, axis=-1):
    return jax.nn.softmax(x, axis=axis)

def _gelu(x):
    return jax.nn.gelu(x, approximate=True)

def _silu(x):
    return jax.nn.silu(x)

def _sigmoid(x):
    return jax.nn.sigmoid(x)

def _layernorm(x, axis=-1, eps=1e-05):
    m = jnp.mean(x, axis=axis, keepdims=True)
    v = jnp.var(x, axis=axis, keepdims=True)
    return (x - m) / jnp.sqrt(v + eps)

def _scatter_add(tgt, idx, src, axis=0):
    return tgt.at[idx].add(src)

def _segment_sum(src, seg, n):
    return jax.ops.segment_sum(src, seg, n)
kernel_name = 'mk_recurrent_d2_jaxref_r4_d43df7'

def setup_inputs(seed: int=0):
    np.random.seed(seed)
    _w = jnp.asarray

    def _L0_attn_setup():
        import jax, jax.numpy as jnp
        import numpy as np
        B, T, C = (4, 1024, 256)

        def wkv_scan(k, v, w, u):
            Bb, Tt, Cc = k.shape
            k_t = jnp.transpose(k, (1, 0, 2))
            v_t = jnp.transpose(v, (1, 0, 2))
            num0 = jnp.zeros((Bb, Cc), dtype=jnp.float32)
            den0 = jnp.zeros((Bb, Cc), dtype=jnp.float32)
            max0 = jnp.full((Bb, Cc), -1e+38, dtype=jnp.float32)

            def step(carry, kv):
                num, den, m = carry
                kk, vv = kv
                mo = jnp.maximum(m, kk + u)
                e1 = jnp.exp(m - mo)
                e2 = jnp.exp(kk + u - mo)
                out = (e1 * num + e2 * vv) / (e1 * den + e2)
                ms = jnp.maximum(m + w, kk)
                e1s = jnp.exp(m + w - ms)
                e2s = jnp.exp(kk - ms)
                return ((e1s * num + e2s * vv, e1s * den + e2s, ms), out)
            _, outs = jax.lax.scan(step, (num0, den0, max0), (k_t, v_t))
            return jnp.transpose(outs, (1, 0, 2))
        key = jax.random.key(seed)
        ks = jax.random.split(key, 10)
        x = jax.random.normal(ks[0], (B, T, C), dtype=jnp.float32)
        Wk = jax.random.normal(ks[1], (C, C), dtype=jnp.float32) * C ** (-0.5)
        Wv = jax.random.normal(ks[2], (C, C), dtype=jnp.float32) * C ** (-0.5)
        Wr = jax.random.normal(ks[3], (C, C), dtype=jnp.float32) * C ** (-0.5)
        Wo = jax.random.normal(ks[4], (C, C), dtype=jnp.float32) * C ** (-0.5)
        time_decay = jax.random.uniform(ks[5], (C,), minval=-6.0, maxval=-5.0, dtype=jnp.float32)
        time_first = jax.random.uniform(ks[6], (C,), minval=-3.0, maxval=0.0, dtype=jnp.float32)
        mix_k = jax.random.uniform(ks[7], (1, 1, C), dtype=jnp.float32)
        mix_v = jax.random.uniform(ks[8], (1, 1, C), dtype=jnp.float32)
        mix_r = jax.random.uniform(ks[9], (1, 1, C), dtype=jnp.float32)
        return {'x': x, 'Wk': Wk, 'Wv': Wv, 'Wr': Wr, 'Wo': Wo, 'time_decay': time_decay, 'time_first': time_first, 'mix_k': mix_k, 'mix_v': mix_v, 'mix_r': mix_r}
    _L0_attn_in = _L0_attn_setup()

    def _L0_ffn_setup():
        import jax, jax.numpy as jnp
        import numpy as np
        HIDDEN = 256
        INTER = 1024
        key = jax.random.key(seed)
        k1, k2, k3, k4, k5 = jax.random.split(key, 5)
        hidden_states = jax.random.normal(k1, (4, 512, HIDDEN), dtype=jnp.float32)
        W1 = jax.random.normal(k2, (HIDDEN, INTER), dtype=jnp.float32) * (1.0 / np.sqrt(HIDDEN))
        b1 = jax.random.normal(k3, (INTER,), dtype=jnp.float32) * 0.02
        W2 = jax.random.normal(k4, (INTER, HIDDEN), dtype=jnp.float32) * (1.0 / np.sqrt(INTER))
        b2 = jax.random.normal(k5, (HIDDEN,), dtype=jnp.float32) * 0.02
        return {'hidden_states': hidden_states, 'W1': W1, 'b1': b1, 'W2': W2, 'b2': b2}
    _L0_ffn_in = _L0_ffn_setup()

    def _L1_attn_setup():
        import jax, jax.numpy as jnp
        import numpy as np
        D_MODEL, N_HEADS = (256, 16)
        D_H = D_MODEL // N_HEADS
        D_HR = D_H // 2
        D_LATENT = 64
        THETA = 10000.0

        def rope(x, theta=THETA):
            S, d = (x.shape[-2], x.shape[-1])
            inv = theta ** (-jnp.arange(0, d, 2, dtype=jnp.float32) / d)
            ang = jnp.arange(S, dtype=jnp.float32)[:, None] * inv
            cos, sin = (jnp.cos(ang), jnp.sin(ang))
            x1, x2 = (x[..., 0::2], x[..., 1::2])
            r1 = x1 * cos - x2 * sin
            r2 = x1 * sin + x2 * cos
            return jnp.stack([r1, r2], axis=-1).reshape(x.shape)
        key = jax.random.key(seed)
        ks = jax.random.split(key, 9)
        s = lambda fan_in: 1.0 / np.sqrt(fan_in)
        return {'x': jax.random.normal(ks[0], (4, 512, D_MODEL), jnp.float32), 'W_DQ': jax.random.normal(ks[1], (D_MODEL, D_LATENT), jnp.float32) * s(D_MODEL), 'W_UQ': jax.random.normal(ks[2], (D_LATENT, N_HEADS * D_H), jnp.float32) * s(D_LATENT), 'W_QR': jax.random.normal(ks[3], (D_LATENT, N_HEADS * D_HR), jnp.float32) * s(D_LATENT), 'W_DKV': jax.random.normal(ks[4], (D_MODEL, D_LATENT), jnp.float32) * s(D_MODEL), 'W_UK': jax.random.normal(ks[5], (D_LATENT, N_HEADS * D_H), jnp.float32) * s(D_LATENT), 'W_UV': jax.random.normal(ks[6], (D_LATENT, N_HEADS * D_H), jnp.float32) * s(D_LATENT), 'W_KR': jax.random.normal(ks[7], (D_MODEL, D_HR), jnp.float32) * s(D_MODEL), 'W_O': jax.random.normal(ks[8], (N_HEADS * D_H, D_MODEL), jnp.float32) * s(N_HEADS * D_H)}
    _L1_attn_in = _L1_attn_setup()

    def _L1_ffn_setup():
        import jax, jax.numpy as jnp
        import numpy as np
        DIM = 256

        def _reference_tuple_inner(x, W_r, W_k, W_v, mu_r, mu_k):
            B, T, C = x.shape
            x_prev = jnp.concatenate([jnp.zeros((B, 1, C), x.dtype), x[:, :-1, :]], axis=1)
            xr = mu_r * x + (1.0 - mu_r) * x_prev
            xk = mu_k * x + (1.0 - mu_k) * x_prev
            r = jax.nn.sigmoid(jnp.einsum('btc,dc->btd', xr, W_r))
            k = jnp.einsum('btc,dc->btd', xk, W_k)
            k_act = jnp.square(jax.nn.relu(k))
            out = r * jnp.einsum('btc,dc->btd', k_act, W_v)
            new_state = x[:, -1, :]
            return (out, new_state)
        key = jax.random.key(seed)
        ks = jax.random.split(key, 6)
        B, T, C = (8, 512, DIM)
        x = jax.random.normal(ks[0], (B, T, C), dtype=jnp.float32)
        s = 1.0 / np.sqrt(C)
        W_r = jax.random.uniform(ks[1], (C, C), jnp.float32, -s, s)
        W_k = jax.random.uniform(ks[2], (C, C), jnp.float32, -s, s)
        W_v = jax.random.uniform(ks[3], (C, C), jnp.float32, -s, s)
        mu_r = jax.random.uniform(ks[4], (C,), jnp.float32)
        mu_k = jax.random.uniform(ks[5], (C,), jnp.float32)
        return {'x': x, 'W_r': W_r, 'W_k': W_k, 'W_v': W_v, 'mu_r': mu_r, 'mu_k': mu_k}
    _L1_ffn_in = _L1_ffn_setup()
    _d = {'L0_attn_x': _L0_attn_in['x'], 'L0_attn_Wk': _L0_attn_in['Wk'], 'L0_attn_Wv': _L0_attn_in['Wv'], 'L0_attn_Wr': _L0_attn_in['Wr'], 'L0_attn_Wo': _L0_attn_in['Wo'], 'L0_attn_time_decay': _L0_attn_in['time_decay'], 'L0_attn_time_first': _L0_attn_in['time_first'], 'L0_attn_mix_k': _L0_attn_in['mix_k'], 'L0_attn_mix_v': _L0_attn_in['mix_v'], 'L0_attn_mix_r': _L0_attn_in['mix_r'], 'L0_ffn_W1': _L0_ffn_in['W1'], 'L0_ffn_b1': _L0_ffn_in['b1'], 'L0_ffn_W2': _L0_ffn_in['W2'], 'L0_ffn_b2': _L0_ffn_in['b2'], 'L1_attn_W_DQ': _L1_attn_in['W_DQ'], 'L1_attn_W_UQ': _L1_attn_in['W_UQ'], 'L1_attn_W_QR': _L1_attn_in['W_QR'], 'L1_attn_W_DKV': _L1_attn_in['W_DKV'], 'L1_attn_W_UK': _L1_attn_in['W_UK'], 'L1_attn_W_UV': _L1_attn_in['W_UV'], 'L1_attn_W_KR': _L1_attn_in['W_KR'], 'L1_attn_W_O': _L1_attn_in['W_O'], 'L1_ffn_W_r': _L1_ffn_in['W_r'], 'L1_ffn_W_k': _L1_ffn_in['W_k'], 'L1_ffn_W_v': _L1_ffn_in['W_v'], 'L1_ffn_mu_r': _L1_ffn_in['mu_r'], 'L1_ffn_mu_k': _L1_ffn_in['mu_k']}
    _x0 = _d['L0_attn_x']
    _d['L0_attn_x'] = jax.random.normal(jax.random.fold_in(jax.random.key(seed), 1), (4, 2048, 256), dtype=_x0.dtype)
    del _x0
    return _d

def reference(L0_attn_x, L0_attn_Wk, L0_attn_Wv, L0_attn_Wr, L0_attn_Wo, L0_attn_time_decay, L0_attn_time_first, L0_attn_mix_k, L0_attn_mix_v, L0_attn_mix_r, L0_ffn_W1, L0_ffn_b1, L0_ffn_W2, L0_ffn_b2, L1_attn_W_DQ, L1_attn_W_UQ, L1_attn_W_QR, L1_attn_W_DKV, L1_attn_W_UK, L1_attn_W_UV, L1_attn_W_KR, L1_attn_W_O, L1_ffn_W_r, L1_ffn_W_k, L1_ffn_W_v, L1_ffn_mu_r, L1_ffn_mu_k):

    def _L0_attn_ref(x, Wk, Wv, Wr, Wo, time_decay, time_first, mix_k, mix_v, mix_r):
        import jax, jax.numpy as jnp
        import numpy as np
        B, T, C = (4, 1024, 256)

        def wkv_scan(k, v, w, u):
            Bb, Tt, Cc = k.shape
            k_t = jnp.transpose(k, (1, 0, 2))
            v_t = jnp.transpose(v, (1, 0, 2))
            num0 = jnp.zeros((Bb, Cc), dtype=jnp.float32)
            den0 = jnp.zeros((Bb, Cc), dtype=jnp.float32)
            max0 = jnp.full((Bb, Cc), -1e+38, dtype=jnp.float32)

            def step(carry, kv):
                num, den, m = carry
                kk, vv = kv
                mo = jnp.maximum(m, kk + u)
                e1 = jnp.exp(m - mo)
                e2 = jnp.exp(kk + u - mo)
                out = (e1 * num + e2 * vv) / (e1 * den + e2)
                ms = jnp.maximum(m + w, kk)
                e1s = jnp.exp(m + w - ms)
                e2s = jnp.exp(kk - ms)
                return ((e1s * num + e2s * vv, e1s * den + e2s, ms), out)
            _, outs = jax.lax.scan(step, (num0, den0, max0), (k_t, v_t))
            return jnp.transpose(outs, (1, 0, 2))
        prev_x = jnp.pad(x, ((0, 0), (1, 0), (0, 0)))[:, :-1, :]
        r_in = x * mix_r + prev_x * (1.0 - mix_r)
        k_in = x * mix_k + prev_x * (1.0 - mix_k)
        v_in = x * mix_v + prev_x * (1.0 - mix_v)
        receptance = jnp.einsum('btc,dc->btd', r_in, Wr)
        key = jnp.einsum('btc,dc->btd', k_in, Wk)
        value = jnp.einsum('btc,dc->btd', v_in, Wv)
        w = -jnp.exp(time_decay)
        u = time_first
        wkv_out = wkv_scan(key, value, w, u)
        rwkv = jax.nn.sigmoid(receptance) * wkv_out
        return jnp.einsum('btc,dc->btd', rwkv, Wo)

    def _L0_ffn_ref(hidden_states, W1, b1, W2, b2):
        import jax, jax.numpy as jnp
        import numpy as np
        HIDDEN = 256
        INTER = 1024
        h = jax.nn.relu(jnp.einsum('bsh,hi->bsi', hidden_states, W1) + b1)
        return jnp.einsum('bsi,ih->bsh', h, W2) + b2

    def _L1_attn_ref(x, W_DQ, W_UQ, W_QR, W_DKV, W_UK, W_UV, W_KR, W_O):
        import jax, jax.numpy as jnp
        import numpy as np
        D_MODEL, N_HEADS = (256, 16)
        D_H = D_MODEL // N_HEADS
        D_HR = D_H // 2
        D_LATENT = 64
        THETA = 10000.0

        def rope(x, theta=THETA):
            S, d = (x.shape[-2], x.shape[-1])
            inv = theta ** (-jnp.arange(0, d, 2, dtype=jnp.float32) / d)
            ang = jnp.arange(S, dtype=jnp.float32)[:, None] * inv
            cos, sin = (jnp.cos(ang), jnp.sin(ang))
            x1, x2 = (x[..., 0::2], x[..., 1::2])
            r1 = x1 * cos - x2 * sin
            r2 = x1 * sin + x2 * cos
            return jnp.stack([r1, r2], axis=-1).reshape(x.shape)
        B, S, _ = x.shape
        d_qk = D_H + D_HR
        c_q = x @ W_DQ
        Qc = (c_q @ W_UQ).reshape(B, S, N_HEADS, D_H).transpose(0, 2, 1, 3)
        Qr = (c_q @ W_QR).reshape(B, S, N_HEADS, D_HR).transpose(0, 2, 1, 3)
        Qr = rope(Qr)
        c_kv = x @ W_DKV
        Kc = (c_kv @ W_UK).reshape(B, S, N_HEADS, D_H).transpose(0, 2, 1, 3)
        Kr = rope((x @ W_KR)[:, None, :, :])
        Kr = jnp.broadcast_to(Kr, (B, N_HEADS, S, D_HR))
        V = (c_kv @ W_UV).reshape(B, S, N_HEADS, D_H).transpose(0, 2, 1, 3)
        Q = jnp.concatenate([Qc, Qr], axis=-1)
        K = jnp.concatenate([Kc, Kr], axis=-1)
        scores = jnp.einsum('bhqd,bhkd->bhqk', Q, K)
        scores = jnp.clip(scores, -80.0, 80.0)
        causal = jnp.tril(jnp.ones((S, S), dtype=bool))
        scores = jnp.where(causal, scores, -jnp.inf)
        weights = jax.nn.softmax(scores / jnp.sqrt(jnp.float32(d_qk)), axis=-1)
        attn = jnp.einsum('bhqk,bhkd->bhqd', weights, V)
        attn = attn.transpose(0, 2, 1, 3).reshape(B, S, N_HEADS * D_H)
        return attn @ W_O

    def _L1_ffn_ref(x, W_r, W_k, W_v, mu_r, mu_k):
        import jax, jax.numpy as jnp
        import numpy as np
        DIM = 256

        def _reference_tuple_inner(x, W_r, W_k, W_v, mu_r, mu_k):
            B, T, C = x.shape
            x_prev = jnp.concatenate([jnp.zeros((B, 1, C), x.dtype), x[:, :-1, :]], axis=1)
            xr = mu_r * x + (1.0 - mu_r) * x_prev
            xk = mu_k * x + (1.0 - mu_k) * x_prev
            r = jax.nn.sigmoid(jnp.einsum('btc,dc->btd', xr, W_r))
            k = jnp.einsum('btc,dc->btd', xk, W_k)
            k_act = jnp.square(jax.nn.relu(k))
            out = r * jnp.einsum('btc,dc->btd', k_act, W_v)
            new_state = x[:, -1, :]
            return (out, new_state)
        return _reference_tuple_inner(x, W_r, W_k, W_v, mu_r, mu_k)[0]
    x = L0_attn_x
    xn = _layernorm(x, axis=-1)
    s = _L0_attn_ref(xn, L0_attn_Wk, L0_attn_Wv, L0_attn_Wr, L0_attn_Wo, L0_attn_time_decay, L0_attn_time_first, L0_attn_mix_k, L0_attn_mix_v, L0_attn_mix_r)
    g = _silu(_L0_ffn_ref(xn, L0_ffn_W1, L0_ffn_b1, L0_ffn_W2, L0_ffn_b2))
    x = x + s * g
    xn = _layernorm(x, axis=-1)
    s = _L1_attn_ref(xn, L1_attn_W_DQ, L1_attn_W_UQ, L1_attn_W_QR, L1_attn_W_DKV, L1_attn_W_UK, L1_attn_W_UV, L1_attn_W_KR, L1_attn_W_O)
    g = _silu(_L1_ffn_ref(xn, L1_ffn_W_r, L1_ffn_W_k, L1_ffn_W_v, L1_ffn_mu_r, L1_ffn_mu_k))
    x = x + s * g
    return x

_drawn_inputs = setup_inputs


def setup_inputs(seed=0):
    import zlib

    import numpy as np

    out = dict(_drawn_inputs(seed))
    spreads = {}
    factors = {}
    for name, (base, spread) in spreads.items():
        noise = np.random.default_rng([zlib.crc32(name.encode()), seed]).standard_normal(out[name].shape)
        drawn = base * np.exp(spread * noise) if base else spread * noise
        out[name] = jnp.asarray(drawn.astype(out[name].dtype))
    for name, factor in factors.items():
        out[name] = (out[name] * factor).astype(out[name].dtype)
    return out
```

```python
from contextlib import ExitStack

import numpy as np
import concourse.bass as bass
import concourse.mybir as mybir

F32 = mybir.dt.float32
F16 = mybir.dt.float16
I32 = mybir.dt.int32
ALU = mybir.AluOpType
ACT = mybir.ActivationFunctionType

P = 128
BATCH, SEQ, DIM = 4, 2048, 256
TOKENS = BATCH * SEQ
KT = DIM // P
CH = 512
NCH = TOKENS // CH
CPB = SEQ // CH
TPC = CH // P
TILES = TOKENS // P
INTER = 1024
MT = INTER // P
HEADS, D_H, D_R, LATENT = 16, 16, 8, 64
D_QK = D_H + D_R
GH = 4
GROUPS = HEADS // GH
VW = 32
KROWS = 4 * D_QK
KEYT = SEQ // P
LN_EPS = 1e-5
MAX_INIT = -1e38
EXP_CAP = 30.0
CLIP = 80.0
INV_SQRT = float(1.0 / np.sqrt(np.float32(D_QK)))
P_MAX = float(np.exp(CLIP * INV_SQRT))
P_MIN = float(np.exp(-CLIP * INV_SQRT))
F16_TARGET = 16384.0


def layer0(nc, a, x1_d):
    with ExitStack() as ctx:
        def sb(name, shape, dt=F32):
            return ctx.enter_context(nc.sbuf_tensor(name, shape, dt))

        def sem(name):
            return ctx.enter_context(nc.semaphore(name))

        x = sb("a_x", [P, 2, TPC, DIM])
        ident = sb("a_ident", [P, P])
        w_r, w_k, w_v, w_o = (sb(f"a_w{n}", [P, KT, DIM]) for n in "rkvo")
        w_1 = sb("a_w1", [P, KT, INTER])
        w_2 = sb("a_w2", [P, MT, DIM])
        b_1 = sb("a_b1", [P, MT])
        b_2 = sb("a_b2", [P, DIM])
        mixes = sb("a_mixes", [P, 3, KT])
        decay = sb("a_decay", [P, KT])
        first = sb("a_first", [P, KT])
        zero_col = sb("a_zero", [P, KT, 1])
        eps = sb("a_eps", [P, TPC])
        half = sb("a_half", [P, TPC])
        stats = sb("a_stats", [P, TPC, 6])
        mv = sb("a_mv", [P, TPC, 2])
        var_eps = sb("a_var", [P, TPC])
        rstd = sb("a_rstd", [P, TPC])
        xhat = sb("a_xhat", [P, TPC, DIM])
        xn = sb("a_xn", [P, 2, KT, CH + 1])
        diff = sb("a_diff", [P, KT, CH])
        x_r, x_k, x_v = (sb(f"a_x{n}", [P, KT, CH]) for n in "rkv")
        sig_r = sb("a_sigr", [P, KT, CH])
        mx = sb("a_mx", [P, KT, CH + 1])
        num = sb("a_num", [P, KT, CH + 1])
        den = sb("a_den", [P, KT, CH + 1])
        dist = sb("a_dist", [P, KT, CH])
        e_bonus = sb("a_eb", [P, KT, CH])
        e_old = sb("a_eo", [P, KT, CH])
        e_new = sb("a_en", [P, KT, CH])
        new_v = sb("a_nv", [P, KT, CH])
        out_num = sb("a_on", [P, KT, CH])
        out_den = sb("a_od", [P, KT, CH])
        rwkv = sb("a_rwkv", [P, KT, CH])
        hid = sb("a_hid", [P, MT, CH])
        gate_in = sb("a_gi", [P, TPC, DIM])
        gate_sig = sb("a_gs", [P, TPC, DIM])
        gate = sb("a_gate", [P, TPC, DIM])
        prod = sb("a_prod", [P, TPC, DIM])
        x1 = sb("a_x1", [P, 2, TPC, DIM])

        ps_a = ctx.enter_context(nc.psum_tensor("a_ps0", [P, 2, CH], F32))
        ps_b = ctx.enter_context(nc.psum_tensor("a_ps1", [P, 2, CH], F32))
        ps_c = ctx.enter_context(nc.psum_tensor("a_ps2", [P, 2, CH], F32))
        ps_t = ctx.enter_context(nc.psum_tensor("a_ps3", [P, 2, CH], F32))
        ps_ffn = ps_b[:].rearrange("p a (j d) -> p (a j) d", d=DIM)
        ps_out = ps_c[:].rearrange("p a (j d) -> p (a j) d", d=DIM)

        weights_loaded = sem("a_weights_loaded")
        ffn_loaded = sem("a_ffn_loaded")
        small_loaded = sem("a_small_loaded")
        x_loaded = [sem(f"a_x_loaded{i}") for i in range(2)]
        x1_stored = [sem(f"a_x1_stored{i}") for i in range(2)]
        consts_set = sem("a_consts_set")
        decay_exp = sem("a_decay_exp")
        decay_set = sem("a_decay_set")
        stats_done = sem("a_stats_done")
        mv_done = sem("a_mv_done")
        var_done = sem("a_var_done")
        rstd_done = sem("a_rstd_done")
        xhat_done = sem("a_xhat_done")
        xt_done = sem("a_xt_done")
        xn_done = sem("a_xn_done")
        diff_done = sem("a_diff_done")
        mix_done = sem("a_mix_done")
        r_done = sem("a_r_done")
        k_done = sem("a_k_done")
        v_done = sem("a_v_done")
        hid_mm = sem("a_hid_mm")
        hid_done = sem("a_hid_done")
        ffn_done = sem("a_ffn_done")
        out_done = sem("a_out_done")
        sig_done = sem("a_sig_done")
        state_set = sem("a_state_set")
        mx_done = sem("a_mx_done")
        dist_done = sem("a_dist_done")
        arg_done = sem("a_arg_done")
        exp_done = sem("a_exp_done")
        new_done = sem("a_new_done")
        scan_done = sem("a_scan_done")
        bonus_done = sem("a_bonus_done")
        num_done = sem("a_num_done")
        den_done = sem("a_den_done")
        ln_done = sem("a_ln_done")
        rden_done = sem("a_rden_done")
        q_done = sem("a_q_done")
        rwkv_done = sem("a_rwkv_done")
        gate_in_done = sem("a_gate_in_done")
        gate_sig_done = sem("a_gate_sig_done")
        gate_done = sem("a_gate_done")
        prod_done = sem("a_prod_done")
        x1_done = sem("a_x1_done")

        x_v3 = a["x"].rearrange("(n j p) c -> n p j c", j=TPC, p=P)
        x1_v3 = x1_d.rearrange("(n j p) c -> n p j c", j=TPC, p=P)

        def chunks(eng, body):
            with eng.Fori(0, BATCH - 1) as b:
                for c in range(CPB):
                    body(b, c, False)
            for c in range(CPB):
                body(BATCH - 1, c, c == CPB - 1)

        def count(b, c):
            return b * CPB + c

        def turns(b, c):
            return b * (CPB // 2) + c // 2

        with nc.Block() as block:
            @block.sync
            def _(sp):
                for s in range(2):
                    sp.sem_inc(x1_stored[s], 16)
                sp.dma_start(x[:, 0], x_v3[0]).then_inc(x_loaded[0], 16)
                sp.dma_start(x[:, 1], x_v3[1]).then_inc(x_loaded[1], 16)
                for w, name in ((w_r, "WrT"), (w_k, "WkT"), (w_v, "WvT")):
                    sp.dma_start(w[:], a[name].rearrange("(k p) d -> p k d", p=P)).then_inc(weights_loaded, 16)

                def store(b, c):
                    n = count(b, c)
                    sp.wait_ge(x1_done, n + 1)
                    sp.dma_start(x1_v3[n], x1[:, c % 2]).then_inc(x1_stored[c % 2], 16)

                def load_ahead(b, c):
                    sp.dma_start(x[:, c % 2], x_v3[count(b, c) + 2]).then_inc(x_loaded[c % 2], 16)

                with sp.Fori(0, BATCH - 1) as b:
                    for c in range(CPB):
                        store(b, c)
                        load_ahead(b, c)
                for c in range(CPB):
                    store(BATCH - 1, c)
                    if c + 2 < CPB:
                        load_ahead(BATCH - 1, c)
                for s in range(2):
                    sp.wait_ge(x1_stored[s], 16 * NCH // 2 + 16)

            @block.gpsimd
            def _(pool):
                for count_from_one in (q_done, gate_done,):
                    pool.sem_inc(count_from_one, 1)
                pool.dma_start(ident[:], a["ident"]).then_inc(small_loaded, 16)
                pool.dma_start(mixes[:], a["mixes"].rearrange("p (m k) -> p m k", m=3)).then_inc(small_loaded, 16)
                pool.dma_start(decay[:], a["time_decay"]).then_inc(small_loaded, 16)
                pool.dma_start(first[:], a["time_first"]).then_inc(small_loaded, 16)
                pool.dma_start(b_1[:], a["b1"]).then_inc(small_loaded, 16)
                pool.dma_start(b_2[:], a["b2"].rearrange("(o d) -> o d", o=1).to_broadcast([P, DIM])).then_inc(small_loaded, 16)
                pool.memset(half[:], -0.5).then_inc(consts_set, 1)
                pool.memset(zero_col[:], 0.0).then_inc(consts_set, 1)
                pool.memset(eps[:], LN_EPS).then_inc(consts_set, 1)
                pool.wait_ge(consts_set, 3)

                def rstd_of(n):
                    pool.wait_ge(mv_done, TPC * n + TPC)
                    nc.gpsimd.tensor_tensor(var_eps[:], mv[:, :, 1], eps[:], ALU.add).then_inc(var_done, 1)
                    pool.wait_ge(var_done, n + 1)
                    nc.gpsimd.tensor_tensor(rstd[:], var_eps[:], half[:], ALU.pow).then_inc(rstd_done, 1)

                def diff_of(n, c):
                    pool.wait_ge(xn_done, 2 * n + 2)
                    nc.gpsimd.tensor_tensor(diff[:], xn[:, c % 2, :, 1:CH + 1], xn[:, c % 2, :, 0:CH],
                                            ALU.subtract).then_inc(diff_done, 1)

                rstd_of(0)
                diff_of(0, 0)

                def body(b, c, last):
                    n = count(b, c)
                    if not last:
                        rstd_of(n + 1)
                    pool.wait_ge(bonus_done, n + 1)
                    nc.gpsimd.tensor_tensor(out_num[:], out_num[:], num[:, :, 0:CH], ALU.add).then_inc(num_done, 1)
                    pool.wait_ge(num_done, n + 1)
                    pool.wait_ge(sig_done, n + 1)
                    nc.gpsimd.tensor_tensor(out_num[:], out_num[:], sig_r[:], ALU.mult).then_inc(q_done, 1)
                    if not last:
                        diff_of(n + 1, (c + 1) % 2)
                    pool.wait_ge(gate_sig_done, n + 1)
                    nc.gpsimd.tensor_tensor(gate[:], gate_in[:], gate_sig[:], ALU.mult).then_inc(gate_done, 1)

                chunks(pool, body)

            @block.scalar
            def _(act):
                for count_from_one in (hid_done,):
                    act.sem_inc(count_from_one, 1)
                act.dma_start(w_1[:], a["W1"].rearrange("(k p) d -> p k d", p=P)).then_inc(ffn_loaded, 16)
                act.dma_start(w_2[:], a["W2"].rearrange("(m p) d -> p m d", p=P)).then_inc(ffn_loaded, 16)
                act.dma_start(w_o[:], a["WoT"].rearrange("(k p) d -> p k d", p=P)).then_inc(ffn_loaded, 16)
                act.wait_ge(small_loaded, 16 * 6)
                nc.scalar.activation(decay[:], decay[:], ACT.Exp).then_inc(decay_exp, 1)

                def xn_of(n, c):
                    s = c % 2
                    if c == 0:
                        act.wait_ge(consts_set, 2)
                        before = zero_col[:]
                    else:
                        act.wait_ge(xn_done, 2 * n)
                        before = xn[:, 1 - s, :, CH:CH + 1]
                    act.wait_ge(xt_done, n + 1)
                    nc.scalar.activation(xn[:, s, :, 0:1], before, ACT.Copy).then_inc(xn_done, 1)
                    nc.scalar.activation(xn[:, s, :, 1:CH + 1], ps_t[:], ACT.Copy).then_inc(xn_done, 1)

                xn_of(0, 0)

                def body(b, c, last):
                    n = count(b, c)
                    act.wait_ge(r_done, n + 1)
                    act.wait_ge(q_done, n + 1)
                    nc.scalar.activation(sig_r[:], ps_a[:], ACT.Sigmoid).then_inc(sig_done, 1)
                    for i, e in enumerate((e_new, e_old, e_bonus)):
                        act.wait_ge(arg_done, 3 * KT * n + KT * (i + 1))
                        nc.scalar.activation(e[:], e[:], ACT.Exp, scale=-1.0 if e is e_old else 1.0).then_inc(exp_done, 1)
                    for m in range(3):
                        hidden(n, m)
                    act.wait_ge(den_done, n + 1)
                    nc.scalar.activation(out_den[:], out_den[:], ACT.Ln).then_inc(ln_done, 1)
                    act.wait_ge(ln_done, n + 1)
                    nc.scalar.activation(out_den[:], out_den[:], ACT.Exp, scale=-1.0).then_inc(rden_done, 1)
                    for m in range(3, MT):
                        hidden(n, m)
                    if not last:
                        xn_of(n + 1, (c + 1) % CPB)
                    act.wait_ge(gate_in_done, n + 1 + 1)
                    nc.scalar.activation(gate_sig[:], gate_in[:], ACT.Sigmoid).then_inc(gate_sig_done, 1)

                def hidden(n, m):
                    act.wait_ge(hid_mm, MT * n + m + 1)
                    nc.scalar.activation(hid[:, m, :], ps_a[:, m % 2, :], ACT.Relu, bias=b_1[:, m:m + 1]).then_inc(hid_done, 1)

                chunks(act, body)

            @block.vector
            def _(dve):
                for count_from_one in (rwkv_done, gate_in_done, prod_done,):
                    dve.sem_inc(count_from_one, 1)
                dve.wait_ge(decay_exp, 1)
                nc.vector.tensor_scalar(decay[:], decay[:], -1.0, None, ALU.mult).then_inc(decay_set, 1)
                dve.wait_ge(decay_set, 1)

                def layernorm(n, c, turn):
                    s = c % 2
                    dve.wait_ge(x_loaded[s], 16 * (turn + 1))
                    for j in range(TPC):
                        nc.vector.bn_stats(stats[:, j, :], x[:, s, j, :]).then_inc(stats_done, 1)

                def aggregate():
                    for j in range(TPC):
                        nc.vector.bn_aggr(mv[:, j, :], stats[:, j, :]).then_inc(mv_done, 1)

                def normalise(n, c):
                    s = c % 2
                    dve.wait_ge(rstd_done, n + 1)
                    dve.wait_ge(xt_done, n)
                    for j in range(TPC):
                        nc.vector.tensor_scalar(xhat[:, j, :], x[:, s, j, :], mv[:, j, 0:1], rstd[:, j:j + 1],
                                                ALU.subtract, ALU.mult).then_inc(xhat_done, 1)

                def mix(n, c):
                    dve.wait_ge(diff_done, n + 1)
                    dve.wait_ge(v_done, n)
                    for i, t in enumerate((x_r, x_k, x_v)):
                        for k in range(KT):
                            nc.vector.scalar_tensor_tensor(t[:, k, :], diff[:, k, :], mixes[:, i, k:k + 1],
                                                           xn[:, c % 2, k, 0:CH], ALU.mult, ALU.add).then_inc(mix_done, 1)

                layernorm(0, 0, 0)
                dve.wait_ge(stats_done, TPC)
                aggregate()
                normalise(0, 0)
                mix(0, 0)

                def body(b, c, last):
                    n = count(b, c)
                    if not last:
                        layernorm(n + 1, (c + 1) % CPB, turns(b, c + 1))
                        dve.wait_ge(stats_done, TPC * (n + 1) + TPC)
                    if c == 0:
                        nc.vector.memset(mx[:, :, 0:1], MAX_INIT).then_inc(state_set, 1)
                        nc.vector.memset(num[:, :, 0:1], 0.0).then_inc(state_set, 1)
                        nc.vector.memset(den[:, :, 0:1], 0.0).then_inc(state_set, 1)
                    else:
                        for t in (mx, num, den):
                            nc.vector.tensor_copy(t[:, :, 0:1], t[:, :, CH:CH + 1]).then_inc(state_set, 1)
                    if not last:
                        aggregate()
                    dve.wait_ge(state_set, 3 * n + 3)
                    dve.wait_ge(k_done, n + 1)
                    for k in range(KT):
                        nc.vector.tensor_tensor_scan(mx[:, k, 1:CH + 1], decay[:, k:k + 1].to_broadcast([P, CH]),
                                                     ps_b[:, k, :], mx[:, k, 0:1], ALU.add, ALU.max).then_inc(mx_done, 1)
                    dve.wait_ge(mx_done, KT * n + KT)
                    nc.vector.tensor_tensor(dist[:], ps_b[:], mx[:, :, 0:CH], ALU.subtract).then_inc(dist_done, 1)
                    dve.wait_ge(dist_done, n + 1)
                    for k in range(KT):
                        nc.vector.tensor_scalar(e_new[:, k, :], dist[:, k, :], decay[:, k:k + 1], 0.0,
                                                ALU.subtract, ALU.min).then_inc(arg_done, 1)
                    for k in range(KT):
                        nc.vector.tensor_scalar(e_old[:, k, :], dist[:, k, :], decay[:, k:k + 1], 0.0,
                                                ALU.subtract, ALU.max).then_inc(arg_done, 1)
                    for k in range(KT):
                        nc.vector.tensor_scalar(e_bonus[:, k, :], dist[:, k, :], first[:, k:k + 1], EXP_CAP,
                                                ALU.add, ALU.min).then_inc(arg_done, 1)
                    if not last:
                        normalise(n + 1, (c + 1) % 2)
                    dve.wait_ge(exp_done, 3 * n + 1)
                    dve.wait_ge(v_done, n + 1)
                    nc.vector.tensor_tensor(new_v[:], e_new[:], ps_c[:], ALU.mult).then_inc(new_done, 1)
                    dve.wait_ge(exp_done, 3 * n + 2)
                    for k in range(KT):
                        nc.vector.tensor_tensor_scan(den[:, k, 1:CH + 1], e_old[:, k, :], e_new[:, k, :],
                                                     den[:, k, 0:1], ALU.mult, ALU.add).then_inc(scan_done, 1)
                    dve.wait_ge(new_done, n + 1)
                    for k in range(KT):
                        nc.vector.tensor_tensor_scan(num[:, k, 1:CH + 1], e_old[:, k, :], new_v[:, k, :],
                                                     num[:, k, 0:1], ALU.mult, ALU.add).then_inc(scan_done, 1)
                    dve.wait_ge(exp_done, 3 * n + 3)
                    dve.wait_ge(rwkv_done, n + 1)
                    dve.wait_ge(scan_done, 2 * KT * n + 2 * KT)
                    nc.vector.tensor_tensor(out_num[:], e_bonus[:], ps_c[:], ALU.mult).then_inc(bonus_done, 1)
                    nc.vector.tensor_tensor(out_den[:], e_bonus[:], den[:, :, 0:CH], ALU.add).then_inc(den_done, 1)
                    dve.wait_ge(q_done, n + 1 + 1)
                    dve.wait_ge(rden_done, n + 1)
                    dve.wait_ge(out_done, n + 1)
                    nc.vector.tensor_tensor(rwkv[:], out_num[:], out_den[:], ALU.mult).then_inc(rwkv_done, 1)
                    if not last:
                        mix(n + 1, (c + 1) % 2)
                    dve.wait_ge(ffn_done, n + 1)
                    dve.wait_ge(gate_done, n + 1)
                    for j in range(TPC):
                        nc.vector.tensor_tensor(gate_in[:, j, :], ps_ffn[:, j, :], b_2[:], ALU.add).then_inc(gate_in_done, 1) if j == TPC - 1 else \
                            nc.vector.tensor_tensor(gate_in[:, j, :], ps_ffn[:, j, :], b_2[:], ALU.add)
                    dve.wait_ge(out_done, n + 1 + 1)
                    dve.wait_ge(gate_done, n + 1 + 1)
                    nc.vector.tensor_tensor(prod[:], ps_out, gate[:], ALU.mult).then_inc(prod_done, 1)
                    dve.wait_ge(prod_done, n + 1 + 1)
                    dve.wait_ge(x1_stored[c % 2], 16 * turns(b, c) + 16)
                    nc.vector.tensor_tensor(x1[:, c % 2], prod[:], x[:, c % 2], ALU.add).then_inc(x1_done, 1)

                chunks(dve, body)

            @block.tensor
            def _(pe):
                for count_from_one in (out_done,):
                    pe.sem_inc(count_from_one, 1)
                def transposes(n):
                    pe.wait_ge(xhat_done, TPC * n + TPC)
                    pe.wait_ge(xn_done, 2 * n)
                    for k in range(KT):
                        for j in range(TPC):
                            last = nc.tensor.transpose(ps_t[:, k, j * P:(j + 1) * P], xhat[:, j, k * P:(k + 1) * P], ident[:])
                    last.then_inc(xt_done, 1)

                def project(ps, w, t):
                    for m in range(KT):
                        for k in range(KT):
                            last = nc.tensor.matmul(ps[:, m, :], w[:, k, m * P:(m + 1) * P], t[:, k, :],
                                                    start=(k == 0), stop=(k == KT - 1))
                    return last

                pe.wait_ge(small_loaded, 16 * 6)
                transposes(0)
                pe.wait_ge(weights_loaded, 16 * 3)
                pe.wait_ge(ffn_loaded, 16 * 3)

                def body(b, c, last):
                    n = count(b, c)
                    pe.wait_ge(mix_done, 3 * KT * n + KT)
                    pe.wait_ge(hid_done, MT * n + 1)
                    project(ps_a, w_r, x_r).then_inc(r_done, 1)
                    pe.wait_ge(mix_done, 3 * KT * n + 2 * KT)
                    pe.wait_ge(gate_in_done, n + 1)
                    project(ps_b, w_k, x_k).then_inc(k_done, 1)
                    pe.wait_ge(mix_done, 3 * KT * n + 3 * KT)
                    pe.wait_ge(prod_done, n + 1)
                    project(ps_c, w_v, x_v).then_inc(v_done, 1)
                    pe.wait_ge(xn_done, 2 * n + 2)
                    for m in range(MT):
                        if m < 2:
                            pe.wait_ge(sig_done, n + 1)
                        else:
                            pe.wait_ge(hid_done, MT * n + m - 1 + 1)
                        for k in range(KT):
                            mm = nc.tensor.matmul(ps_a[:, m % 2, :], w_1[:, k, m * P:(m + 1) * P],
                                                  xn[:, c % 2, k, 1:CH + 1], start=(k == 0), stop=(k == KT - 1))
                        mm.then_inc(hid_mm, 1)
                    if not last:
                        transposes(n + 1)
                    pe.wait_ge(hid_done, MT * n + MT + 1)
                    pe.wait_ge(dist_done, n + 1)
                    for j in range(TPC):
                        for m in range(MT):
                            mm = nc.tensor.matmul(ps_ffn[:, j, :], hid[:, m, j * P:(j + 1) * P], w_2[:, m, :],
                                                  start=(m == 0), stop=(m == MT - 1))
                    mm.then_inc(ffn_done, 1)
                    pe.wait_ge(rwkv_done, n + 1 + 1)
                    for j in range(TPC):
                        for k in range(KT):
                            mm = nc.tensor.matmul(ps_out[:, j, :], rwkv[:, k, j * P:(j + 1) * P], w_o[:, k, :],
                                                  start=(k == 0), stop=(k == KT - 1))
                    mm.then_inc(out_done, 1)

                chunks(pe, body)


def scratch(nc):
    def dram(name, shape, dt=F32):
        return nc.dram_tensor(name, shape, dt, kind="Internal").ap()

    return {
        "x1": dram("x1_d", [TOKENS, DIM]),
        "qc": dram("qc_d", [BATCH, 2, DIM, SEQ], F16),
        "qr": dram("qr_d", [BATCH, 2, HEADS * D_R, SEQ], F16),
        "kc": dram("kc_d", [BATCH, 2, DIM, SEQ], F16),
        "kr": dram("kr_d", [BATCH, 2, D_R, SEQ], F16),
        "v": dram("v_d", [TOKENS, HEADS * VW]),
        "gate": dram("gate_d", [TOKENS, DIM]),
        "attn": dram("attn_d", [TOKENS, DIM]),
    }


STORES = 8


def layer1_projections(nc, a, d, score_scale):
    with ExitStack() as ctx:
        def sb(name, shape, dt=F32):
            return ctx.enter_context(nc.sbuf_tensor(name, shape, dt))

        def sem(name):
            return ctx.enter_context(nc.semaphore(name))

        x = sb("b_x", [P, 2, TPC, DIM])
        ident = sb("b_ident", [P, P])
        ones = sb("b_ones", [P, P])
        w_c = sb("b_wc", [P, KT, 2 * LATENT])
        w_kr = sb("b_wkr", [P, KT, VW + D_R])
        w_q = sb("b_wq", [P, DIM + 2 * HEADS * D_R])
        w_uk = sb("b_wuk", [P, DIM])
        w_uv = sb("b_wuv", [P, DIM])
        w_r, w_k, w_v = (sb(f"b_w{n}", [P, KT, DIM]) for n in "rkv")
        mixes = sb("b_mixes", [P, 2, KT])
        cos = sb("b_cos", [P, SEQ])
        sin = sb("b_sin", [P, SEQ])
        squares = sb("b_squares", [P, DIM + 2 * HEADS * D_R])
        sums = sb("b_sums", [P, 5])
        roots = sb("b_roots", [P, 5])
        bound = sb("b_bound", [P, 2])
        kr_bound = sb("b_kr_bound", [P, 1])
        power = sb("b_power", [P, 2])
        scale = sb("b_scale", [P, 2])
        eps = sb("b_eps", [P, TPC])
        half = sb("b_half", [P, TPC])
        zero_col = sb("b_zero", [P, KT, 1])
        stats = sb("b_stats", [P, TPC, 6])
        mv = sb("b_mv", [P, TPC, 2])
        var_eps = sb("b_var", [P, TPC])
        rstd = sb("b_rstd", [P, TPC])
        xhat = sb("b_xhat", [P, TPC, DIM])
        xn = sb("b_xn", [P, 2, KT, CH + 1])
        diff = sb("b_diff", [P, KT, CH])
        x_r, x_k = (sb(f"b_x{n}", [P, KT, CH]) for n in "rk")
        lat = sb("b_lat", [P, CH])
        q_cos = sb("b_qcos", [P, CH])
        q_sin = sb("b_qsin", [P, CH])
        k_cos = sb("b_kcos", [D_R, CH])
        k_sin = sb("b_ksin", [D_R, CH])
        qc = sb("b_qc", [P, 2, 2, KT, CH], F16)
        kc = sb("b_kc", [P, 2, 2, KT, CH], F16)
        qr = sb("b_qr", [P, 2, 2, CH], F16)
        kr = sb("b_kr", [D_R, 2, 2, CH], F16)
        val = sb("b_val", [P, 2, TPC, HEADS, VW])
        relu = sb("b_relu", [P, KT, CH])
        act_k = sb("b_actk", [P, KT, CH])
        sig_r = sb("b_sigr", [P, TPC, DIM])
        gate_in = sb("b_gi", [P, TPC, DIM])
        gate_sig = sb("b_gs", [P, TPC, DIM])
        gate = sb("b_gate", [P, 2, TPC, DIM])

        ps_a = ctx.enter_context(nc.psum_tensor("b_ps0", [P, 2, CH], F32))
        ps_b = ctx.enter_context(nc.psum_tensor("b_ps1", [P, 2, CH], F32))
        ps_c = ctx.enter_context(nc.psum_tensor("b_ps2", [P, 2, CH], F32))
        ps_t = ctx.enter_context(nc.psum_tensor("b_ps3", [P, 2, CH], F32))
        ps_val = ps_a[:].rearrange("p a (j d) -> p (a j) d", d=DIM)
        ps_r = ps_b[:].rearrange("p a (j d) -> p (a j) d", d=DIM)
        ps_kv = ps_c[:].rearrange("p a (j d) -> p (a j) d", d=DIM)

        weights_loaded = sem("b_weights_loaded")
        consts_loaded = sem("b_consts_loaded")
        x_loaded = [sem(f"b_x_loaded{i}") for i in range(2)]
        stored = [sem(f"b_stored{i}") for i in range(2)]
        consts_set = sem("b_consts_set")
        squares_done = sem("b_squares_done")
        sums_done = sem("b_sums_done")
        roots_done = sem("b_roots_done")
        bound_done = sem("b_bound_done")
        scale_done = sem("b_scale_done")
        stats_done = sem("b_stats_done")
        mv_done = sem("b_mv_done")
        var_done = sem("b_var_done")
        rstd_done = sem("b_rstd_done")
        xhat_done = sem("b_xhat_done")
        xt_done = sem("b_xt_done")
        xn_done = sem("b_xn_done")
        diff_done = sem("b_diff_done")
        mix_done = sem("b_mix_done")
        lat_mm = sem("b_lat_mm")
        lat_done = sem("b_lat_done")
        kr_mm = sem("b_kr_mm")
        k_mm = sem("b_k_mm")
        qc_mm = sem("b_qc_mm")
        qr_mm = sem("b_qr_mm")
        kc_mm = sem("b_kc_mm")
        r_mm = sem("b_r_mm")
        val_mm = sem("b_val_mm")
        kv_mm = sem("b_kv_mm")
        relu_done = sem("b_relu_done")
        act_done = sem("b_act_done")
        qc_high = sem("b_qc_high")
        qc_low = sem("b_qc_low")
        kc_high = sem("b_kc_high")
        kc_low = sem("b_kc_low")
        kr_parts = sem("b_kr_parts")
        kr_sum = sem("b_kr_sum")
        kr_high = sem("b_kr_high")
        kr_low = sem("b_kr_low")
        qr_parts = sem("b_qr_parts")
        qr_sum = sem("b_qr_sum")
        qr_high = sem("b_qr_high")
        qr_low = sem("b_qr_low")
        sig_done = sem("b_sig_done")
        val_done = sem("b_val_done")
        gate_in_done = sem("b_gate_in_done")
        gate_sig_done = sem("b_gate_sig_done")
        gate_done = sem("b_gate_done")

        x_v3 = d["x1"].rearrange("(n j p) c -> n p j c", j=TPC, p=P)
        gate_v3 = d["gate"].rearrange("(n j p) c -> n p j c", j=TPC, p=P)
        val_v3 = d["v"].rearrange("(n j p) c -> n p j c", j=TPC, p=P)
        WEIGHTS = 8

        def chunks(eng, body):
            with eng.Fori(0, BATCH - 1) as b:
                for c in range(CPB):
                    body(b, c, False)
            for c in range(CPB):
                body(BATCH - 1, c, c == CPB - 1)

        def count(b, c):
            return b * CPB + c

        def turns(b, c):
            return b * (CPB // 2) + c // 2

        with nc.Block() as block:
            @block.sync
            def _(sp):
                for s in range(2):
                    sp.sem_inc(stored[s], 16)
                sp.dma_start(x[:, 0], x_v3[0]).then_inc(x_loaded[0], 16)
                sp.dma_start(x[:, 1], x_v3[1]).then_inc(x_loaded[1], 16)
                sp.dma_start(ident[:], a["ident"]).then_inc(consts_loaded, 16)
                sp.dma_start(mixes[:], a["mixes1"].rearrange("p (m k) -> p m k", m=2)).then_inc(consts_loaded, 16)
                sp.dma_start(cos[:], a["cos"]).then_inc(consts_loaded, 16)
                sp.dma_start(sin[:], a["sin"]).then_inc(consts_loaded, 16)

                def store(b, c):
                    n, s, t = count(b, c), c % 2, slice(c * CH, (c + 1) * CH)
                    sp.wait_ge(kr_low, n + 1)
                    sp.dma_start(d["kr"][b, :, :, t].rearrange("h p t -> p h t"), kr[:, s]).then_inc(stored[s], 16)
                    sp.wait_ge(qc_low, KT * n + KT)
                    for h in range(2):
                        sp.dma_start(d["qc"][b, h, :, t].rearrange("(m p) t -> p m t", p=P), qc[:, s, h]).then_inc(stored[s], 16)
                    sp.wait_ge(kc_low, KT * n + KT)
                    for h in range(2):
                        sp.dma_start(d["kc"][b, h, :, t].rearrange("(m p) t -> p m t", p=P), kc[:, s, h]).then_inc(stored[s], 16)
                    sp.wait_ge(qr_low, n + 1)
                    sp.dma_start(d["qr"][b, :, :, t].rearrange("h p t -> p h t"), qr[:, s]).then_inc(stored[s], 16)
                    sp.wait_ge(val_done, n + 1 + 1)
                    sp.dma_start(val_v3[n], val[:, s].rearrange("p j h e -> p j (h e)")).then_inc(stored[s], 16)
                    sp.wait_ge(gate_done, n + 1 + 1)
                    sp.dma_start(gate_v3[n], gate[:, s]).then_inc(stored[s], 16)

                def load_ahead(b, c):
                    sp.wait_ge(xhat_done, TPC * count(b, c) + TPC)
                    sp.dma_start(x[:, c % 2], x_v3[count(b, c) + 2]).then_inc(x_loaded[c % 2], 16)

                with sp.Fori(0, BATCH - 1) as b:
                    for c in range(CPB):
                        load_ahead(b, c)
                        store(b, c)
                for c in range(CPB):
                    if c + 2 < CPB:
                        load_ahead(BATCH - 1, c)
                    store(BATCH - 1, c)
                for s in range(2):
                    sp.wait_ge(stored[s], 16 * STORES * NCH // 2 + 16)

            @block.gpsimd
            def _(pool):
                for count_from_one in (gate_done,):
                    pool.sem_inc(count_from_one, 1)
                pool.memset(half[:], -0.5).then_inc(consts_set, 1)
                pool.memset(zero_col[:], 0.0).then_inc(consts_set, 1)
                pool.memset(ones[:], 1.0).then_inc(consts_set, 1)
                pool.memset(eps[:], LN_EPS).then_inc(consts_set, 1)
                pool.memset(val[:], 0.0).then_inc(consts_set, 1)
                pool.wait_ge(consts_set, 5)
                for s in range(2):
                    pool.memset(val[:, s, :, :, D_H:D_H + 1], 1.0).then_inc(consts_set, 1)

                def rstd_of(n):
                    pool.wait_ge(mv_done, TPC * n + TPC)
                    nc.gpsimd.tensor_tensor(var_eps[:], mv[:, :, 1], eps[:], ALU.add).then_inc(var_done, 1)
                    pool.wait_ge(var_done, n + 1)
                    nc.gpsimd.tensor_tensor(rstd[:], var_eps[:], half[:], ALU.pow).then_inc(rstd_done, 1)

                def diff_of(n, c):
                    pool.wait_ge(xn_done, 2 * n + 2)
                    nc.gpsimd.tensor_tensor(diff[:], xn[:, c % 2, :, 1:CH + 1], xn[:, c % 2, :, 0:CH],
                                            ALU.subtract).then_inc(diff_done, 1)

                rstd_of(0)
                diff_of(0, 0)

                def body(b, c, last):
                    n = count(b, c)
                    if not last:
                        rstd_of(n + 1)
                        diff_of(n + 1, (c + 1) % 2)
                    pool.wait_ge(gate_sig_done, n + 1)
                    pool.wait_ge(stored[c % 2], 16 * STORES * turns(b, c) + 16)
                    nc.gpsimd.tensor_tensor(gate[:, c % 2], gate_in[:], gate_sig[:], ALU.mult).then_inc(gate_done, 1)

                chunks(pool, body)

            @block.scalar
            def _(act):
                for count_from_one in (val_done, sig_done,):
                    act.sem_inc(count_from_one, 1)
                for t, name in ((w_c, "Wc"), (w_kr, "Wkr"), (w_r, "W1rT"), (w_k, "W1kT"), (w_v, "W1vT")):
                    act.dma_start(t[:], a[name].rearrange("(k p) n -> p k n", p=P)).then_inc(weights_loaded, 16)
                for t, name in ((w_q, "Wq"), (w_uk, "Wuk"), (w_uv, "Wuv")):
                    act.dma_start(t[:], a[name]).then_inc(weights_loaded, 16)
                act.wait_ge(sums_done, 1)
                nc.scalar.activation(roots[:], ps_a[:, 0, 0:5], ACT.Sqrt).then_inc(roots_done, 1)

                def xn_of(n, c):
                    s = c % 2
                    if c == 0:
                        act.wait_ge(consts_set, 2)
                        before = zero_col[:]
                    else:
                        act.wait_ge(xn_done, 2 * n)
                        before = xn[:, 1 - s, :, CH:CH + 1]
                    act.wait_ge(xt_done, n + 1)
                    nc.scalar.activation(xn[:, s, :, 0:1], before, ACT.Copy).then_inc(xn_done, 1)
                    nc.scalar.activation(xn[:, s, :, 1:CH + 1], ps_t[:], ACT.Copy).then_inc(xn_done, 1)

                xn_of(0, 0)
                act.wait_ge(scale_done, 1)

                def body(b, c, last):
                    n, s = count(b, c), c % 2
                    act.wait_ge(lat_mm, n + 1)
                    nc.scalar.activation(lat[:], ps_a[:, 0, :], ACT.Copy).then_inc(lat_done, 1)
                    act.wait_ge(stored[s], 16 * STORES * turns(b, c) + 16)
                    act.wait_ge(kr_sum, n + 1)
                    nc.scalar.activation(kr[:, s, 0, :], k_cos[:], ACT.Copy).then_inc(kr_high, 1)
                    act.wait_ge(k_mm, n + 1)
                    nc.scalar.activation(relu[:], ps_b[:], ACT.Relu).then_inc(relu_done, 1)
                    for m in range(KT):
                        act.wait_ge(qc_mm, KT * n + m + 1)
                        nc.scalar.activation(qc[:, s, 0, m, :], ps_c[:, m, :], ACT.Copy, scale=scale[:, 0:1]).then_inc(qc_high, 1)
                    for m in range(KT):
                        act.wait_ge(kc_mm, KT * n + m + 1)
                        nc.scalar.activation(kc[:, s, 0, m, :], ps_c[:, m, :], ACT.Copy, scale=scale[:, 1:2]).then_inc(kc_high, 1)
                    act.wait_ge(qr_sum, n + 1)
                    nc.scalar.activation(qr[:, s, 0, :], q_cos[:], ACT.Copy).then_inc(qr_high, 1)
                    if not last:
                        xn_of(n + 1, (c + 1) % CPB)
                    act.wait_ge(r_mm, n + 1)
                    nc.scalar.activation(sig_r[:], ps_r, ACT.Sigmoid).then_inc(sig_done, 1)
                    act.wait_ge(val_mm, n + 1)
                    act.wait_ge(consts_set, 7)
                    for j in range(TPC):
                        ins = nc.scalar.activation(val[:, s, j, :, 0:D_H], ps_val[:, j, :].rearrange("p (h e) -> p h e", e=D_H), ACT.Copy)
                    ins.then_inc(val_done, 1)
                    act.wait_ge(gate_in_done, n + 1 + 1)
                    nc.scalar.activation(gate_sig[:], gate_in[:], ACT.Sigmoid).then_inc(gate_sig_done, 1)

                chunks(act, body)

            @block.vector
            def _(dve):
                for count_from_one in (gate_in_done,):
                    dve.sem_inc(count_from_one, 1)
                dve.wait_ge(weights_loaded, 16 * WEIGHTS)
                flat = (w_c[:, :, 0:LATENT], w_c[:, :, LATENT:], w_q[:], w_uk[:], w_kr[:])
                for i, w in enumerate(flat):
                    size = w.free_size()
                    if i:
                        dve.wait_ge(squares_done, i)
                    sq = squares[:, 0:size]
                    if len(w.shape) == 3:
                        sq = sq.rearrange("p (k n) -> p k n", k=w.shape[1])
                    nc.vector.tensor_tensor_reduce(out=sq, in0=w, in1=w, scale=1.0, scalar=0.0, op0=ALU.mult, op1=ALU.add,
                                                   accum_out=sums[:, i:i + 1]).then_inc(squares_done, 1)
                dve.wait_ge(roots_done, 1)
                nc.vector.tensor_tensor(bound[:, 0:1], roots[:, 0:1], roots[:, 2:3], ALU.mult).then_inc(bound_done, 1)
                nc.vector.tensor_tensor(bound[:, 1:2], roots[:, 1:2], roots[:, 3:4], ALU.mult).then_inc(bound_done, 1)
                dve.wait_ge(bound_done, 2)
                nc.vector.tensor_tensor(bound[:, 1:2], bound[:, 1:2], roots[:, 4:5], ALU.max).then_inc(bound_done, 1)
                dve.wait_ge(bound_done, 3)
                nc.vector.tensor_scalar(bound[:], bound[:], 2.0 * float(np.sqrt(DIM)), 1e-20, ALU.mult, ALU.max).then_inc(bound_done, 1)
                dve.wait_ge(bound_done, 4)
                nc.vector.tensor_scalar(power[:].bitcast(I32), bound[:].bitcast(I32), 0x7F800000, None,
                                        ALU.bitwise_and).then_inc(bound_done, 1)
                dve.wait_ge(bound_done, 5)
                nc.vector.reciprocal(scale[:], power[:]).then_inc(bound_done, 1)
                nc.vector.tensor_tensor(score_scale[:], power[:, 0:1], power[:, 1:2], ALU.mult).then_inc(bound_done, 1)
                dve.wait_ge(bound_done, 7)
                nc.vector.tensor_scalar(score_scale[:], score_scale[:], INV_SQRT / F16_TARGET ** 2, None, ALU.mult)
                nc.vector.tensor_scalar(scale[:], scale[:], F16_TARGET, None, ALU.mult).then_inc(scale_done, 1)
                dve.wait_ge(scale_done, 1)

                def layernorm(n, c, turn):
                    s = c % 2
                    dve.wait_ge(x_loaded[s], 16 * (turn + 1))
                    for j in range(TPC):
                        nc.vector.bn_stats(stats[:, j, :], x[:, s, j, :]).then_inc(stats_done, 1)

                def aggregate():
                    for j in range(TPC):
                        nc.vector.bn_aggr(mv[:, j, :], stats[:, j, :]).then_inc(mv_done, 1)

                def normalise(n, c):
                    dve.wait_ge(rstd_done, n + 1)
                    dve.wait_ge(xt_done, n)
                    for j in range(TPC):
                        nc.vector.tensor_scalar(xhat[:, j, :], x[:, c % 2, j, :], mv[:, j, 0:1], rstd[:, j:j + 1],
                                                ALU.subtract, ALU.mult).then_inc(xhat_done, 1)

                def mix(n, c):
                    dve.wait_ge(diff_done, n + 1)
                    dve.wait_ge(r_mm, n)
                    for i, t in ((1, x_k), (0, x_r)):
                        for k in range(KT):
                            nc.vector.scalar_tensor_tensor(t[:, k, :], diff[:, k, :], mixes[:, i, k:k + 1],
                                                           xn[:, c % 2, k, 0:CH], ALU.mult, ALU.add).then_inc(mix_done, 1)

                layernorm(0, 0, 0)
                dve.wait_ge(stats_done, TPC)
                aggregate()
                normalise(0, 0)
                dve.wait_ge(consts_loaded, 16 * 4)
                mix(0, 0)

                def body(b, c, last):
                    n, s, t = count(b, c), c % 2, slice(c * CH, (c + 1) * CH)
                    dve.wait_ge(kr_mm, n + 1)
                    dve.wait_ge(stored[s], 16 * STORES * turns(b, c) + 16)
                    nc.vector.scalar_tensor_tensor(k_cos[:], ps_a[0:D_R, 1, :], scale[0:D_R, 1:2], cos[0:D_R, t],
                                                   ALU.mult, ALU.mult).then_inc(kr_parts, 1)
                    nc.vector.scalar_tensor_tensor(k_sin[:], ps_a[VW:VW + D_R, 1, :], scale[VW:VW + D_R, 1:2], sin[VW:VW + D_R, t],
                                                   ALU.mult, ALU.mult).then_inc(kr_parts, 1)
                    dve.wait_ge(kr_parts, 2 * n + 2)
                    nc.vector.tensor_tensor(k_cos[:], k_cos[:], k_sin[:], ALU.add).then_inc(kr_sum, 1)
                    if not last:
                        layernorm(n + 1, (c + 1) % CPB, turns(b, c + 1))
                        dve.wait_ge(stats_done, TPC * (n + 1) + TPC)
                    dve.wait_ge(kr_high, n + 1)
                    nc.vector.tensor_tensor(kr[:, s, 1, :], k_cos[:], kr[:, s, 0, :], ALU.subtract).then_inc(kr_low, 1)
                    if not last:
                        aggregate()
                    dve.wait_ge(relu_done, n + 1)
                    dve.wait_ge(kv_mm, n + 1)
                    nc.vector.tensor_tensor(act_k[:], relu[:], relu[:], ALU.mult).then_inc(act_done, 1)
                    for m in range(KT):
                        dve.wait_ge(qc_high, KT * n + m + 1)
                        nc.vector.scalar_tensor_tensor(qc[:, s, 1, m, :], ps_c[:, m, :], scale[:, 0:1], qc[:, s, 0, m, :],
                                                       ALU.mult, ALU.subtract).then_inc(qc_low, 1)
                    dve.wait_ge(qr_mm, 2 * n + 1)
                    nc.vector.scalar_tensor_tensor(q_cos[:], ps_a[:, 0, :], scale[:, 0:1], cos[:, t], ALU.mult, ALU.mult).then_inc(qr_parts, 1)
                    dve.wait_ge(qr_mm, 2 * n + 2)
                    nc.vector.scalar_tensor_tensor(q_sin[:], ps_a[:, 1, :], scale[:, 0:1], sin[:, t], ALU.mult, ALU.mult).then_inc(qr_parts, 1)
                    dve.wait_ge(qr_parts, 2 * n + 2)
                    nc.vector.tensor_tensor(q_cos[:], q_cos[:], q_sin[:], ALU.add).then_inc(qr_sum, 1)
                    for m in range(KT):
                        dve.wait_ge(kc_high, KT * n + m + 1)
                        nc.vector.scalar_tensor_tensor(kc[:, s, 1, m, :], ps_c[:, m, :], scale[:, 1:2], kc[:, s, 0, m, :],
                                                       ALU.mult, ALU.subtract).then_inc(kc_low, 1)
                    dve.wait_ge(qr_high, n + 1)
                    nc.vector.tensor_tensor(qr[:, s, 1, :], q_cos[:], qr[:, s, 0, :], ALU.subtract).then_inc(qr_low, 1)
                    if not last:
                        normalise(n + 1, (c + 1) % 2)
                        mix(n + 1, (c + 1) % 2)
                    dve.wait_ge(kv_mm, n + 1 + 1)
                    dve.wait_ge(sig_done, n + 1 + 1)
                    dve.wait_ge(gate_done, n + 1)
                    nc.vector.tensor_tensor(gate_in[:], ps_kv, sig_r[:], ALU.mult).then_inc(gate_in_done, 1)

                chunks(dve, body)

            @block.tensor
            def _(pe):
                for count_from_one in (kv_mm,):
                    pe.sem_inc(count_from_one, 1)
                pe.wait_ge(consts_set, 3)
                pe.wait_ge(squares_done, 5)
                nc.tensor.matmul(ps_a[:, 0, 0:5], ones[:], sums[:], start=True, stop=True).then_inc(sums_done, 1)

                def transposes(n):
                    pe.wait_ge(xhat_done, TPC * n + TPC)
                    pe.wait_ge(xn_done, 2 * n)
                    for k in range(KT):
                        for j in range(TPC):
                            last = nc.tensor.transpose(ps_t[:, k, j * P:(j + 1) * P], xhat[:, j, k * P:(k + 1) * P], ident[:])
                    last.then_inc(xt_done, 1)

                def project(ps, w, t):
                    for k in range(KT):
                        last = nc.tensor.matmul(ps, w(k), t(k), start=(k == 0), stop=(k == KT - 1))
                    return last

                pe.wait_ge(consts_loaded, 16 * 4)
                transposes(0)
                pe.wait_ge(roots_done, 1)

                def body(b, c, last):
                    n, s = count(b, c), c % 2
                    xs = lambda k: xn[:, s, k, 1:CH + 1]
                    pe.wait_ge(xn_done, 2 * n + 2)
                    pe.wait_ge(val_done, n + 1)
                    project(ps_a[:, 0, :], lambda k: w_c[:, k, :], xs).then_inc(lat_mm, 1)
                    project(ps_a[0:VW + D_R, 1, :], lambda k: w_kr[:, k, :], xs).then_inc(kr_mm, 1)
                    pe.wait_ge(mix_done, 2 * KT * n + KT)
                    pe.wait_ge(sig_done, n + 1)
                    for m in range(KT):
                        mm = project(ps_b[:, m, :], lambda k: w_k[:, k, m * P:(m + 1) * P], lambda k: x_k[:, k, :])
                    mm.then_inc(k_mm, 1)
                    pe.wait_ge(lat_done, n + 1)
                    pe.wait_ge(gate_in_done, n + 1)
                    for m in range(KT):
                        nc.tensor.matmul(ps_c[:, m, :], w_q[:, m * P:(m + 1) * P], lat[:], start=True, stop=True).then_inc(qc_mm, 1)
                    pe.wait_ge(kr_parts, 2 * n + 2)
                    for m in range(2):
                        nc.tensor.matmul(ps_a[:, m, :], w_q[:, DIM + m * P:DIM + (m + 1) * P], lat[:], start=True, stop=True).then_inc(qr_mm, 1)
                    pe.wait_ge(relu_done, n + 1)
                    pe.wait_ge(mix_done, 2 * KT * n + 2 * KT)
                    for j in range(TPC):
                        mm = project(ps_r[:, j, :], lambda k: x_r[:, k, j * P:(j + 1) * P], lambda k: w_r[:, k, :])
                    mm.then_inc(r_mm, 1)
                    for m in range(KT):
                        pe.wait_ge(qc_low, KT * n + m + 1)
                        nc.tensor.matmul(ps_c[:, m, :], w_uk[:, m * P:(m + 1) * P], lat[:], start=True, stop=True).then_inc(kc_mm, 1)
                    pe.wait_ge(qr_parts, 2 * n + 2)
                    for j in range(TPC):
                        mm = nc.tensor.matmul(ps_val[:, j, :], lat[:, j * P:(j + 1) * P], w_uv[:], start=True, stop=True)
                    mm.then_inc(val_mm, 1)
                    if not last:
                        transposes(n + 1)
                    pe.wait_ge(kc_low, KT * n + KT)
                    pe.wait_ge(act_done, n + 1)
                    for j in range(TPC):
                        mm = project(ps_kv[:, j, :], lambda k: act_k[:, k, j * P:(j + 1) * P], lambda k: w_v[:, k, :])
                    mm.then_inc(kv_mm, 1)

                chunks(pe, body)



def attention(nc, d, score_scale):
    tiles = [[kt for j in range(TPC) for kt in [TPC * c + j] + [c * j + f for f in range(c)]] for c in range(CPB)]
    steps = [(s, c, kt) for s in range(2) for c in range(CPB) for kt in tiles[c]]
    N = len(steps)
    starts = [i for i, (s, c, kt) in enumerate(steps) if kt == tiles[c][0]]
    ends = [i for i, (s, c, kt) in enumerate(steps) if kt == tiles[c][-1]]
    AHEAD = 3
    LEAD = 3
    NC = len(ends)
    PAIRS = BATCH * GROUPS // 2
    HALF = GH // 2
    NBUF, NPROB = 3, 4
    LOADS = 17
    bufs = [h % NBUF for h in range(2 * N)]
    if bufs[-1] == 0:
        bufs[-2], bufs[-1] = bufs[-1], bufs[-2]
    before = []
    for h in range(2 * N):
        back = [g for g in range(h - 2 * N, h) if bufs[g] == bufs[h]]
        before.append(back[-1])
    diags = [i for i, (s, c, kt) in enumerate(steps) if kt >= TPC * c]

    def offset(i):
        _, c, kt = steps[i]
        return max(0, kt - TPC * c) * P

    with ExitStack() as ctx:
        def sb(name, shape, dt=F32):
            return ctx.enter_context(nc.sbuf_tensor(name, shape, dt))

        def sem(name):
            return ctx.enter_context(nc.semaphore(name))

        q = sb("c_q", [KROWS, 2, GH, SEQ], F16)
        k = sb("c_k", [KROWS, 2, GH, SEQ], F16)
        v = sb("c_v", [P, 2, KEYT, GH * VW])
        ident = sb("c_ident", [P, P])
        probs = sb("c_probs", [P, NPROB, GH, CH])
        causal = sb("c_causal", [P, HALF, P])
        o_t = sb("c_ot", [P, 2, CH])
        recip = sb("c_recip", [P, 2, TPC, GH])
        attn = sb("c_attn", [P, 2, TPC, GH, D_H])
        ps_s = ctx.enter_context(nc.psum_tensor("c_ps_s", [P, NBUF, HALF, CH], F32))
        ps_o = ctx.enter_context(nc.psum_tensor("c_ps_o", [P, 2, CH], F32))
        ps_tok = ps_o[:].rearrange("p a (j h e) -> p a j h e", j=TPC, h=GH)

        ident_loaded = sem("c_ident_loaded")
        causal_set = sem("c_causal_set")
        loaded = [sem(f"c_loaded{i}") for i in range(2)]
        stored = [sem(f"c_stored{i}") for i in range(2)]
        qk_done = sem("c_qk_done")
        exp_done = sem("c_exp_done")
        clip_done = sem("c_clip_done")
        mask_done = sem("c_mask_done")
        pv_done = sem("c_pv_done")
        ot_done = sem("c_ot_done")
        tok_done = sem("c_tok_done")
        recip_done = sem("c_recip_done")
        norm_done = sem("c_norm_done")

        def pairs(eng, body):
            with eng.Fori(0, PAIRS - 1) as i:
                body(i, False)
            body(PAIRS - 1, True)

        attn_v = d["attn"].rearrange("(b c j p) (g e) -> b c g p j e", c=CPB, j=TPC, p=P, g=GROUPS)

        with nc.Block() as block:
            @block.sync
            def _(sp):
                for s in range(2):
                    sp.sem_inc(stored[s], 16)
                sp.dma_start(ident[:], d["ident"]).then_inc(ident_loaded, 16)

                def load(i, s):
                    b, g = (i * 2 + s) // GROUPS, (i * 2 + s) % GROUPS
                    at = 0
                    for hq, hk in ((0, 0), (0, 1), (1, 0), (1, 1)):
                        for t, name, half in ((q, "q", hq), (k, "k", hk)):
                            src = d[name + "c"][b, half].rearrange("(g h r) t -> g r h t", g=GROUPS, h=GH)[g]
                            sp.dma_start(t[at:at + D_H, s], src).then_inc(loaded[s], 16)
                            if name == "q":
                                src = d["qr"][b, half].rearrange("(g h r) t -> g r h t", g=GROUPS, h=GH)[g]
                            else:
                                src = d["kr"][b, half].rearrange("r (o t) -> r o t", o=1).to_broadcast([D_R, GH, SEQ])
                            sp.dma_start(t[at + D_H:at + D_QK, s], src).then_inc(loaded[s], 16)
                        at += D_QK
                    src = d["v"].rearrange("(b m p) (g e) -> b g p m e", b=BATCH, p=P, g=GROUPS)[b, g]
                    sp.dma_start(v[:, s], src).then_inc(loaded[s], 16)

                load(0, 0)
                load(0, 1)

                def body(i, last):
                    for s in range(2):
                        b, g = (i * 2 + s) // GROUPS, (i * 2 + s) % GROUPS
                        for c in range(CPB):
                            e = s * CPB + c
                            sp.wait_ge(norm_done, NC * i + e + 1 + 2)
                            sp.dma_start(attn_v[b, c, g], attn[:, c % 2].rearrange("p j h e -> p j (h e)")).then_inc(stored[c % 2], 16)
                        if not last:
                            sp.wait_ge(pv_done, N * i + (s + 1) * N // 2 + NPROB)
                            load(i + 1, s)

                pairs(sp, body)
                for s in range(2):
                    sp.wait_ge(stored[s], 16 * BATCH * GROUPS * CPB // 2 + 16)

            @block.scalar
            def _(act):
                act.sem_inc(exp_done, NBUF)
                unscale = act.alloc_register("c_unscale")
                act.load(unscale, score_scale[0:1, 0:1].bitcast(I32))

                def body(i, last):
                    for st in range(N):
                        o = offset(st)
                        for h in range(2):
                            hs = 2 * st + h
                            if h == 0:
                                act.wait_ge(pv_done, N * i + st + 1)
                            act.wait_ge(qk_done, 2 * N * i + hs + 1)
                            nc.scalar.activation(probs[:, st % NPROB, h * HALF:(h + 1) * HALF, o:CH], ps_s[:, bufs[hs], :, o:CH],
                                                 ACT.Exp, scale=unscale).then_inc(exp_done, 1)

                pairs(act, body)

            @block.vector
            def _(dve):
                dve.sem_inc(norm_done, 2)

                def rows_out(i, e):
                    dve.wait_ge(pv_done, N * i + ends[e] + 1 + NPROB)
                    nc.vector.tensor_copy(o_t[:, e % 2, :], ps_o[:, e % 2, :]).then_inc(ot_done, 1)

                def normalise(i, e):
                    a = e % 2
                    dve.wait_ge(tok_done, NC * i + e + 1)
                    nc.vector.reciprocal(recip[:, a], ps_tok[:, a, :, :, D_H]).then_inc(recip_done, 1)
                    dve.wait_ge(stored[a], 16 * (NC // 2 * i + e // 2) + 16)
                    dve.wait_ge(recip_done, NC * i + e + 1)
                    nc.vector.tensor_tensor(attn[:, a], ps_tok[:, a, :, :, 0:D_H],
                                            recip[:, a].rearrange("p j (h o) -> p j h o", o=1).to_broadcast([P, TPC, GH, D_H]),
                                            ALU.mult).then_inc(norm_done, 1)

                def clip(i, st):
                    o = offset(st)
                    for h in range(2):
                        hs = 2 * st + h
                        dve.wait_ge(exp_done, 2 * N * i + hs + 1 + NBUF)
                        tile = probs[:, st % NPROB, h * HALF:(h + 1) * HALF, o:CH]
                        nc.vector.tensor_scalar(tile, tile, P_MAX, P_MIN, ALU.min, ALU.max).then_inc(clip_done, 1)

                for st in range(AHEAD):
                    clip(0, st)
                for st in range(LEAD):
                    clip(0, st + AHEAD)

                def body(i, last):
                    todo = {}
                    for e, st in enumerate(ends):
                        todo.setdefault(st, []).append((rows_out, e))
                        todo.setdefault(st + 3, []).append((normalise, e))
                    for st in range(LEAD, N + LEAD):
                        if st + AHEAD < N:
                            clip(i, st + AHEAD)
                        elif not last:
                            clip(i + 1, st + AHEAD - N)
                        for task, e in todo.get(st, []):
                            task(i, e)

                pairs(dve, body)

            @block.gpsimd
            def _(pool):
                pool.memset(causal[:], 1.0).then_inc(causal_set, 1)
                pool.wait_ge(causal_set, 1)
                pool.affine_select(out=causal[:], in_=causal[:], compare_op=ALU.is_ge, fill=0.0, base=0,
                                   pattern=[[0, HALF], [1, P]], channel_multiplier=-1).then_inc(causal_set, 1)
                pool.wait_ge(causal_set, 2)

                def body(i, last):
                    for st in diags:
                        o = offset(st)
                        for h in range(2):
                            pool.wait_ge(clip_done, 2 * N * i + 2 * st + h + 1)
                            tile = probs[:, st % NPROB, h * HALF:(h + 1) * HALF, o:o + P]
                            nc.gpsimd.tensor_tensor(tile, tile, causal[:], ALU.mult).then_inc(mask_done, 1)

                pairs(pool, body)

            @block.tensor
            def _(pe):
                pe.sem_inc(pv_done, NPROB)
                pe.wait_ge(ident_loaded, 16)

                def scores(i, st):
                    s, c, kt = steps[st]
                    o = offset(st)
                    if st in starts and c == 0:
                        pe.wait_ge(loaded[s], 16 * LOADS * (i + 1))
                    for h in range(2):
                        hs = 2 * st + h
                        pe.wait_ge(exp_done, 2 * N * i + before[hs] + 1 + NBUF)
                        for j in range(HALF):
                            mm = nc.tensor.matmul(ps_s[:, bufs[hs], j, o:CH], k[:, s, h * HALF + j, kt * P:(kt + 1) * P],
                                                  q[:, s, h * HALF + j, c * CH + o:(c + 1) * CH], start=True, stop=True)
                        mm.then_inc(qk_done, 1)

                def values(i, st):
                    s, c, kt = steps[st]
                    o = offset(st)
                    e = s * CPB + c
                    if st in starts:
                        pe.wait_ge(norm_done, NC * i + e - 2 + 1 + 2)
                    if st in diags:
                        pe.wait_ge(mask_done, 2 * len(diags) * i + 2 * diags.index(st) + 2)
                    else:
                        pe.wait_ge(clip_done, 2 * N * i + 2 * st + 2)
                    for j in range(GH):
                        mm = nc.tensor.matmul(ps_o[j * VW:(j + 1) * VW, c % 2, o:CH], v[:, s, kt, j * VW:(j + 1) * VW],
                                              probs[:, st % NPROB, j, o:CH], start=(st in starts), stop=(st in ends),
                                              tile_position=(0, j * VW))
                    mm.then_inc(pv_done, 1)

                def tokens(i, e):
                    pe.wait_ge(ot_done, NC * i + e + 1)
                    for j in range(TPC):
                        mm = nc.tensor.transpose(ps_o[:, e % 2, j * P:(j + 1) * P], o_t[:, e % 2, j * P:(j + 1) * P], ident[:])
                    mm.then_inc(tok_done, 1)

                for st in range(AHEAD):
                    scores(0, st)
                for st in range(LEAD):
                    scores(0, st + AHEAD)
                    values(0, st)

                def body(i, last):
                    todo = {}
                    for e, st in enumerate(ends):
                        todo.setdefault(st + 2, []).append(e)
                    for st in range(LEAD, N + LEAD):
                        if st + AHEAD < N:
                            scores(i, st + AHEAD)
                        elif not last:
                            scores(i + 1, st + AHEAD - N)
                        if st < N:
                            values(i, st)
                        elif not last:
                            values(i + 1, st - N)
                        for e in todo.get(st, []):
                            tokens(i, e)

                pairs(pe, body)


def layer1_output(nc, a, d, out):
    with ExitStack() as ctx:
        def sb(name, shape, dt=F32):
            return ctx.enter_context(nc.sbuf_tensor(name, shape, dt))

        def sem(name):
            return ctx.enter_context(nc.semaphore(name))

        ident = sb("d_ident", [P, P])
        SLOTS = 4
        w_o = sb("d_wo", [P, KT, DIM])
        attn = sb("d_attn", [P, SLOTS, TPC, DIM])
        gate = sb("d_gate", [P, SLOTS, TPC, DIM])
        x1 = sb("d_x1", [P, SLOTS, TPC, DIM])
        attn_t = sb("d_attn_t", [P, 2, KT, CH])
        prod = sb("d_prod", [P, SLOTS, TPC, DIM])
        ps_t = ctx.enter_context(nc.psum_tensor("d_ps_t", [P, 2, KT, CH], F32))
        ps_o = ctx.enter_context(nc.psum_tensor("d_ps_o", [P, 2, TPC, DIM], F32))

        weights_loaded = sem("d_weights_loaded")
        attn_loaded = [sem(f"d_attn_loaded{i}") for i in range(SLOTS)]
        rest_loaded = [sem(f"d_rest_loaded{i}") for i in range(SLOTS)]
        stored = [sem(f"d_stored{i}") for i in range(SLOTS)]
        t_mm = sem("d_t_mm")
        t_done = sem("d_t_done")
        out_mm = sem("d_out_mm")
        prod_done = sem("d_prod_done")
        sum_done = sem("d_sum_done")

        def view(t):
            return t.rearrange("(n j p) c -> n p j c", j=TPC, p=P)

        attn_v, gate_v, x1_v, out_v = view(d["attn"]), view(d["gate"]), view(d["x1"]), view(out)

        ROUNDS = NCH // SLOTS

        def rounds(eng, body):
            with eng.Fori(0, ROUNDS - 1) as i:
                body(i, False)
            body(ROUNDS - 1, True)

        with nc.Block() as block:
            @block.sync
            def _(sp):
                for s in range(SLOTS):
                    sp.sem_inc(stored[s], 16)

                def load(n, s):
                    sp.dma_start(attn[:, s], attn_v[n]).then_inc(attn_loaded[s], 16)
                    sp.dma_start(gate[:, s], gate_v[n]).then_inc(rest_loaded[s], 16)
                    sp.dma_start(x1[:, s], x1_v[n]).then_inc(rest_loaded[s], 16)

                sp.dma_start(ident[:], d["ident"]).then_inc(weights_loaded, 16)
                sp.dma_start(w_o[:], a["W_O"].rearrange("(k p) n -> p k n", p=P)).then_inc(weights_loaded, 16)
                for s in range(SLOTS):
                    load(s, s)

                def body(i, last):
                    for s in range(SLOTS):
                        n = SLOTS * i + s
                        sp.wait_ge(sum_done, n + 1)
                        sp.dma_start(out_v[n], prod[:, s]).then_inc(stored[s], 16)
                        if not last:
                            load(n + SLOTS, s)

                rounds(sp, body)
                for s in range(SLOTS):
                    sp.wait_ge(stored[s], 16 * ROUNDS + 16)

            @block.tensor
            def _(pe):
                pe.sem_inc(out_mm, 2)
                pe.wait_ge(weights_loaded, 32)

                def transposes(i, s):
                    pe.wait_ge(attn_loaded[s], 16 * i + 16)
                    for k in range(KT):
                        for j in range(TPC):
                            mm = nc.tensor.transpose(ps_t[:, s % 2, k, j * P:(j + 1) * P], attn[:, s, j, k * P:(k + 1) * P], ident[:])
                    mm.then_inc(t_mm, 1)

                def product(i, s):
                    n = SLOTS * i + s
                    pe.wait_ge(t_done, n + 1)
                    pe.wait_ge(prod_done, n + 1)
                    for j in range(TPC):
                        for k in range(KT):
                            mm = nc.tensor.matmul(ps_o[:, s % 2, j, :], attn_t[:, s % 2, k, j * P:(j + 1) * P], w_o[:, k, :],
                                                  start=(k == 0), stop=(k == KT - 1))
                    mm.then_inc(out_mm, 1)

                transposes(0, 0)

                def body(i, last):
                    for s in range(SLOTS):
                        if s + 1 < SLOTS:
                            transposes(i, s + 1)
                        elif not last:
                            transposes(i + 1, 0)
                        product(i, s)

                rounds(pe, body)

            @block.scalar
            def _(act):
                def body(i, last):
                    for s in range(SLOTS):
                        n = SLOTS * i + s
                        act.wait_ge(t_mm, n + 1)
                        act.wait_ge(out_mm, n + 1)
                        nc.scalar.activation(attn_t[:, s % 2], ps_t[:, s % 2], ACT.Copy).then_inc(t_done, 1)

                rounds(act, body)

            @block.vector
            def _(dve):
                dve.sem_inc(prod_done, 2)

                def body(i, last):
                    for s in range(SLOTS):
                        n = SLOTS * i + s
                        dve.wait_ge(rest_loaded[s], 32 * i + 32)
                        dve.wait_ge(out_mm, n + 1 + 2)
                        dve.wait_ge(stored[s], 16 * i + 16)
                        nc.vector.tensor_tensor(prod[:, s], ps_o[:, s % 2], gate[:, s], ALU.mult).then_inc(prod_done, 1)
                        dve.wait_ge(prod_done, n + 1 + 2)
                        nc.vector.tensor_tensor(prod[:, s], prod[:, s], x1[:, s], ALU.add).then_inc(sum_done, 1)

                rounds(dve, body)


def build(nc, a, out):
    d = scratch(nc)
    d["ident"] = a["ident"]
    layer0(nc, a, d["x1"])
    with nc.sbuf_tensor("score_scale", [P, 1], F32) as score_scale:
        layer1_projections(nc, a, d, score_scale)
        attention(nc, d, score_scale)
    layer1_output(nc, a, d, out)


def rotary_tables():
    inv = np.float32(10000.0) ** (-np.arange(0, D_R, 2, dtype=np.float32) / np.float32(D_R))
    ang = np.arange(SEQ, dtype=np.float32)[None, :] * inv.astype(np.float32)[:, None]
    cos = np.repeat(np.cos(ang), 2, axis=0)
    sin = np.repeat(np.sin(ang), 2, axis=0)
    sin[0::2] *= -1
    return (np.ascontiguousarray(np.tile(t, (HEADS, 1)).astype(np.float32)) for t in (cos, sin))


def layout(inputs):
    i = {k: np.asarray(v) for k, v in inputs.items()}
    cols = lambda v: np.reshape(v, (-1, P)).T
    swap = lambda w: np.reshape(np.reshape(w, (w.shape[0], -1, 2))[:, :, ::-1], w.shape)
    zeros = np.zeros((LATENT, DIM + 2 * HEADS * D_R), np.float32)
    w_qr, w_kr = i["L1_attn_W_QR"], i["L1_attn_W_KR"]
    cos, sin = rotary_tables()
    arrays = {
        "x": np.reshape(i["L0_attn_x"], (TOKENS, DIM)),
        "ident": np.eye(P, dtype=np.float32),
        "WrT": i["L0_attn_Wr"].T, "WkT": i["L0_attn_Wk"].T, "WvT": i["L0_attn_Wv"].T, "WoT": i["L0_attn_Wo"].T,
        "W1": i["L0_ffn_W1"], "W2": i["L0_ffn_W2"], "b1": cols(i["L0_ffn_b1"]), "b2": i["L0_ffn_b2"],
        "time_decay": cols(i["L0_attn_time_decay"]), "time_first": cols(i["L0_attn_time_first"]),
        "mixes": np.concatenate([cols(i["L0_attn_mix_" + n]) for n in "rkv"], axis=1),
        "Wc": np.concatenate([i["L1_attn_W_DQ"], i["L1_attn_W_DKV"]], axis=1),
        "Wkr": np.concatenate([w_kr] * (VW // D_R) + [swap(w_kr)], axis=1),
        "Wq": np.concatenate([np.concatenate([i["L1_attn_W_UQ"], w_qr, swap(w_qr)], axis=1), zeros], axis=0),
        "Wuk": np.concatenate([zeros[:, :DIM], i["L1_attn_W_UK"]], axis=0),
        "Wuv": np.concatenate([zeros[:, :DIM], i["L1_attn_W_UV"]], axis=0),
        "W_O": i["L1_attn_W_O"],
        "W1rT": i["L1_ffn_W_r"].T, "W1kT": i["L1_ffn_W_k"].T, "W1vT": i["L1_ffn_W_v"].T,
        "mixes1": np.concatenate([cols(i["L1_ffn_mu_r"]), cols(i["L1_ffn_mu_k"])], axis=1),
        "cos": cos, "sin": sin,
    }
    return {k: np.ascontiguousarray(v) for k, v in arrays.items()}


def kernel(**inputs):
    import concourse.bacc as bacc
    from concourse.bass_utils import run_bass_kernel_spmd

    nc = bacc.Bacc("TRN2", target_bir_lowering=False, num_devices=1)
    arrays = layout(inputs)
    a = {k: nc.dram_tensor(f"in_{k}", list(v.shape), mybir.dt.from_np(v.dtype), kind="ExternalInput").ap() for k, v in arrays.items()}
    out = nc.dram_tensor("out", [TOKENS, DIM], F32, kind="ExternalOutput").ap()
    build(nc, a, out)
    r = run_bass_kernel_spmd(nc, [{f"in_{k}": v for k, v in arrays.items()}], core_ids=[0])
    return r.results[0]["out"].reshape(BATCH, SEQ, DIM)
```

```python
from contextlib import ExitStack

import numpy as np
import concourse.bass as bass
import concourse.mybir as mybir

F32 = mybir.dt.float32
F16 = mybir.dt.float16
I32 = mybir.dt.int32
ALU = mybir.AluOpType
ACT = mybir.ActivationFunctionType

P = 128
BATCH, SEQ, DIM = 4, 2048, 256
TOKENS = BATCH * SEQ
KT = DIM // P
CH = 512
NCH = TOKENS // CH
CPB = SEQ // CH
TPC = CH // P
TILES = TOKENS // P
INTER = 1024
MT = INTER // P
HEADS, D_H, D_R, LATENT = 16, 16, 8, 64
D_QK = D_H + D_R
GH = 4
GROUPS = HEADS // GH
VW = 32
KROWS = 4 * D_QK
KEYT = SEQ // P
LN_EPS = 1e-5
MAX_INIT = -1e38
EXP_CAP = 30.0
CLIP = 80.0
INV_SQRT = float(1.0 / np.sqrt(np.float32(D_QK)))
P_MAX = float(np.exp(CLIP * INV_SQRT))
P_MIN = float(np.exp(-CLIP * INV_SQRT))
F16_TARGET = 16384.0
X_TARGET = 2048.0


def layer0(nc, a, x1_d):
    with ExitStack() as ctx:
        def sb(name, shape, dt=F32):
            return ctx.enter_context(nc.sbuf_tensor(name, shape, dt))

        def sem(name):
            return ctx.enter_context(nc.semaphore(name))

        RING = 4
        X = CPB
        ident = sb("a_ident", [P, P])
        ones = sb("a_ones", [P, P])
        w_o = sb("a_wo", [P, KT, DIM])
        w_r, w_k, w_v = (sb(f"a_w{n}", [P, 2, KT, DIM], F16) for n in "rkv")
        w_1 = sb("a_w1", [P, 2, KT, INTER], F16)
        w_2 = sb("a_w2", [P, 2, MT, DIM], F16)
        b_1 = sb("a_b1", [P, MT])
        b_2 = sb("a_b2", [P, DIM])
        mixes = sb("a_mixes", [P, 3, KT])
        decay = sb("a_decay", [P, KT])
        first = sb("a_first", [P, KT])
        cap = sb("a_cap", [P, 1])
        zero_col = sb("a_zero", [P, KT, 1])
        eps = sb("a_eps", [P, TPC])
        half = sb("a_half", [P, TPC])
        sums = sb("a_sums", [P, 7])
        roots = sb("a_roots", [P, 7])
        bound = sb("a_bound", [P, 7])
        power = sb("a_power", [P, 7])
        scale = sb("a_scale", [P, 7])
        unscale = sb("a_unscale", [P, 5])
        neg_k = sb("a_neg_k", [P, 1])
        key_scale = sb("a_key_scale", [P, 1])
        stats = sb("a_stats", [P, TPC, 6])
        mv = sb("a_mv", [P, TPC, 2])
        var_eps = sb("a_var", [P, TPC])
        rstd = sb("a_rstd", [P, TPC])
        x = sb("a_x", [P, X, TPC, DIM])
        xhat = sb("a_xhat", [P, TPC, DIM])
        xn = sb("a_xn", [P, 2, KT, CH + 1])
        xn_half = sb("a_xnh", [P, 2, 2, KT, CH], F16)
        diff = sb("a_diff", [P, KT, CH])
        mixed = sb("a_mixed", [P, 3, KT, CH])
        mixed_half = sb("a_mixedh", [P, 3, 2, KT, CH], F16)
        sig_r = sb("a_sigr", [P, KT, CH])
        mx = sb("a_mx", [P, KT, CH + 1])
        num = sb("a_num", [P, KT, CH + 1])
        den = sb("a_den", [P, KT, CH + 1])
        dist = sb("a_dist", [P, KT, CH])
        e_bonus = sb("a_eb", [P, KT, CH])
        e_old = sb("a_eo", [P, KT, CH])
        e_new = sb("a_en", [P, KT, CH])
        new_v = sb("a_nv", [P, KT, CH])
        out_num = sb("a_on", [P, KT, CH])
        out_den = sb("a_od", [P, KT, CH])
        rwkv = sb("a_rwkv", [P, KT, CH])
        hid = sb("a_hid", [P, RING, CH])
        hid_half = sb("a_hidh", [P, 2, MT, CH], F16)
        gate_parts = sb("a_gp", [P, 2, TPC, DIM])
        gate = sb("a_gate", [P, TPC, DIM])
        prod = sb("a_prod", [P, TPC, DIM])
        x1 = sb("a_x1", [P, 2, TPC, DIM])
        gate_in, gate_sig = gate_parts[:, 0], gate_parts[:, 1]
        early = x1[:].rearrange("p s j d -> p (s j d)")
        raw_rkv = [early[:, i * KT * DIM:(i + 1) * KT * DIM].rearrange("p (k d) -> p k d", k=KT) for i in range(3)]
        raw_1 = gate_parts[:].rearrange("p s j d -> p (s j d)").rearrange("p (k n) -> p k n", k=KT)
        raw_2 = hid[:].rearrange("p r c -> p (r c)").rearrange("p (m d) -> p m d", m=MT)
        squares = mixed[:].rearrange("p i k c -> p (i k c)")
        raw = raw_rkv + [raw_1, raw_2]
        split = [w_r, w_k, w_v, w_1, w_2]

        ps_a = ctx.enter_context(nc.psum_tensor("a_ps0", [P, 2, CH], F32))
        ps_b = ctx.enter_context(nc.psum_tensor("a_ps1", [P, 2, CH], F32))
        ps_c = ctx.enter_context(nc.psum_tensor("a_ps2", [P, 2, CH], F32))
        ps_t = ctx.enter_context(nc.psum_tensor("a_ps3", [P, 2, CH], F32))
        ps_ffn = ps_b[:].rearrange("p a (j d) -> p (a j) d", d=DIM)
        ps_out = ps_t[:].rearrange("p a (j d) -> p (a j) d", d=DIM)

        weights_loaded = [sem(f"a_weights_loaded{i}") for i in range(len(raw))]
        wo_loaded = sem("a_wo_loaded")
        small_loaded = sem("a_small_loaded")
        x_loaded = [sem(f"a_x_loaded{i}") for i in range(X)]
        x1_stored = [sem(f"a_x1_stored{i}") for i in range(2)]
        consts_set = sem("a_consts_set")
        decay_exp = sem("a_decay_exp")
        squares_done = sem("a_squares_done")
        sums_done = sem("a_sums_done")
        roots_done = sem("a_roots_done")
        bound_done = sem("a_bound_done")
        scale_done = sem("a_scale_done")
        consts_done = sem("a_consts_done")
        w_high = sem("a_w_high")
        w_low = sem("a_w_low")
        stats_done = sem("a_stats_done")
        mv_done = sem("a_mv_done")
        var_done = sem("a_var_done")
        rstd_done = sem("a_rstd_done")
        xhat_done = sem("a_xhat_done")
        xt_done = sem("a_xt_done")
        xn_done = sem("a_xn_done")
        xn_high = sem("a_xn_high")
        xn_low = sem("a_xn_low")
        diff_done = sem("a_diff_done")
        mix_done = sem("a_mix_done")
        mix_high = sem("a_mix_high")
        mix_low = sem("a_mix_low")
        r_done = sem("a_r_done")
        k_done = sem("a_k_done")
        v_done = sem("a_v_done")
        hid_mm = sem("a_hid_mm")
        hid_done = sem("a_hid_done")
        hid_high = sem("a_hid_high")
        hid_low = sem("a_hid_low")
        ffn_done = sem("a_ffn_done")
        out_done = sem("a_out_done")
        sig_done = sem("a_sig_done")
        state_set = sem("a_state_set")
        mx_done = sem("a_mx_done")
        dist_done = sem("a_dist_done")
        arg_done = sem("a_arg_done")
        exp_done = sem("a_exp_done")
        new_done = sem("a_new_done")
        scan_done = sem("a_scan_done")
        bonus_done = sem("a_bonus_done")
        num_done = sem("a_num_done")
        den_done = sem("a_den_done")
        ln_done = sem("a_ln_done")
        rden_done = sem("a_rden_done")
        q_done = sem("a_q_done")
        rwkv_done = sem("a_rwkv_done")
        gate_in_done = sem("a_gate_in_done")
        gate_sig_done = sem("a_gate_sig_done")
        gate_done = sem("a_gate_done")
        prod_done = sem("a_prod_done")
        x1_done = sem("a_x1_done")

        x_v3 = a["x"].rearrange("(n j p) c -> n p j c", j=TPC, p=P)
        x1_v3 = x1_d.rearrange("(n j p) c -> n p j c", j=TPC, p=P)

        def chunks(eng, body):
            with eng.Fori(0, BATCH - 1) as b:
                for c in range(CPB):
                    body(b, c, CPB)
            for c in range(CPB):
                body(BATCH - 1, c, CPB - 1 - c)

        def count(b, c):
            return b * CPB + c

        with nc.Block() as block:
            @block.sync
            def _(sp):
                for s in range(2):
                    sp.sem_inc(x1_stored[s], 16)
                sp.dma_start(x[:, 0], x_v3[0]).then_inc(x_loaded[0], 16)
                for i, name in enumerate(("WrT", "WkT", "WvT")):
                    sp.dma_start(raw_rkv[i], a[name].rearrange("(k p) d -> p k d", p=P)).then_inc(weights_loaded[i], 16)
                for s in range(1, X):
                    sp.dma_start(x[:, s], x_v3[s]).then_inc(x_loaded[s], 16)
                sp.dma_start(w_o[:], a["WoT"].rearrange("(k p) d -> p k d", p=P)).then_inc(wo_loaded, 16)

                def body(b, c, left):
                    n = count(b, c)
                    sp.wait_ge(x1_done, n + 1)
                    sp.dma_start(x1_v3[n], x1[:, c % 2]).then_inc(x1_stored[c % 2], 16)
                    if left >= X:
                        sp.dma_start(x[:, c], x_v3[n + X]).then_inc(x_loaded[c], 16)

                chunks(sp, body)
                for s in range(2):
                    sp.wait_ge(x1_stored[s], 16 * NCH // 2 + 16)

            @block.gpsimd
            def _(pool):
                for counts_from_one in (num_done, q_done, gate_done):
                    pool.sem_inc(counts_from_one, 1)
                pool.sem_inc(hid_low, RING)
                pool.dma_start(mixes[:], a["mixes"].rearrange("p (m k) -> p m k", m=3)).then_inc(small_loaded, 16)
                pool.dma_start(b_1[:], a["b1"]).then_inc(small_loaded, 16)
                pool.dma_start(ident[:], a["ident"]).then_inc(small_loaded, 16)
                pool.dma_start(decay[:], a["time_decay"]).then_inc(small_loaded, 16)
                pool.dma_start(first[:], a["time_first"]).then_inc(small_loaded, 16)
                pool.dma_start(b_2[:], a["b2"].rearrange("(o d) -> o d", o=1).to_broadcast([P, DIM])).then_inc(small_loaded, 16)
                pool.memset(half[:], -0.5).then_inc(consts_set, 1)
                pool.memset(zero_col[:], 0.0).then_inc(consts_set, 1)
                pool.memset(eps[:], LN_EPS).then_inc(consts_set, 1)
                pool.memset(ones[:], 1.0).then_inc(consts_set, 1)
                pool.wait_ge(consts_set, 4)

                def rstd_of(n):
                    pool.wait_ge(mv_done, TPC * n + TPC)
                    nc.gpsimd.tensor_tensor(var_eps[:], mv[:, :, 1], eps[:], ALU.add).then_inc(var_done, 1)
                    pool.wait_ge(var_done, n + 1)
                    nc.gpsimd.tensor_tensor(rstd[:], var_eps[:], half[:], ALU.pow).then_inc(rstd_done, 1)

                def diff_of(n, c, first=False):
                    pool.wait_ge(xn_done, 2 * n + 2)
                    if not first:
                        pool.wait_ge(mix_done, 3 * KT * n)
                    nc.gpsimd.tensor_tensor(diff[:], xn[:, c % 2, :, 1:CH + 1], xn[:, c % 2, :, 0:CH],
                                            ALU.subtract).then_inc(diff_done, 1)

                def xn_low_of(n, c):
                    pool.wait_ge(xn_high, n + 1)
                    nc.gpsimd.tensor_tensor(xn_half[:, c % 2, 1], xn[:, c % 2, :, 1:CH + 1], xn_half[:, c % 2, 0],
                                            ALU.subtract).then_inc(xn_low, 1)

                def hidden_low(n):
                    for m in range(MT):
                        pool.wait_ge(hid_high, MT * n + m + 1)
                        nc.gpsimd.tensor_tensor(hid_half[:, 1, m], hid[:, m % RING], hid_half[:, 0, m], ALU.subtract).then_inc(hid_low, 1)

                def numerator(n):
                    pool.wait_ge(bonus_done, n + 1 + 1)
                    nc.gpsimd.tensor_tensor(out_num[:], out_num[:], num[:, :, 0:CH], ALU.add).then_inc(num_done, 1)
                    pool.wait_ge(num_done, n + 1 + 1)
                    pool.wait_ge(sig_done, n + 1)
                    nc.gpsimd.tensor_tensor(out_num[:], out_num[:], sig_r[:], ALU.mult).then_inc(q_done, 1)

                rstd_of(0)
                diff_of(0, 0, first=True)
                xn_low_of(0, 0)
                rstd_of(1)
                rstd_of(2)
                diff_of(1, 1)
                hidden_low(0)
                xn_low_of(1, 1)
                numerator(0)

                def body(b, c, left):
                    n = count(b, c)
                    pool.wait_ge(gate_sig_done, n + 1)
                    pool.wait_ge(prod_done, n + 1)
                    nc.gpsimd.tensor_tensor(gate[:], gate_in, gate_sig, ALU.mult).then_inc(gate_done, 1)
                    if left >= 3:
                        rstd_of(n + 3)
                    if left >= 2:
                        diff_of(n + 2, c + 2)
                    if left >= 1:
                        hidden_low(n + 1)
                    if left >= 2:
                        xn_low_of(n + 2, c + 2)
                    if left >= 1:
                        numerator(n + 1)

                chunks(pool, body)

            @block.scalar
            def _(act):
                act.sem_inc(hid_done, 1)
                act.dma_start(raw_1, a["W1"].rearrange("(k p) d -> p k d", p=P)).then_inc(weights_loaded[3], 16)
                act.dma_start(raw_2, a["W2"].rearrange("(m p) d -> p m d", p=P)).then_inc(weights_loaded[4], 16)
                act.wait_ge(sums_done, 1)
                nc.scalar.activation(roots[:], ps_a[:, 0, 0:7], ACT.Sqrt).then_inc(roots_done, 1)
                act.wait_ge(small_loaded, 16 * 6)
                nc.scalar.activation(decay[:], decay[:], ACT.Exp).then_inc(decay_exp, 1)

                def load(name, source):
                    register = act.alloc_register(name)
                    act.load(register, source[0:1].bitcast(I32))
                    return register

                act.wait_ge(scale_done, 1)
                x_scale = load("a_x_scale", scale[:, 5:6])
                w_scales = [load(f"a_w_scale{i}", scale[:, i:i + 1]) for i in range(len(raw))]

                def weight_high(i):
                    act.wait_ge(weights_loaded[i], 16)
                    nc.scalar.activation(split[i][:, 0], raw[i], ACT.Copy, scale=w_scales[i]).then_inc(w_high, 1)

                def xn_of(n, c):
                    s = c % 2
                    if c % CPB == 0:
                        act.wait_ge(consts_set, 2)
                        before = zero_col[:]
                    else:
                        act.wait_ge(xn_done, 2 * n)
                        before = xn[:, 1 - s, :, CH:CH + 1]
                    act.wait_ge(xt_done, n + 1)
                    nc.scalar.activation(xn[:, s, :, 0:1], before, ACT.Copy).then_inc(xn_done, 1)
                    nc.scalar.activation(xn[:, s, :, 1:CH + 1], ps_t[:], ACT.Copy, scale=x_scale).then_inc(xn_done, 1)

                def xn_high_of(c):
                    nc.scalar.activation(xn_half[:, c % 2, 0], ps_t[:], ACT.Copy, scale=x_scale).then_inc(xn_high, 1)

                def mixed_high(n, first=False):
                    if not first:
                        act.wait_ge(v_done, n)
                    for i in range(3):
                        act.wait_ge(mix_done, 3 * KT * n + KT * (i + 1))
                        nc.scalar.activation(mixed_half[:, i, 0], mixed[:, i], ACT.Copy).then_inc(mix_high, 1)

                def receptance(n):
                    act.wait_ge(r_done, n + 1)
                    act.wait_ge(q_done, n + 1)
                    nc.scalar.activation(sig_r[:], ps_a[:], ACT.Sigmoid, scale=r_unscale).then_inc(sig_done, 1)
                    act.preload_act_table_set("natural_log_exp_and_others")

                def exponential(n, i):
                    e = (e_new, e_old, e_bonus)[i]
                    act.wait_ge(arg_done, 3 * KT * n + KT * (i + 1))
                    nc.scalar.activation(e[:], e[:], ACT.Exp, scale=k_negated if e is e_old else k_unscale).then_inc(exp_done, 1)

                def hidden(n, m):
                    act.wait_ge(hid_mm, MT * n + m + 1)
                    act.wait_ge(hid_low, MT * n + m + 1)
                    nc.scalar.activation(hid[:, m % RING, :], ps_a[:, m % 2, :], ACT.Relu, bias=b_1[:, m:m + 1],
                                         scale=hid_scale).then_inc(hid_done, 1)

                def hidden_high(n, m):
                    act.wait_ge(hid_done, MT * n + m + 1 + 1)
                    nc.scalar.activation(hid_half[:, 0, m], hid[:, m % RING], ACT.Copy).then_inc(hid_high, 1)

                def reciprocal(n):
                    act.wait_ge(den_done, n + 1)
                    nc.scalar.activation(out_den[:], out_den[:], ACT.Ln).then_inc(ln_done, 1)
                    act.wait_ge(ln_done, n + 1)
                    nc.scalar.activation(out_den[:], out_den[:], ACT.Exp, scale=-1.0).then_inc(rden_done, 1)

                def chunk(n, c, following):
                    receptance(n)
                    if following:
                        xn_of(n + 1, c + 1)
                    for m in range(MT):
                        if m < 3:
                            exponential(n, m)
                        hidden(n, m)
                        if m:
                            hidden_high(n, m - 1)
                        if m == 3 and following:
                            xn_high_of(c + 1)
                    hidden_high(n, MT - 1)

                for i in range(3):
                    weight_high(i)
                xn_of(0, 0)
                xn_high_of(0)
                mixed_high(0, first=True)
                act.wait_ge(consts_done, 1)
                r_unscale = load("a_r_unscale", unscale[:, 0:1])
                k_unscale = load("a_k_unscale", unscale[:, 1:2])
                k_negated = load("a_k_negated", neg_k[:])
                hid_scale = load("a_hid_scale", unscale[:, 3:4])
                for i in (3, 4):
                    weight_high(i)
                chunk(0, 0, True)
                reciprocal(0)
                mixed_high(1)

                def body(b, c, left):
                    n = count(b, c)
                    act.wait_ge(gate_in_done, n + 1 + 1)
                    nc.scalar.activation(gate_sig, gate_in, ACT.Sigmoid).then_inc(gate_sig_done, 1)
                    if left >= 1:
                        chunk(n + 1, c + 1, left >= 2)
                        reciprocal(n + 1)
                    if left >= 2:
                        mixed_high(n + 2)

                chunks(act, body)

            @block.vector
            def _(dve):
                for counts_from_one in (bonus_done, rwkv_done, gate_in_done, prod_done):
                    dve.sem_inc(counts_from_one, 1)

                def layernorm(n, c, turn):
                    dve.wait_ge(x_loaded[c % X], 16 * (turn + 1))
                    for j in range(TPC):
                        nc.vector.bn_stats(stats[:, j, :], x[:, c % X, j, :]).then_inc(stats_done, 1)

                def aggregate():
                    for j in range(TPC):
                        nc.vector.bn_aggr(mv[:, j, :], stats[:, j, :]).then_inc(mv_done, 1)

                def normalise(n, c, first=False):
                    dve.wait_ge(rstd_done, n + 1)
                    if not first:
                        dve.wait_ge(xt_done, n)
                    for j in range(TPC):
                        nc.vector.tensor_scalar(xhat[:, j, :], x[:, c % X, j, :], mv[:, j, 0:1], rstd[:, j:j + 1],
                                                ALU.subtract, ALU.mult).then_inc(xhat_done, 1)

                def mix(n, c, first=False):
                    dve.wait_ge(diff_done, n + 1)
                    for i in range(3):
                        for k in range(KT):
                            nc.vector.scalar_tensor_tensor(mixed[:, i, k, :], diff[:, k, :], mixes[:, i, k:k + 1],
                                                           xn[:, c % 2, k, 0:CH], ALU.mult, ALU.add).then_inc(mix_done, 1)
                    if not first:
                        dve.wait_ge(v_done, n)
                    for i in range(3):
                        dve.wait_ge(mix_high, 3 * n + i + 1)
                        nc.vector.tensor_tensor(mixed_half[:, i, 1], mixed[:, i], mixed_half[:, i, 0], ALU.subtract).then_inc(mix_low, 1)

                def weight_low(i):
                    dve.wait_ge(w_high, i + 1)
                    nc.vector.scalar_tensor_tensor(split[i][:, 1], raw[i], scale[:, i:i + 1], split[i][:, 0],
                                                   ALU.mult, ALU.subtract).then_inc(w_low, 1)

                def old_states(n, c):
                    dve.wait_ge(num_done, n + 1)
                    if c % CPB == 0:
                        nc.vector.memset(mx[:, :, 0:1], MAX_INIT).then_inc(state_set, 1)
                        nc.vector.memset(num[:, :, 0:1], 0.0).then_inc(state_set, 1)
                        nc.vector.memset(den[:, :, 0:1], 0.0).then_inc(state_set, 1)
                    else:
                        for t in (mx, num, den):
                            nc.vector.tensor_copy(t[:, :, 0:1], t[:, :, CH:CH + 1]).then_inc(state_set, 1)

                def keys(n):
                    dve.wait_ge(state_set, 3 * n + 3)
                    dve.wait_ge(k_done, n + 1)
                    for k in range(KT):
                        nc.vector.tensor_tensor_scan(mx[:, k, 1:CH + 1], decay[:, k:k + 1].to_broadcast([P, CH]),
                                                     ps_b[:, k, :], mx[:, k, 0:1], ALU.add, ALU.max).then_inc(mx_done, 1)
                    dve.wait_ge(mx_done, KT * n + KT)
                    nc.vector.tensor_tensor(dist[:], ps_b[:], mx[:, :, 0:CH], ALU.subtract).then_inc(dist_done, 1)
                    dve.wait_ge(dist_done, n + 1)
                    for k in range(KT):
                        nc.vector.tensor_scalar(e_new[:, k, :], dist[:, k, :], decay[:, k:k + 1], 0.0,
                                                ALU.subtract, ALU.min).then_inc(arg_done, 1)
                    for k in range(KT):
                        nc.vector.tensor_scalar(e_old[:, k, :], dist[:, k, :], decay[:, k:k + 1], 0.0,
                                                ALU.subtract, ALU.max).then_inc(arg_done, 1)
                    for k in range(KT):
                        nc.vector.tensor_scalar(e_bonus[:, k, :], dist[:, k, :], first[:, k:k + 1], cap[:],
                                                ALU.add, ALU.min).then_inc(arg_done, 1)

                def states(n):
                    dve.wait_ge(exp_done, 3 * n + 1)
                    dve.wait_ge(v_done, n + 1)
                    nc.vector.scalar_tensor_tensor(new_v[:], ps_c[:], unscale[:, 2:3], e_new[:], ALU.mult, ALU.mult).then_inc(new_done, 1)
                    dve.wait_ge(exp_done, 3 * n + 2)
                    for k in range(KT):
                        nc.vector.tensor_tensor_scan(den[:, k, 1:CH + 1], e_old[:, k, :], e_new[:, k, :],
                                                     den[:, k, 0:1], ALU.mult, ALU.add).then_inc(scan_done, 1)
                    dve.wait_ge(new_done, n + 1)
                    for k in range(KT):
                        nc.vector.tensor_tensor_scan(num[:, k, 1:CH + 1], e_old[:, k, :], new_v[:, k, :],
                                                     num[:, k, 0:1], ALU.mult, ALU.add).then_inc(scan_done, 1)
                    dve.wait_ge(exp_done, 3 * n + 3)
                    dve.wait_ge(rwkv_done, n + 1)
                    dve.wait_ge(scan_done, 2 * KT * n + 2 * KT)
                    nc.vector.scalar_tensor_tensor(out_num[:], ps_c[:], unscale[:, 2:3], e_bonus[:], ALU.mult, ALU.mult).then_inc(bonus_done, 1)
                    nc.vector.tensor_tensor(out_den[:], e_bonus[:], den[:, :, 0:CH], ALU.add).then_inc(den_done, 1)

                dve.wait_ge(small_loaded, 16 * 6)
                for i, t in enumerate(raw + [mixes[:], b_1[:]]):
                    size = t.free_size()
                    if i < len(raw):
                        dve.wait_ge(weights_loaded[i], 16)
                    if i:
                        dve.wait_ge(squares_done, i)
                    sq = squares[:, 0:size]
                    if len(t.shape) == 3:
                        sq = sq.rearrange("p (k n) -> p k n", k=t.shape[1])
                    nc.vector.tensor_tensor_reduce(out=sq, in0=t, in1=t, scale=1.0, scalar=0.0, op0=ALU.mult, op1=ALU.add,
                                                   accum_out=sums[:, i:i + 1]).then_inc(squares_done, 1)
                layernorm(0, 0, 0)
                dve.wait_ge(stats_done, TPC)
                aggregate()
                dve.wait_ge(roots_done, 1)
                xn_max = float(np.sqrt(DIM))
                nc.vector.tensor_scalar(bound[:, 0:5], roots[:, 0:5], 1e-20, None, ALU.max).then_inc(bound_done, 1)
                nc.vector.tensor_scalar(bound[:, 5:6], roots[:, 5:6], 2.0 * xn_max, xn_max, ALU.mult, ALU.add).then_inc(bound_done, 1)
                nc.vector.tensor_scalar(bound[:, 6:7], roots[:, 3:4], xn_max, 1e-20, ALU.mult, ALU.max).then_inc(bound_done, 1)
                dve.wait_ge(bound_done, 3)
                nc.vector.tensor_tensor(bound[:, 6:7], bound[:, 6:7], roots[:, 6:7], ALU.add).then_inc(bound_done, 1)
                dve.wait_ge(bound_done, 4)
                nc.vector.tensor_scalar(power[:].bitcast(I32), bound[:].bitcast(I32), 0x7F800000, None,
                                        ALU.bitwise_and).then_inc(bound_done, 1)
                dve.wait_ge(bound_done, 5)
                nc.vector.reciprocal(scale[:], power[:]).then_inc(bound_done, 1)
                nc.vector.tensor_scalar(unscale[:, 0:4], power[:, 0:4], power[:, 5:6], 1.0 / (F16_TARGET * X_TARGET),
                                        ALU.mult, ALU.mult).then_inc(bound_done, 1)
                nc.vector.tensor_scalar(unscale[:, 4:5], power[:, 4:5], power[:, 6:7], 1.0 / (F16_TARGET * F16_TARGET),
                                        ALU.mult, ALU.mult).then_inc(bound_done, 1)
                dve.wait_ge(bound_done, 8)
                nc.vector.tensor_scalar(scale[:, 0:5], scale[:, 0:5], F16_TARGET, None, ALU.mult)
                nc.vector.tensor_scalar(scale[:, 5:6], scale[:, 5:6], X_TARGET, None, ALU.mult)
                nc.vector.tensor_scalar(scale[:, 6:7], scale[:, 6:7], F16_TARGET, None, ALU.mult).then_inc(scale_done, 1)
                dve.wait_ge(scale_done, 1)
                normalise(0, 0, first=True)
                nc.vector.tensor_tensor(key_scale[:], scale[:, 1:2], scale[:, 5:6], ALU.mult).then_inc(bound_done, 1)
                nc.vector.tensor_scalar(neg_k[:], unscale[:, 1:2], -1.0, None, ALU.mult)
                nc.vector.tensor_tensor(unscale[:, 3:4], unscale[:, 3:4], scale[:, 6:7], ALU.mult)
                nc.vector.tensor_scalar(b_1[:], b_1[:], scale[:, 6:7], None, ALU.mult)
                dve.wait_ge(decay_exp, 1)
                dve.wait_ge(bound_done, 9)
                nc.vector.tensor_scalar(decay[:], decay[:], key_scale[:], -1.0, ALU.mult, ALU.mult)
                nc.vector.tensor_scalar(first[:], first[:], key_scale[:], None, ALU.mult)
                nc.vector.tensor_scalar(cap[:], key_scale[:], EXP_CAP, None, ALU.mult).then_inc(consts_done, 1)
                for i in range(3):
                    weight_low(i)
                layernorm(1, 1, 0)
                dve.wait_ge(stats_done, 2 * TPC)
                aggregate()
                mix(0, 0, first=True)
                normalise(1, 1)
                for i in (3, 4):
                    weight_low(i)
                layernorm(2, 2, 0)
                dve.wait_ge(stats_done, 3 * TPC)
                dve.wait_ge(consts_done, 1)
                aggregate()
                old_states(0, 0)
                keys(0)
                normalise(2, 2)
                states(0)
                mix(1, 1)

                def body(b, c, left):
                    n = count(b, c)
                    dve.wait_ge(ffn_done, n + 1)
                    dve.wait_ge(gate_done, n + 1)
                    nc.vector.scalar_tensor_tensor(gate_in, ps_ffn, unscale[:, 4:5],
                                                   b_2[:].rearrange("p (o d) -> p o d", o=1).to_broadcast([P, TPC, DIM]),
                                                   ALU.mult, ALU.add).then_inc(gate_in_done, 1)
                    dve.wait_ge(q_done, n + 1 + 1)
                    dve.wait_ge(rden_done, n + 1)
                    dve.wait_ge(out_done, n + 1)
                    nc.vector.tensor_tensor(rwkv[:], out_num[:], out_den[:], ALU.mult).then_inc(rwkv_done, 1)
                    if left >= 3:
                        layernorm(n + 3, c + 3, b + (c + 3) // X)
                        dve.wait_ge(stats_done, TPC * (n + 3) + TPC)
                    if left >= 1:
                        old_states(n + 1, c + 1)
                    if left >= 3:
                        aggregate()
                    if left >= 1:
                        keys(n + 1)
                    if left >= 1:
                        states(n + 1)
                    if left >= 3:
                        normalise(n + 3, c + 3)
                    if left >= 2:
                        mix(n + 2, c + 2)
                    dve.wait_ge(out_done, n + 1 + 1)
                    dve.wait_ge(gate_done, n + 1 + 1)
                    nc.vector.tensor_tensor(prod[:], ps_out, gate[:], ALU.mult).then_inc(prod_done, 1)
                    dve.wait_ge(prod_done, n + 1 + 1)
                    dve.wait_ge(x1_stored[c % 2], 16 * (b * (CPB // 2) + c // 2) + 16)
                    nc.vector.tensor_tensor(x1[:, c % 2], prod[:], x[:, c], ALU.add).then_inc(x1_done, 1)

                chunks(dve, body)

            @block.tensor
            def _(pe):
                pe.sem_inc(out_done, 1)

                def products(ps, pairs):
                    steps = [(l[h], r[g]) for l, r in pairs for h, g in ((0, 0), (0, 1), (1, 0))]
                    for i, (l, r) in enumerate(steps):
                        mm = nc.tensor.matmul(ps, l, r, start=(i == 0), stop=(i == len(steps) - 1))
                    return mm

                def halves(t, *at):
                    return [t[(slice(None), h) + at] for h in range(2)]

                def transposes(n):
                    pe.wait_ge(xhat_done, TPC * n + TPC)
                    for k in range(KT):
                        for j in range(TPC):
                            last = nc.tensor.transpose(ps_t[:, k, j * P:(j + 1) * P], xhat[:, j, k * P:(k + 1) * P], ident[:])
                    last.then_inc(xt_done, 1)

                def project(ps, w, i):
                    for m in range(KT):
                        last = products(ps[:, m, :], [(halves(w, k, slice(m * P, (m + 1) * P)),
                                                       [mixed_half[:, i, h, k, :] for h in range(2)]) for k in range(KT)])
                    return last

                def projections(n):
                    pe.wait_ge(hid_done, MT * n + 1)
                    pe.wait_ge(mix_low, 3 * n + 1)
                    project(ps_a, w_r, 0).then_inc(r_done, 1)
                    pe.wait_ge(gate_in_done, n + 1)
                    pe.wait_ge(mix_low, 3 * n + 2)
                    project(ps_b, w_k, 1).then_inc(k_done, 1)
                    pe.wait_ge(bonus_done, n + 1)
                    pe.wait_ge(mix_low, 3 * n + 3)
                    project(ps_c, w_v, 2).then_inc(v_done, 1)

                def hidden(n, c):
                    pe.wait_ge(xn_low, n + 1)
                    for m in range(MT):
                        if m < 2:
                            pe.wait_ge(sig_done, n + 1)
                        else:
                            pe.wait_ge(hid_done, MT * n + m - 1 + 1)
                        products(ps_a[:, m % 2, :], [(halves(w_1, k, slice(m * P, (m + 1) * P)),
                                                      [xn_half[:, c % 2, h, k, :] for h in range(2)])
                                                     for k in range(KT)]).then_inc(hid_mm, 1)

                def ffn(n):
                    pe.wait_ge(hid_low, MT * n + MT + RING)
                    pe.wait_ge(dist_done, n + 1)
                    for j in range(TPC):
                        mm = products(ps_ffn[:, j, :], [(halves(hid_half, m, slice(j * P, (j + 1) * P)), halves(w_2, m))
                                                        for m in range(MT)])
                    mm.then_inc(ffn_done, 1)

                pe.wait_ge(consts_set, 4)
                pe.wait_ge(squares_done, 7)
                nc.tensor.matmul(ps_a[:, 0, 0:7], ones[:], sums[:], start=True, stop=True).then_inc(sums_done, 1)
                pe.wait_ge(small_loaded, 16 * 6)
                pe.wait_ge(roots_done, 1)
                transposes(0)
                pe.wait_ge(w_low, 3)
                projections(0)
                pe.wait_ge(xn_high, 1)
                transposes(1)
                pe.wait_ge(w_low, 5)
                hidden(0, 0)
                ffn(0)
                pe.wait_ge(wo_loaded, 16)

                def body(b, c, left):
                    n = count(b, c)
                    if left >= 1:
                        projections(n + 1)
                    if left >= 2:
                        pe.wait_ge(prod_done, n + 1)
                        pe.wait_ge(xn_high, n + 2)
                        transposes(n + 2)
                    if left >= 1:
                        hidden(n + 1, c + 1)
                    pe.wait_ge(rwkv_done, n + 1 + 1)
                    if left >= 2:
                        pe.wait_ge(xn_high, n + 3)
                    pe.wait_ge(prod_done, n + 1)
                    for j in range(TPC):
                        for k in range(KT):
                            mm = nc.tensor.matmul(ps_out[:, j, :], rwkv[:, k, j * P:(j + 1) * P], w_o[:, k, :],
                                                  start=(k == 0), stop=(k == KT - 1))
                    mm.then_inc(out_done, 1)
                    if left >= 1:
                        ffn(n + 1)

                chunks(pe, body)


def scratch(nc):
    def dram(name, shape, dt=F32):
        return nc.dram_tensor(name, shape, dt, kind="Internal").ap()

    return {
        "x1": dram("x1_d", [TOKENS, DIM]),
        "qc": dram("qc_d", [BATCH, 2, DIM, SEQ], F16),
        "qr": dram("qr_d", [BATCH, 2, HEADS * D_R, SEQ], F16),
        "kc": dram("kc_d", [BATCH, 2, DIM, SEQ], F16),
        "kr": dram("kr_d", [BATCH, 2, D_R, SEQ], F16),
        "v": dram("v_d", [TOKENS, HEADS * VW]),
        "gate": dram("gate_d", [TOKENS, DIM]),
        "attn": dram("attn_d", [TOKENS, DIM]),
    }


STORES = 8


def layer1_projections(nc, a, d, score_scale):
    with ExitStack() as ctx:
        def sb(name, shape, dt=F32):
            return ctx.enter_context(nc.sbuf_tensor(name, shape, dt))

        def sem(name):
            return ctx.enter_context(nc.semaphore(name))

        x = sb("b_x", [P, 2, TPC, DIM])
        ident = sb("b_ident", [P, P])
        ones = sb("b_ones", [P, P])
        w_c = sb("b_wc", [P, KT, 2 * LATENT])
        w_kr = sb("b_wkr", [P, KT, VW + D_R])
        w_q = sb("b_wq", [P, DIM + 2 * HEADS * D_R])
        w_uk = sb("b_wuk", [P, DIM])
        w_uv = sb("b_wuv", [P, DIM])
        w_r, w_k, w_v = (sb(f"b_w{n}", [P, KT, DIM]) for n in "rkv")
        mixes = sb("b_mixes", [P, 2, KT])
        cos = sb("b_cos", [P, SEQ])
        sin = sb("b_sin", [P, SEQ])
        squares = sb("b_squares", [P, DIM + 2 * HEADS * D_R])
        sums = sb("b_sums", [P, 5])
        roots = sb("b_roots", [P, 5])
        bound = sb("b_bound", [P, 2])
        kr_bound = sb("b_kr_bound", [P, 1])
        power = sb("b_power", [P, 2])
        scale = sb("b_scale", [P, 2])
        eps = sb("b_eps", [P, TPC])
        half = sb("b_half", [P, TPC])
        zero_col = sb("b_zero", [P, KT, 1])
        stats = sb("b_stats", [P, TPC, 6])
        mv = sb("b_mv", [P, TPC, 2])
        var_eps = sb("b_var", [P, TPC])
        rstd = sb("b_rstd", [P, TPC])
        xhat = sb("b_xhat", [P, TPC, DIM])
        xn = sb("b_xn", [P, 2, KT, CH + 1])
        diff = sb("b_diff", [P, KT, CH])
        x_r, x_k = (sb(f"b_x{n}", [P, KT, CH]) for n in "rk")
        lat = sb("b_lat", [P, CH])
        q_cos = sb("b_qcos", [P, CH])
        q_sin = sb("b_qsin", [P, CH])
        k_cos = sb("b_kcos", [D_R, CH])
        k_sin = sb("b_ksin", [D_R, CH])
        qc = sb("b_qc", [P, 2, 2, KT, CH], F16)
        kc = sb("b_kc", [P, 2, 2, KT, CH], F16)
        qr = sb("b_qr", [P, 2, 2, CH], F16)
        kr = sb("b_kr", [D_R, 2, 2, CH], F16)
        val = sb("b_val", [P, 2, TPC, HEADS, VW])
        relu = sb("b_relu", [P, KT, CH])
        act_k = sb("b_actk", [P, KT, CH])
        sig_r = sb("b_sigr", [P, TPC, DIM])
        gate_in = sb("b_gi", [P, TPC, DIM])
        gate_sig = sb("b_gs", [P, TPC, DIM])
        gate = sb("b_gate", [P, 2, TPC, DIM])

        ps_a = ctx.enter_context(nc.psum_tensor("b_ps0", [P, 2, CH], F32))
        ps_b = ctx.enter_context(nc.psum_tensor("b_ps1", [P, 2, CH], F32))
        ps_c = ctx.enter_context(nc.psum_tensor("b_ps2", [P, 2, CH], F32))
        ps_t = ctx.enter_context(nc.psum_tensor("b_ps3", [P, 2, CH], F32))
        ps_val = ps_a[:].rearrange("p a (j d) -> p (a j) d", d=DIM)
        ps_r = ps_b[:].rearrange("p a (j d) -> p (a j) d", d=DIM)
        ps_kv = ps_c[:].rearrange("p a (j d) -> p (a j) d", d=DIM)

        weights_loaded = sem("b_weights_loaded")
        consts_loaded = sem("b_consts_loaded")
        x_loaded = [sem(f"b_x_loaded{i}") for i in range(2)]
        stored = [sem(f"b_stored{i}") for i in range(2)]
        consts_set = sem("b_consts_set")
        squares_done = sem("b_squares_done")
        sums_done = sem("b_sums_done")
        roots_done = sem("b_roots_done")
        bound_done = sem("b_bound_done")
        scale_done = sem("b_scale_done")
        stats_done = sem("b_stats_done")
        mv_done = sem("b_mv_done")
        var_done = sem("b_var_done")
        rstd_done = sem("b_rstd_done")
        xhat_done = sem("b_xhat_done")
        xt_done = sem("b_xt_done")
        xn_done = sem("b_xn_done")
        diff_done = sem("b_diff_done")
        mix_done = sem("b_mix_done")
        lat_mm = sem("b_lat_mm")
        lat_done = sem("b_lat_done")
        kr_mm = sem("b_kr_mm")
        k_mm = sem("b_k_mm")
        qc_mm = sem("b_qc_mm")
        qr_mm = sem("b_qr_mm")
        kc_mm = sem("b_kc_mm")
        r_mm = sem("b_r_mm")
        val_mm = sem("b_val_mm")
        kv_mm = sem("b_kv_mm")
        relu_done = sem("b_relu_done")
        act_done = sem("b_act_done")
        qc_high = sem("b_qc_high")
        qc_low = sem("b_qc_low")
        kc_high = sem("b_kc_high")
        kc_low = sem("b_kc_low")
        kr_parts = sem("b_kr_parts")
        kr_sum = sem("b_kr_sum")
        kr_high = sem("b_kr_high")
        kr_low = sem("b_kr_low")
        qr_parts = sem("b_qr_parts")
        qr_sum = sem("b_qr_sum")
        qr_high = sem("b_qr_high")
        qr_low = sem("b_qr_low")
        sig_done = sem("b_sig_done")
        val_done = sem("b_val_done")
        gate_in_done = sem("b_gate_in_done")
        gate_sig_done = sem("b_gate_sig_done")
        gate_done = sem("b_gate_done")

        x_v3 = d["x1"].rearrange("(n j p) c -> n p j c", j=TPC, p=P)
        gate_v3 = d["gate"].rearrange("(n j p) c -> n p j c", j=TPC, p=P)
        val_v3 = d["v"].rearrange("(n j p) c -> n p j c", j=TPC, p=P)
        WEIGHTS = 8

        def chunks(eng, body):
            with eng.Fori(0, BATCH - 1) as b:
                for c in range(CPB):
                    body(b, c, False)
            for c in range(CPB):
                body(BATCH - 1, c, c == CPB - 1)

        def count(b, c):
            return b * CPB + c

        def turns(b, c):
            return b * (CPB // 2) + c // 2

        with nc.Block() as block:
            @block.sync
            def _(sp):
                for s in range(2):
                    sp.sem_inc(stored[s], 16)
                sp.dma_start(x[:, 0], x_v3[0]).then_inc(x_loaded[0], 16)
                sp.dma_start(x[:, 1], x_v3[1]).then_inc(x_loaded[1], 16)
                sp.dma_start(ident[:], a["ident"]).then_inc(consts_loaded, 16)
                sp.dma_start(mixes[:], a["mixes1"].rearrange("p (m k) -> p m k", m=2)).then_inc(consts_loaded, 16)
                sp.dma_start(cos[:], a["cos"]).then_inc(consts_loaded, 16)
                sp.dma_start(sin[:], a["sin"]).then_inc(consts_loaded, 16)

                def store(b, c):
                    n, s, t = count(b, c), c % 2, slice(c * CH, (c + 1) * CH)
                    sp.wait_ge(kr_low, n + 1)
                    sp.dma_start(d["kr"][b, :, :, t].rearrange("h p t -> p h t"), kr[:, s]).then_inc(stored[s], 16)
                    sp.wait_ge(qc_low, KT * n + KT)
                    for h in range(2):
                        sp.dma_start(d["qc"][b, h, :, t].rearrange("(m p) t -> p m t", p=P), qc[:, s, h]).then_inc(stored[s], 16)
                    sp.wait_ge(kc_low, KT * n + KT)
                    for h in range(2):
                        sp.dma_start(d["kc"][b, h, :, t].rearrange("(m p) t -> p m t", p=P), kc[:, s, h]).then_inc(stored[s], 16)
                    sp.wait_ge(qr_low, n + 1)
                    sp.dma_start(d["qr"][b, :, :, t].rearrange("h p t -> p h t"), qr[:, s]).then_inc(stored[s], 16)
                    sp.wait_ge(val_done, n + 1 + 1)
                    sp.dma_start(val_v3[n], val[:, s].rearrange("p j h e -> p j (h e)")).then_inc(stored[s], 16)
                    sp.wait_ge(gate_done, n + 1 + 1)
                    sp.dma_start(gate_v3[n], gate[:, s]).then_inc(stored[s], 16)

                def load_ahead(b, c):
                    sp.wait_ge(xhat_done, TPC * count(b, c) + TPC)
                    sp.dma_start(x[:, c % 2], x_v3[count(b, c) + 2]).then_inc(x_loaded[c % 2], 16)

                with sp.Fori(0, BATCH - 1) as b:
                    for c in range(CPB):
                        load_ahead(b, c)
                        store(b, c)
                for c in range(CPB):
                    if c + 2 < CPB:
                        load_ahead(BATCH - 1, c)
                    store(BATCH - 1, c)
                for s in range(2):
                    sp.wait_ge(stored[s], 16 * STORES * NCH // 2 + 16)

            @block.gpsimd
            def _(pool):
                for count_from_one in (gate_done,):
                    pool.sem_inc(count_from_one, 1)
                pool.memset(half[:], -0.5).then_inc(consts_set, 1)
                pool.memset(zero_col[:], 0.0).then_inc(consts_set, 1)
                pool.memset(ones[:], 1.0).then_inc(consts_set, 1)
                pool.memset(eps[:], LN_EPS).then_inc(consts_set, 1)
                pool.memset(val[:], 0.0).then_inc(consts_set, 1)
                pool.wait_ge(consts_set, 5)
                for s in range(2):
                    pool.memset(val[:, s, :, :, D_H:D_H + 1], 1.0).then_inc(consts_set, 1)

                def rstd_of(n):
                    pool.wait_ge(mv_done, TPC * n + TPC)
                    nc.gpsimd.tensor_tensor(var_eps[:], mv[:, :, 1], eps[:], ALU.add).then_inc(var_done, 1)
                    pool.wait_ge(var_done, n + 1)
                    nc.gpsimd.tensor_tensor(rstd[:], var_eps[:], half[:], ALU.pow).then_inc(rstd_done, 1)

                def diff_of(n, c):
                    pool.wait_ge(xn_done, 2 * n + 2)
                    nc.gpsimd.tensor_tensor(diff[:], xn[:, c % 2, :, 1:CH + 1], xn[:, c % 2, :, 0:CH],
                                            ALU.subtract).then_inc(diff_done, 1)

                rstd_of(0)
                diff_of(0, 0)

                def body(b, c, last):
                    n = count(b, c)
                    if not last:
                        rstd_of(n + 1)
                        diff_of(n + 1, (c + 1) % 2)
                    pool.wait_ge(gate_sig_done, n + 1)
                    pool.wait_ge(stored[c % 2], 16 * STORES * turns(b, c) + 16)
                    nc.gpsimd.tensor_tensor(gate[:, c % 2], gate_in[:], gate_sig[:], ALU.mult).then_inc(gate_done, 1)

                chunks(pool, body)

            @block.scalar
            def _(act):
                for count_from_one in (val_done, sig_done,):
                    act.sem_inc(count_from_one, 1)
                for t, name in ((w_c, "Wc"), (w_kr, "Wkr"), (w_r, "W1rT"), (w_k, "W1kT"), (w_v, "W1vT")):
                    act.dma_start(t[:], a[name].rearrange("(k p) n -> p k n", p=P)).then_inc(weights_loaded, 16)
                for t, name in ((w_q, "Wq"), (w_uk, "Wuk"), (w_uv, "Wuv")):
                    act.dma_start(t[:], a[name]).then_inc(weights_loaded, 16)
                act.wait_ge(sums_done, 1)
                nc.scalar.activation(roots[:], ps_a[:, 0, 0:5], ACT.Sqrt).then_inc(roots_done, 1)

                def xn_of(n, c):
                    s = c % 2
                    if c == 0:
                        act.wait_ge(consts_set, 2)
                        before = zero_col[:]
                    else:
                        act.wait_ge(xn_done, 2 * n)
                        before = xn[:, 1 - s, :, CH:CH + 1]
                    act.wait_ge(xt_done, n + 1)
                    nc.scalar.activation(xn[:, s, :, 0:1], before, ACT.Copy).then_inc(xn_done, 1)
                    nc.scalar.activation(xn[:, s, :, 1:CH + 1], ps_t[:], ACT.Copy).then_inc(xn_done, 1)

                xn_of(0, 0)
                act.wait_ge(scale_done, 1)

                def body(b, c, last):
                    n, s = count(b, c), c % 2
                    act.wait_ge(lat_mm, n + 1)
                    nc.scalar.activation(lat[:], ps_a[:, 0, :], ACT.Copy).then_inc(lat_done, 1)
                    act.wait_ge(stored[s], 16 * STORES * turns(b, c) + 16)
                    act.wait_ge(kr_sum, n + 1)
                    nc.scalar.activation(kr[:, s, 0, :], k_cos[:], ACT.Copy).then_inc(kr_high, 1)
                    act.wait_ge(k_mm, n + 1)
                    nc.scalar.activation(relu[:], ps_b[:], ACT.Relu).then_inc(relu_done, 1)
                    for m in range(KT):
                        act.wait_ge(qc_mm, KT * n + m + 1)
                        nc.scalar.activation(qc[:, s, 0, m, :], ps_c[:, m, :], ACT.Copy, scale=scale[:, 0:1]).then_inc(qc_high, 1)
                    for m in range(KT):
                        act.wait_ge(kc_mm, KT * n + m + 1)
                        nc.scalar.activation(kc[:, s, 0, m, :], ps_c[:, m, :], ACT.Copy, scale=scale[:, 1:2]).then_inc(kc_high, 1)
                    act.wait_ge(qr_sum, n + 1)
                    nc.scalar.activation(qr[:, s, 0, :], q_cos[:], ACT.Copy).then_inc(qr_high, 1)
                    if not last:
                        xn_of(n + 1, (c + 1) % CPB)
                    act.wait_ge(r_mm, n + 1)
                    nc.scalar.activation(sig_r[:], ps_r, ACT.Sigmoid).then_inc(sig_done, 1)
                    act.wait_ge(val_mm, n + 1)
                    act.wait_ge(consts_set, 7)
                    for j in range(TPC):
                        ins = nc.scalar.activation(val[:, s, j, :, 0:D_H], ps_val[:, j, :].rearrange("p (h e) -> p h e", e=D_H), ACT.Copy)
                    ins.then_inc(val_done, 1)
                    act.wait_ge(gate_in_done, n + 1 + 1)
                    nc.scalar.activation(gate_sig[:], gate_in[:], ACT.Sigmoid).then_inc(gate_sig_done, 1)

                chunks(act, body)

            @block.vector
            def _(dve):
                for count_from_one in (gate_in_done,):
                    dve.sem_inc(count_from_one, 1)
                dve.wait_ge(weights_loaded, 16 * WEIGHTS)
                flat = (w_c[:, :, 0:LATENT], w_c[:, :, LATENT:], w_q[:], w_uk[:], w_kr[:])
                for i, w in enumerate(flat):
                    size = w.free_size()
                    if i:
                        dve.wait_ge(squares_done, i)
                    sq = squares[:, 0:size]
                    if len(w.shape) == 3:
                        sq = sq.rearrange("p (k n) -> p k n", k=w.shape[1])
                    nc.vector.tensor_tensor_reduce(out=sq, in0=w, in1=w, scale=1.0, scalar=0.0, op0=ALU.mult, op1=ALU.add,
                                                   accum_out=sums[:, i:i + 1]).then_inc(squares_done, 1)
                dve.wait_ge(roots_done, 1)
                nc.vector.tensor_tensor(bound[:, 0:1], roots[:, 0:1], roots[:, 2:3], ALU.mult).then_inc(bound_done, 1)
                nc.vector.tensor_tensor(bound[:, 1:2], roots[:, 1:2], roots[:, 3:4], ALU.mult).then_inc(bound_done, 1)
                dve.wait_ge(bound_done, 2)
                nc.vector.tensor_tensor(bound[:, 1:2], bound[:, 1:2], roots[:, 4:5], ALU.max).then_inc(bound_done, 1)
                dve.wait_ge(bound_done, 3)
                nc.vector.tensor_scalar(bound[:], bound[:], 2.0 * float(np.sqrt(DIM)), 1e-20, ALU.mult, ALU.max).then_inc(bound_done, 1)
                dve.wait_ge(bound_done, 4)
                nc.vector.tensor_scalar(power[:].bitcast(I32), bound[:].bitcast(I32), 0x7F800000, None,
                                        ALU.bitwise_and).then_inc(bound_done, 1)
                dve.wait_ge(bound_done, 5)
                nc.vector.reciprocal(scale[:], power[:]).then_inc(bound_done, 1)
                nc.vector.tensor_tensor(score_scale[:], power[:, 0:1], power[:, 1:2], ALU.mult).then_inc(bound_done, 1)
                dve.wait_ge(bound_done, 7)
                nc.vector.tensor_scalar(score_scale[:], score_scale[:], INV_SQRT / F16_TARGET ** 2, None, ALU.mult)
                nc.vector.tensor_scalar(scale[:], scale[:], F16_TARGET, None, ALU.mult).then_inc(scale_done, 1)
                dve.wait_ge(scale_done, 1)

                def layernorm(n, c, turn):
                    s = c % 2
                    dve.wait_ge(x_loaded[s], 16 * (turn + 1))
                    for j in range(TPC):
                        nc.vector.bn_stats(stats[:, j, :], x[:, s, j, :]).then_inc(stats_done, 1)

                def aggregate():
                    for j in range(TPC):
                        nc.vector.bn_aggr(mv[:, j, :], stats[:, j, :]).then_inc(mv_done, 1)

                def normalise(n, c):
                    dve.wait_ge(rstd_done, n + 1)
                    dve.wait_ge(xt_done, n)
                    for j in range(TPC):
                        nc.vector.tensor_scalar(xhat[:, j, :], x[:, c % 2, j, :], mv[:, j, 0:1], rstd[:, j:j + 1],
                                                ALU.subtract, ALU.mult).then_inc(xhat_done, 1)

                def mix(n, c):
                    dve.wait_ge(diff_done, n + 1)
                    dve.wait_ge(r_mm, n)
                    for i, t in ((1, x_k), (0, x_r)):
                        for k in range(KT):
                            nc.vector.scalar_tensor_tensor(t[:, k, :], diff[:, k, :], mixes[:, i, k:k + 1],
                                                           xn[:, c % 2, k, 0:CH], ALU.mult, ALU.add).then_inc(mix_done, 1)

                layernorm(0, 0, 0)
                dve.wait_ge(stats_done, TPC)
                aggregate()
                normalise(0, 0)
                dve.wait_ge(consts_loaded, 16 * 4)
                mix(0, 0)

                def body(b, c, last):
                    n, s, t = count(b, c), c % 2, slice(c * CH, (c + 1) * CH)
                    dve.wait_ge(kr_mm, n + 1)
                    dve.wait_ge(stored[s], 16 * STORES * turns(b, c) + 16)
                    nc.vector.scalar_tensor_tensor(k_cos[:], ps_a[0:D_R, 1, :], scale[0:D_R, 1:2], cos[0:D_R, t],
                                                   ALU.mult, ALU.mult).then_inc(kr_parts, 1)
                    nc.vector.scalar_tensor_tensor(k_sin[:], ps_a[VW:VW + D_R, 1, :], scale[VW:VW + D_R, 1:2], sin[VW:VW + D_R, t],
                                                   ALU.mult, ALU.mult).then_inc(kr_parts, 1)
                    dve.wait_ge(kr_parts, 2 * n + 2)
                    nc.vector.tensor_tensor(k_cos[:], k_cos[:], k_sin[:], ALU.add).then_inc(kr_sum, 1)
                    if not last:
                        layernorm(n + 1, (c + 1) % CPB, turns(b, c + 1))
                        dve.wait_ge(stats_done, TPC * (n + 1) + TPC)
                    dve.wait_ge(kr_high, n + 1)
                    nc.vector.tensor_tensor(kr[:, s, 1, :], k_cos[:], kr[:, s, 0, :], ALU.subtract).then_inc(kr_low, 1)
                    if not last:
                        aggregate()
                    dve.wait_ge(relu_done, n + 1)
                    dve.wait_ge(kv_mm, n + 1)
                    nc.vector.tensor_tensor(act_k[:], relu[:], relu[:], ALU.mult).then_inc(act_done, 1)
                    for m in range(KT):
                        dve.wait_ge(qc_high, KT * n + m + 1)
                        nc.vector.scalar_tensor_tensor(qc[:, s, 1, m, :], ps_c[:, m, :], scale[:, 0:1], qc[:, s, 0, m, :],
                                                       ALU.mult, ALU.subtract).then_inc(qc_low, 1)
                    dve.wait_ge(qr_mm, 2 * n + 1)
                    nc.vector.scalar_tensor_tensor(q_cos[:], ps_a[:, 0, :], scale[:, 0:1], cos[:, t], ALU.mult, ALU.mult).then_inc(qr_parts, 1)
                    dve.wait_ge(qr_mm, 2 * n + 2)
                    nc.vector.scalar_tensor_tensor(q_sin[:], ps_a[:, 1, :], scale[:, 0:1], sin[:, t], ALU.mult, ALU.mult).then_inc(qr_parts, 1)
                    dve.wait_ge(qr_parts, 2 * n + 2)
                    nc.vector.tensor_tensor(q_cos[:], q_cos[:], q_sin[:], ALU.add).then_inc(qr_sum, 1)
                    for m in range(KT):
                        dve.wait_ge(kc_high, KT * n + m + 1)
                        nc.vector.scalar_tensor_tensor(kc[:, s, 1, m, :], ps_c[:, m, :], scale[:, 1:2], kc[:, s, 0, m, :],
                                                       ALU.mult, ALU.subtract).then_inc(kc_low, 1)
                    dve.wait_ge(qr_high, n + 1)
                    nc.vector.tensor_tensor(qr[:, s, 1, :], q_cos[:], qr[:, s, 0, :], ALU.subtract).then_inc(qr_low, 1)
                    if not last:
                        normalise(n + 1, (c + 1) % 2)
                        mix(n + 1, (c + 1) % 2)
                    dve.wait_ge(kv_mm, n + 1 + 1)
                    dve.wait_ge(sig_done, n + 1 + 1)
                    dve.wait_ge(gate_done, n + 1)
                    nc.vector.tensor_tensor(gate_in[:], ps_kv, sig_r[:], ALU.mult).then_inc(gate_in_done, 1)

                chunks(dve, body)

            @block.tensor
            def _(pe):
                for count_from_one in (kv_mm,):
                    pe.sem_inc(count_from_one, 1)
                pe.wait_ge(consts_set, 3)
                pe.wait_ge(squares_done, 5)
                nc.tensor.matmul(ps_a[:, 0, 0:5], ones[:], sums[:], start=True, stop=True).then_inc(sums_done, 1)

                def transposes(n):
                    pe.wait_ge(xhat_done, TPC * n + TPC)
                    pe.wait_ge(xn_done, 2 * n)
                    for k in range(KT):
                        for j in range(TPC):
                            last = nc.tensor.transpose(ps_t[:, k, j * P:(j + 1) * P], xhat[:, j, k * P:(k + 1) * P], ident[:])
                    last.then_inc(xt_done, 1)

                def project(ps, w, t):
                    for k in range(KT):
                        last = nc.tensor.matmul(ps, w(k), t(k), start=(k == 0), stop=(k == KT - 1))
                    return last

                pe.wait_ge(consts_loaded, 16 * 4)
                transposes(0)
                pe.wait_ge(roots_done, 1)

                def body(b, c, last):
                    n, s = count(b, c), c % 2
                    xs = lambda k: xn[:, s, k, 1:CH + 1]
                    pe.wait_ge(xn_done, 2 * n + 2)
                    pe.wait_ge(val_done, n + 1)
                    project(ps_a[:, 0, :], lambda k: w_c[:, k, :], xs).then_inc(lat_mm, 1)
                    project(ps_a[0:VW + D_R, 1, :], lambda k: w_kr[:, k, :], xs).then_inc(kr_mm, 1)
                    pe.wait_ge(mix_done, 2 * KT * n + KT)
                    pe.wait_ge(sig_done, n + 1)
                    for m in range(KT):
                        mm = project(ps_b[:, m, :], lambda k: w_k[:, k, m * P:(m + 1) * P], lambda k: x_k[:, k, :])
                    mm.then_inc(k_mm, 1)
                    pe.wait_ge(lat_done, n + 1)
                    pe.wait_ge(gate_in_done, n + 1)
                    for m in range(KT):
                        nc.tensor.matmul(ps_c[:, m, :], w_q[:, m * P:(m + 1) * P], lat[:], start=True, stop=True).then_inc(qc_mm, 1)
                    pe.wait_ge(kr_parts, 2 * n + 2)
                    for m in range(2):
                        nc.tensor.matmul(ps_a[:, m, :], w_q[:, DIM + m * P:DIM + (m + 1) * P], lat[:], start=True, stop=True).then_inc(qr_mm, 1)
                    pe.wait_ge(relu_done, n + 1)
                    pe.wait_ge(mix_done, 2 * KT * n + 2 * KT)
                    for j in range(TPC):
                        mm = project(ps_r[:, j, :], lambda k: x_r[:, k, j * P:(j + 1) * P], lambda k: w_r[:, k, :])
                    mm.then_inc(r_mm, 1)
                    for m in range(KT):
                        pe.wait_ge(qc_low, KT * n + m + 1)
                        nc.tensor.matmul(ps_c[:, m, :], w_uk[:, m * P:(m + 1) * P], lat[:], start=True, stop=True).then_inc(kc_mm, 1)
                    pe.wait_ge(qr_parts, 2 * n + 2)
                    for j in range(TPC):
                        mm = nc.tensor.matmul(ps_val[:, j, :], lat[:, j * P:(j + 1) * P], w_uv[:], start=True, stop=True)
                    mm.then_inc(val_mm, 1)
                    if not last:
                        transposes(n + 1)
                    pe.wait_ge(kc_low, KT * n + KT)
                    pe.wait_ge(act_done, n + 1)
                    for j in range(TPC):
                        mm = project(ps_kv[:, j, :], lambda k: act_k[:, k, j * P:(j + 1) * P], lambda k: w_v[:, k, :])
                    mm.then_inc(kv_mm, 1)

                chunks(pe, body)



def attention(nc, d, score_scale):
    tiles = [[kt for j in range(TPC) for kt in [TPC * c + j] + [c * j + f for f in range(c)]] for c in range(CPB)]
    steps = [(s, c, kt) for s in range(2) for c in range(CPB) for kt in tiles[c]]
    N = len(steps)
    starts = [i for i, (s, c, kt) in enumerate(steps) if kt == tiles[c][0]]
    ends = [i for i, (s, c, kt) in enumerate(steps) if kt == tiles[c][-1]]
    AHEAD = 3
    LEAD = 3
    NC = len(ends)
    PAIRS = BATCH * GROUPS // 2
    HALF = GH // 2
    NBUF, NPROB = 3, 4
    LOADS = 17
    bufs = [h % NBUF for h in range(2 * N)]
    if bufs[-1] == 0:
        bufs[-2], bufs[-1] = bufs[-1], bufs[-2]
    before = []
    for h in range(2 * N):
        back = [g for g in range(h - 2 * N, h) if bufs[g] == bufs[h]]
        before.append(back[-1])
    diags = [i for i, (s, c, kt) in enumerate(steps) if kt >= TPC * c]

    def offset(i):
        _, c, kt = steps[i]
        return max(0, kt - TPC * c) * P

    with ExitStack() as ctx:
        def sb(name, shape, dt=F32):
            return ctx.enter_context(nc.sbuf_tensor(name, shape, dt))

        def sem(name):
            return ctx.enter_context(nc.semaphore(name))

        q = sb("c_q", [KROWS, 2, GH, SEQ], F16)
        k = sb("c_k", [KROWS, 2, GH, SEQ], F16)
        v = sb("c_v", [P, 2, KEYT, GH * VW])
        ident = sb("c_ident", [P, P])
        probs = sb("c_probs", [P, NPROB, GH, CH])
        causal = sb("c_causal", [P, HALF, P])
        o_t = sb("c_ot", [P, 2, CH])
        recip = sb("c_recip", [P, 2, TPC, GH])
        attn = sb("c_attn", [P, 2, TPC, GH, D_H])
        ps_s = ctx.enter_context(nc.psum_tensor("c_ps_s", [P, NBUF, HALF, CH], F32))
        ps_o = ctx.enter_context(nc.psum_tensor("c_ps_o", [P, 2, CH], F32))
        ps_tok = ps_o[:].rearrange("p a (j h e) -> p a j h e", j=TPC, h=GH)

        ident_loaded = sem("c_ident_loaded")
        causal_set = sem("c_causal_set")
        loaded = [sem(f"c_loaded{i}") for i in range(2)]
        stored = [sem(f"c_stored{i}") for i in range(2)]
        qk_done = sem("c_qk_done")
        exp_done = sem("c_exp_done")
        clip_done = sem("c_clip_done")
        mask_done = sem("c_mask_done")
        pv_done = sem("c_pv_done")
        ot_done = sem("c_ot_done")
        tok_done = sem("c_tok_done")
        recip_done = sem("c_recip_done")
        norm_done = sem("c_norm_done")

        def pairs(eng, body):
            with eng.Fori(0, PAIRS - 1) as i:
                body(i, False)
            body(PAIRS - 1, True)

        attn_v = d["attn"].rearrange("(b c j p) (g e) -> b c g p j e", c=CPB, j=TPC, p=P, g=GROUPS)

        with nc.Block() as block:
            @block.sync
            def _(sp):
                for s in range(2):
                    sp.sem_inc(stored[s], 16)
                sp.dma_start(ident[:], d["ident"]).then_inc(ident_loaded, 16)

                def load(i, s):
                    b, g = (i * 2 + s) // GROUPS, (i * 2 + s) % GROUPS
                    at = 0
                    for hq, hk in ((0, 0), (0, 1), (1, 0), (1, 1)):
                        for t, name, half in ((q, "q", hq), (k, "k", hk)):
                            src = d[name + "c"][b, half].rearrange("(g h r) t -> g r h t", g=GROUPS, h=GH)[g]
                            sp.dma_start(t[at:at + D_H, s], src).then_inc(loaded[s], 16)
                            if name == "q":
                                src = d["qr"][b, half].rearrange("(g h r) t -> g r h t", g=GROUPS, h=GH)[g]
                            else:
                                src = d["kr"][b, half].rearrange("r (o t) -> r o t", o=1).to_broadcast([D_R, GH, SEQ])
                            sp.dma_start(t[at + D_H:at + D_QK, s], src).then_inc(loaded[s], 16)
                        at += D_QK
                    src = d["v"].rearrange("(b m p) (g e) -> b g p m e", b=BATCH, p=P, g=GROUPS)[b, g]
                    sp.dma_start(v[:, s], src).then_inc(loaded[s], 16)

                load(0, 0)
                load(0, 1)

                def body(i, last):
                    for s in range(2):
                        b, g = (i * 2 + s) // GROUPS, (i * 2 + s) % GROUPS
                        for c in range(CPB):
                            e = s * CPB + c
                            sp.wait_ge(norm_done, NC * i + e + 1 + 2)
                            sp.dma_start(attn_v[b, c, g], attn[:, c % 2].rearrange("p j h e -> p j (h e)")).then_inc(stored[c % 2], 16)
                        if not last:
                            sp.wait_ge(pv_done, N * i + (s + 1) * N // 2 + NPROB)
                            load(i + 1, s)

                pairs(sp, body)
                for s in range(2):
                    sp.wait_ge(stored[s], 16 * BATCH * GROUPS * CPB // 2 + 16)

            @block.scalar
            def _(act):
                act.sem_inc(exp_done, NBUF)
                unscale = act.alloc_register("c_unscale")
                act.load(unscale, score_scale[0:1, 0:1].bitcast(I32))

                def body(i, last):
                    for st in range(N):
                        o = offset(st)
                        for h in range(2):
                            hs = 2 * st + h
                            if h == 0:
                                act.wait_ge(pv_done, N * i + st + 1)
                            act.wait_ge(qk_done, 2 * N * i + hs + 1)
                            nc.scalar.activation(probs[:, st % NPROB, h * HALF:(h + 1) * HALF, o:CH], ps_s[:, bufs[hs], :, o:CH],
                                                 ACT.Exp, scale=unscale).then_inc(exp_done, 1)

                pairs(act, body)

            @block.vector
            def _(dve):
                dve.sem_inc(norm_done, 2)

                def rows_out(i, e):
                    dve.wait_ge(pv_done, N * i + ends[e] + 1 + NPROB)
                    nc.vector.tensor_copy(o_t[:, e % 2, :], ps_o[:, e % 2, :]).then_inc(ot_done, 1)

                def normalise(i, e):
                    a = e % 2
                    dve.wait_ge(tok_done, NC * i + e + 1)
                    nc.vector.reciprocal(recip[:, a], ps_tok[:, a, :, :, D_H]).then_inc(recip_done, 1)
                    dve.wait_ge(stored[a], 16 * (NC // 2 * i + e // 2) + 16)
                    dve.wait_ge(recip_done, NC * i + e + 1)
                    nc.vector.tensor_tensor(attn[:, a], ps_tok[:, a, :, :, 0:D_H],
                                            recip[:, a].rearrange("p j (h o) -> p j h o", o=1).to_broadcast([P, TPC, GH, D_H]),
                                            ALU.mult).then_inc(norm_done, 1)

                def clip(i, st):
                    o = offset(st)
                    for h in range(2):
                        hs = 2 * st + h
                        dve.wait_ge(exp_done, 2 * N * i + hs + 1 + NBUF)
                        tile = probs[:, st % NPROB, h * HALF:(h + 1) * HALF, o:CH]
                        nc.vector.tensor_scalar(tile, tile, P_MAX, P_MIN, ALU.min, ALU.max).then_inc(clip_done, 1)

                for st in range(AHEAD):
                    clip(0, st)
                for st in range(LEAD):
                    clip(0, st + AHEAD)

                def body(i, last):
                    todo = {}
                    for e, st in enumerate(ends):
                        todo.setdefault(st, []).append((rows_out, e))
                        todo.setdefault(st + 3, []).append((normalise, e))
                    for st in range(LEAD, N + LEAD):
                        if st + AHEAD < N:
                            clip(i, st + AHEAD)
                        elif not last:
                            clip(i + 1, st + AHEAD - N)
                        for task, e in todo.get(st, []):
                            task(i, e)

                pairs(dve, body)

            @block.gpsimd
            def _(pool):
                pool.memset(causal[:], 1.0).then_inc(causal_set, 1)
                pool.wait_ge(causal_set, 1)
                pool.affine_select(out=causal[:], in_=causal[:], compare_op=ALU.is_ge, fill=0.0, base=0,
                                   pattern=[[0, HALF], [1, P]], channel_multiplier=-1).then_inc(causal_set, 1)
                pool.wait_ge(causal_set, 2)

                def body(i, last):
                    for st in diags:
                        o = offset(st)
                        for h in range(2):
                            pool.wait_ge(clip_done, 2 * N * i + 2 * st + h + 1)
                            tile = probs[:, st % NPROB, h * HALF:(h + 1) * HALF, o:o + P]
                            nc.gpsimd.tensor_tensor(tile, tile, causal[:], ALU.mult).then_inc(mask_done, 1)

                pairs(pool, body)

            @block.tensor
            def _(pe):
                pe.sem_inc(pv_done, NPROB)
                pe.wait_ge(ident_loaded, 16)

                def scores(i, st):
                    s, c, kt = steps[st]
                    o = offset(st)
                    if st in starts and c == 0:
                        pe.wait_ge(loaded[s], 16 * LOADS * (i + 1))
                    for h in range(2):
                        hs = 2 * st + h
                        pe.wait_ge(exp_done, 2 * N * i + before[hs] + 1 + NBUF)
                        for j in range(HALF):
                            mm = nc.tensor.matmul(ps_s[:, bufs[hs], j, o:CH], k[:, s, h * HALF + j, kt * P:(kt + 1) * P],
                                                  q[:, s, h * HALF + j, c * CH + o:(c + 1) * CH], start=True, stop=True)
                        mm.then_inc(qk_done, 1)

                def values(i, st):
                    s, c, kt = steps[st]
                    o = offset(st)
                    e = s * CPB + c
                    if st in starts:
                        pe.wait_ge(norm_done, NC * i + e - 2 + 1 + 2)
                    if st in diags:
                        pe.wait_ge(mask_done, 2 * len(diags) * i + 2 * diags.index(st) + 2)
                    else:
                        pe.wait_ge(clip_done, 2 * N * i + 2 * st + 2)
                    for j in range(GH):
                        mm = nc.tensor.matmul(ps_o[j * VW:(j + 1) * VW, c % 2, o:CH], v[:, s, kt, j * VW:(j + 1) * VW],
                                              probs[:, st % NPROB, j, o:CH], start=(st in starts), stop=(st in ends),
                                              tile_position=(0, j * VW))
                    mm.then_inc(pv_done, 1)

                def tokens(i, e):
                    pe.wait_ge(ot_done, NC * i + e + 1)
                    for j in range(TPC):
                        mm = nc.tensor.transpose(ps_o[:, e % 2, j * P:(j + 1) * P], o_t[:, e % 2, j * P:(j + 1) * P], ident[:])
                    mm.then_inc(tok_done, 1)

                for st in range(AHEAD):
                    scores(0, st)
                for st in range(LEAD):
                    scores(0, st + AHEAD)
                    values(0, st)

                def body(i, last):
                    todo = {}
                    for e, st in enumerate(ends):
                        todo.setdefault(st + 2, []).append(e)
                    for st in range(LEAD, N + LEAD):
                        if st + AHEAD < N:
                            scores(i, st + AHEAD)
                        elif not last:
                            scores(i + 1, st + AHEAD - N)
                        if st < N:
                            values(i, st)
                        elif not last:
                            values(i + 1, st - N)
                        for e in todo.get(st, []):
                            tokens(i, e)

                pairs(pe, body)


def layer1_output(nc, a, d, out):
    with ExitStack() as ctx:
        def sb(name, shape, dt=F32):
            return ctx.enter_context(nc.sbuf_tensor(name, shape, dt))

        def sem(name):
            return ctx.enter_context(nc.semaphore(name))

        ident = sb("d_ident", [P, P])
        SLOTS = 4
        w_o = sb("d_wo", [P, KT, DIM])
        attn = sb("d_attn", [P, SLOTS, TPC, DIM])
        gate = sb("d_gate", [P, SLOTS, TPC, DIM])
        x1 = sb("d_x1", [P, SLOTS, TPC, DIM])
        attn_t = sb("d_attn_t", [P, 2, KT, CH])
        prod = sb("d_prod", [P, SLOTS, TPC, DIM])
        ps_t = ctx.enter_context(nc.psum_tensor("d_ps_t", [P, 2, KT, CH], F32))
        ps_o = ctx.enter_context(nc.psum_tensor("d_ps_o", [P, 2, TPC, DIM], F32))

        weights_loaded = sem("d_weights_loaded")
        attn_loaded = [sem(f"d_attn_loaded{i}") for i in range(SLOTS)]
        rest_loaded = [sem(f"d_rest_loaded{i}") for i in range(SLOTS)]
        stored = [sem(f"d_stored{i}") for i in range(SLOTS)]
        t_mm = sem("d_t_mm")
        t_done = sem("d_t_done")
        out_mm = sem("d_out_mm")
        prod_done = sem("d_prod_done")
        sum_done = sem("d_sum_done")

        def view(t):
            return t.rearrange("(n j p) c -> n p j c", j=TPC, p=P)

        attn_v, gate_v, x1_v, out_v = view(d["attn"]), view(d["gate"]), view(d["x1"]), view(out)

        ROUNDS = NCH // SLOTS

        def rounds(eng, body):
            with eng.Fori(0, ROUNDS - 1) as i:
                body(i, False)
            body(ROUNDS - 1, True)

        with nc.Block() as block:
            @block.sync
            def _(sp):
                for s in range(SLOTS):
                    sp.sem_inc(stored[s], 16)

                def load(n, s):
                    sp.dma_start(attn[:, s], attn_v[n]).then_inc(attn_loaded[s], 16)
                    sp.dma_start(gate[:, s], gate_v[n]).then_inc(rest_loaded[s], 16)
                    sp.dma_start(x1[:, s], x1_v[n]).then_inc(rest_loaded[s], 16)

                sp.dma_start(ident[:], d["ident"]).then_inc(weights_loaded, 16)
                sp.dma_start(w_o[:], a["W_O"].rearrange("(k p) n -> p k n", p=P)).then_inc(weights_loaded, 16)
                for s in range(SLOTS):
                    load(s, s)

                def body(i, last):
                    for s in range(SLOTS):
                        n = SLOTS * i + s
                        sp.wait_ge(sum_done, n + 1)
                        sp.dma_start(out_v[n], prod[:, s]).then_inc(stored[s], 16)
                        if not last:
                            load(n + SLOTS, s)

                rounds(sp, body)
                for s in range(SLOTS):
                    sp.wait_ge(stored[s], 16 * ROUNDS + 16)

            @block.tensor
            def _(pe):
                pe.sem_inc(out_mm, 2)
                pe.wait_ge(weights_loaded, 32)

                def transposes(i, s):
                    pe.wait_ge(attn_loaded[s], 16 * i + 16)
                    for k in range(KT):
                        for j in range(TPC):
                            mm = nc.tensor.transpose(ps_t[:, s % 2, k, j * P:(j + 1) * P], attn[:, s, j, k * P:(k + 1) * P], ident[:])
                    mm.then_inc(t_mm, 1)

                def product(i, s):
                    n = SLOTS * i + s
                    pe.wait_ge(t_done, n + 1)
                    pe.wait_ge(prod_done, n + 1)
                    for j in range(TPC):
                        for k in range(KT):
                            mm = nc.tensor.matmul(ps_o[:, s % 2, j, :], attn_t[:, s % 2, k, j * P:(j + 1) * P], w_o[:, k, :],
                                                  start=(k == 0), stop=(k == KT - 1))
                    mm.then_inc(out_mm, 1)

                transposes(0, 0)

                def body(i, last):
                    for s in range(SLOTS):
                        if s + 1 < SLOTS:
                            transposes(i, s + 1)
                        elif not last:
                            transposes(i + 1, 0)
                        product(i, s)

                rounds(pe, body)

            @block.scalar
            def _(act):
                def body(i, last):
                    for s in range(SLOTS):
                        n = SLOTS * i + s
                        act.wait_ge(t_mm, n + 1)
                        act.wait_ge(out_mm, n + 1)
                        nc.scalar.activation(attn_t[:, s % 2], ps_t[:, s % 2], ACT.Copy).then_inc(t_done, 1)

                rounds(act, body)

            @block.vector
            def _(dve):
                dve.sem_inc(prod_done, 2)

                def body(i, last):
                    for s in range(SLOTS):
                        n = SLOTS * i + s
                        dve.wait_ge(rest_loaded[s], 32 * i + 32)
                        dve.wait_ge(out_mm, n + 1 + 2)
                        dve.wait_ge(stored[s], 16 * i + 16)
                        nc.vector.tensor_tensor(prod[:, s], ps_o[:, s % 2], gate[:, s], ALU.mult).then_inc(prod_done, 1)
                        dve.wait_ge(prod_done, n + 1 + 2)
                        nc.vector.tensor_tensor(prod[:, s], prod[:, s], x1[:, s], ALU.add).then_inc(sum_done, 1)

                rounds(dve, body)


def build(nc, a, out):
    d = scratch(nc)
    d["ident"] = a["ident"]
    layer0(nc, a, d["x1"])
    with nc.sbuf_tensor("score_scale", [P, 1], F32) as score_scale:
        layer1_projections(nc, a, d, score_scale)
        attention(nc, d, score_scale)
    layer1_output(nc, a, d, out)


def rotary_tables():
    inv = np.float32(10000.0) ** (-np.arange(0, D_R, 2, dtype=np.float32) / np.float32(D_R))
    ang = np.arange(SEQ, dtype=np.float32)[None, :] * inv.astype(np.float32)[:, None]
    cos = np.repeat(np.cos(ang), 2, axis=0)
    sin = np.repeat(np.sin(ang), 2, axis=0)
    sin[0::2] *= -1
    return (np.ascontiguousarray(np.tile(t, (HEADS, 1)).astype(np.float32)) for t in (cos, sin))


def layout(inputs):
    i = {k: np.asarray(v) for k, v in inputs.items()}
    cols = lambda v: np.reshape(v, (-1, P)).T
    swap = lambda w: np.reshape(np.reshape(w, (w.shape[0], -1, 2))[:, :, ::-1], w.shape)
    zeros = np.zeros((LATENT, DIM + 2 * HEADS * D_R), np.float32)
    w_qr, w_kr = i["L1_attn_W_QR"], i["L1_attn_W_KR"]
    cos, sin = rotary_tables()
    arrays = {
        "x": np.reshape(i["L0_attn_x"], (TOKENS, DIM)),
        "ident": np.eye(P, dtype=np.float32),
        "WrT": i["L0_attn_Wr"].T, "WkT": i["L0_attn_Wk"].T, "WvT": i["L0_attn_Wv"].T, "WoT": i["L0_attn_Wo"].T,
        "W1": i["L0_ffn_W1"], "W2": i["L0_ffn_W2"], "b1": cols(i["L0_ffn_b1"]), "b2": i["L0_ffn_b2"],
        "time_decay": cols(i["L0_attn_time_decay"]), "time_first": cols(i["L0_attn_time_first"]),
        "mixes": np.concatenate([cols(i["L0_attn_mix_" + n]) for n in "rkv"], axis=1),
        "Wc": np.concatenate([i["L1_attn_W_DQ"], i["L1_attn_W_DKV"]], axis=1),
        "Wkr": np.concatenate([w_kr] * (VW // D_R) + [swap(w_kr)], axis=1),
        "Wq": np.concatenate([np.concatenate([i["L1_attn_W_UQ"], w_qr, swap(w_qr)], axis=1), zeros], axis=0),
        "Wuk": np.concatenate([zeros[:, :DIM], i["L1_attn_W_UK"]], axis=0),
        "Wuv": np.concatenate([zeros[:, :DIM], i["L1_attn_W_UV"]], axis=0),
        "W_O": i["L1_attn_W_O"],
        "W1rT": i["L1_ffn_W_r"].T, "W1kT": i["L1_ffn_W_k"].T, "W1vT": i["L1_ffn_W_v"].T,
        "mixes1": np.concatenate([cols(i["L1_ffn_mu_r"]), cols(i["L1_ffn_mu_k"])], axis=1),
        "cos": cos, "sin": sin,
    }
    return {k: np.ascontiguousarray(v) for k, v in arrays.items()}


def kernel(**inputs):
    import concourse.bacc as bacc
    from concourse.bass_utils import run_bass_kernel_spmd

    nc = bacc.Bacc("TRN2", target_bir_lowering=False, num_devices=1)
    arrays = layout(inputs)
    a = {k: nc.dram_tensor(f"in_{k}", list(v.shape), mybir.dt.from_np(v.dtype), kind="ExternalInput").ap() for k, v in arrays.items()}
    out = nc.dram_tensor("out", [TOKENS, DIM], F32, kind="ExternalOutput").ap()
    build(nc, a, out)
    r = run_bass_kernel_spmd(nc, [{f"in_{k}": v for k, v in arrays.items()}], core_ids=[0])
    return r.results[0]["out"].reshape(BATCH, SEQ, DIM)
```

```python
from contextlib import ExitStack

import numpy as np
import concourse.bass as bass
import concourse.mybir as mybir

F32 = mybir.dt.float32
F16 = mybir.dt.float16
I32 = mybir.dt.int32
ALU = mybir.AluOpType
ACT = mybir.ActivationFunctionType

P = 128
BATCH, SEQ, DIM = 4, 2048, 256
TOKENS = BATCH * SEQ
KT = DIM // P
CH = 512
NCH = TOKENS // CH
CPB = SEQ // CH
TPC = CH // P
TILES = TOKENS // P
INTER = 1024
MT = INTER // P
HEADS, D_H, D_R, LATENT = 16, 16, 8, 64
D_QK = D_H + D_R
GH = 4
GROUPS = HEADS // GH
VW = 32
KROWS = 4 * D_QK
KEYT = SEQ // P
LN_EPS = 1e-5
MAX_INIT = -1e38
EXP_CAP = 30.0
CLIP = 80.0
INV_SQRT = float(1.0 / np.sqrt(np.float32(D_QK)))
P_MAX = float(np.exp(CLIP * INV_SQRT))
P_MIN = float(np.exp(-CLIP * INV_SQRT))
F16_TARGET = 16384.0
X_TARGET = 2048.0


def layer0(nc, a, x1_d, ident, early):
    with ExitStack() as ctx:
        def sb(name, shape, dt=F32):
            return ctx.enter_context(nc.sbuf_tensor(name, shape, dt))

        def sem(name):
            return ctx.enter_context(nc.semaphore(name))

        RING = MT
        X = CPB
        ones = sb("a_ones", [P, P])
        w_r, w_k, w_v, w_o = (sb(f"a_w{n}", [P, 2, KT, DIM], F16) for n in "rkvo")
        w_1 = sb("a_w1", [P, 2, KT, INTER], F16)
        w_2 = sb("a_w2", [P, 2, MT, DIM], F16)
        b_1 = sb("a_b1", [P, MT])
        b_2 = sb("a_b2", [P, DIM])
        mixes = sb("a_mixes", [P, 3, KT])
        decay = sb("a_decay", [P, KT])
        first = sb("a_first", [P, KT])
        cap = sb("a_cap", [P, 1])
        zero_col = sb("a_zero", [P, KT, 1])
        eps = sb("a_eps", [P, TPC])
        half = sb("a_half", [P, TPC])
        WR, WK, WV, XM, VAL, W1, W2, WO, HID = range(9)
        COLUMNS = HID + 1
        sums = sb("a_sums", [P, COLUMNS])
        roots = sb("a_roots", [P, COLUMNS])
        bound = sb("a_bound", [P, COLUMNS])
        power = sb("a_power", [P, COLUMNS])
        scale = sb("a_scale", [P, COLUMNS])
        unscale = sb("a_unscale", [P, COLUMNS])
        neg_k = sb("a_neg_k", [P, 1])
        key_scale = sb("a_key_scale", [P, 1])
        stats = sb("a_stats", [P, TPC, 6])
        mv = sb("a_mv", [P, TPC, 2])
        var_eps = sb("a_var", [P, TPC])
        rstd = sb("a_rstd", [P, TPC])
        x = early.x
        xhat = sb("a_xhat", [P, TPC, DIM])
        xn = sb("a_xn", [P, 2, KT, CH + 1])
        xn_half = sb("a_xnh", [P, 2, 2, KT, CH], F16)
        diff = sb("a_diff", [P, KT, CH])
        mixed = sb("a_mixed", [P, 3, KT, CH])
        mixed_half = sb("a_mixedh", [P, 3, 2, KT, CH], F16)
        sig_r = sb("a_sigr", [P, KT, CH])
        mx = sb("a_mx", [P, KT, CH + 1])
        num = sb("a_num", [P, KT, CH + 1])
        den = sb("a_den", [P, KT, CH + 1])
        dist = sb("a_dist", [P, KT, CH])
        e_bonus = sb("a_eb", [P, KT, CH])
        e_old = sb("a_eo", [P, KT, CH])
        e_new = sb("a_en", [P, KT, CH])
        new_v = sb("a_nv", [P, KT, CH])
        out_num = sb("a_on", [P, KT, CH])
        out_den = sb("a_od", [P, KT, CH])
        rwkv = sb("a_rwkv", [P, KT, CH])
        rwkv_half = sb("a_rwkvh", [P, 2, KT, CH], F16)
        hid = sb("a_hid", [P, RING, CH])
        hid_half = sb("a_hidh", [P, 2, MT, CH], F16)
        gate_parts = sb("a_gp", [P, 2, TPC, DIM])
        gate = sb("a_gate", [P, TPC, DIM])
        x1 = sb("a_x1", [P, 2, TPC, DIM])
        gate_in, gate_sig = gate_parts[:, 0], gate_parts[:, 1]
        x1_slots = x1[:].rearrange("p s j d -> p (s j d)")
        raw_rkv = [x1_slots[:, i * KT * DIM:(i + 1) * KT * DIM].rearrange("p (k d) -> p k d", k=KT) for i in range(3)]
        raw_1 = gate_parts[:].rearrange("p s j d -> p (s j d)").rearrange("p (k n) -> p k n", k=KT)
        raw_2 = hid[:].rearrange("p r c -> p (r c)")[:, MT * DIM:].rearrange("p (m d) -> p m d", m=MT)
        squares = mixed[:].rearrange("p i k c -> p (i k c)")
        act_squares = hid[:].rearrange("p r c -> p (r c)")[:, 0:MT * DIM]
        raw_o = rwkv[:, 0].rearrange("p (k d) -> p k d", k=KT)
        raw = raw_rkv + [raw_1, raw_2, raw_o]
        split = [w_r, w_k, w_v, w_1, w_2, w_o]
        columns = [WR, WK, WV, W1, W2, WO]

        ps_a = ctx.enter_context(nc.psum_tensor("a_ps0", [P, 2, CH], F32))
        ps_b = ctx.enter_context(nc.psum_tensor("a_ps1", [P, 2, CH], F32))
        ps_c = ctx.enter_context(nc.psum_tensor("a_ps2", [P, 2, CH], F32))
        ps_t = ctx.enter_context(nc.psum_tensor("a_ps3", [P, 2, CH], F32))
        ps_ffn = ps_b[:].rearrange("p a (j d) -> p (a j) d", d=DIM)
        ps_out = ps_t[:].rearrange("p a (j d) -> p (a j) d", d=DIM)

        rkv_loaded = sem("a_rkv_loaded")
        ffn_loaded = [sem(f"a_ffn_loaded{i}") for i in range(2)]
        raw_o_loaded = sem("a_raw_o_loaded")
        mixes_loaded = sem("a_mixes_loaded")
        small_loaded = sem("a_small_loaded")
        x_loaded = [sem(f"a_x_loaded{i}") for i in range(X)]
        x1_stored = [sem(f"a_x1_stored{i}") for i in range(2)]
        consts_set = sem("a_consts_set")
        decay_exp = sem("a_decay_exp")
        squares_done = sem("a_squares_done")
        act_squared = sem("a_act_squared")
        sums_done = sem("a_sums_done")
        roots_done = sem("a_roots_done")
        bound_done = sem("a_bound_done")
        scale_done = sem("a_scale_done")
        consts_done = sem("a_consts_done")
        w_high = sem("a_w_high")
        w_low = sem("a_w_low")
        stats_done = sem("a_stats_done")
        mv_done = sem("a_mv_done")
        rstd_done = sem("a_rstd_done")
        xhat_done = sem("a_xhat_done")
        xt_done = sem("a_xt_done")
        xn_done = sem("a_xn_done")
        xn_high = sem("a_xn_high")
        xn_low = sem("a_xn_low")
        diff_done = sem("a_diff_done")
        mix_done = sem("a_mix_done")
        mix_high = sem("a_mix_high")
        mix_low = sem("a_mix_low")
        r_done = sem("a_r_done")
        k_done = sem("a_k_done")
        v_done = sem("a_v_done")
        hid_mm = sem("a_hid_mm")
        hid_done = sem("a_hid_done")
        hid_high = sem("a_hid_high")
        hid_low = sem("a_hid_low")
        ffn_done = sem("a_ffn_done")
        out_done = sem("a_out_done")
        sig_done = sem("a_sig_done")
        state_set = sem("a_state_set")
        mx_done = sem("a_mx_done")
        dist_done = sem("a_dist_done")
        arg_done = sem("a_arg_done")
        exp_done = sem("a_exp_done")
        new_done = sem("a_new_done")
        scan_done = sem("a_scan_done")
        bonus_done = sem("a_bonus_done")
        num_done = sem("a_num_done")
        den_done = sem("a_den_done")
        rden_done = sem("a_rden_done")
        q_done = sem("a_q_done")
        rwkv_done = sem("a_rwkv_done")
        rwkv_high = sem("a_rwkv_high")
        rwkv_low = sem("a_rwkv_low")
        gate_in_done = sem("a_gate_in_done")
        gate_sig_done = sem("a_gate_sig_done")
        gate_done = sem("a_gate_done")
        prod_done = sem("a_prod_done")
        x1_done = sem("a_x1_done")

        x_v3 = a["x"].rearrange("(n j p) c -> n p j c", j=TPC, p=P)
        x1_v3 = x1_d.rearrange("(n j p) c -> n p j c", j=TPC, p=P)

        def chunks(eng, body):
            with eng.Fori(0, BATCH - 1) as b:
                for c in range(CPB):
                    body(b, c, CPB)
            for c in range(CPB):
                body(BATCH - 1, c, CPB - 1 - c)

        def count(b, c):
            return b * CPB + c

        with nc.Block() as block:
            @block.sync
            def _(sp):
                for s in range(2):
                    sp.sem_inc(x1_stored[s], 16)
                sp.dma_start(x[:, 0], x_v3[0]).then_inc(x_loaded[0], 16)
                for i, name in enumerate(("WrT", "WkT", "WvT")):
                    sp.dma_start(raw_rkv[i], a[name].rearrange("(k p) d -> p k d", p=P)).then_inc(rkv_loaded, 16)
                sp.dma_start(ident[:], a["ident"]).then_inc(small_loaded, 16)
                for i in range(2):
                    sp.wait_ge(ffn_loaded[i], 16)
                sp.dma_start(x[:, 1], x_v3[1]).then_inc(x_loaded[1], 16)
                sp.dma_start(raw_o, a["WoT"].rearrange("(k p) d -> p k d", p=P)).then_inc(raw_o_loaded, 16)
                for s in range(2, X):
                    sp.dma_start(x[:, s], x_v3[s]).then_inc(x_loaded[s], 16)

                def body(b, c, left):
                    n = count(b, c)
                    sp.wait_ge(x1_done, n + 1)
                    sp.dma_start(x1_v3[n], x1[:, c % 2]).then_inc(x1_stored[c % 2], 16)
                    if left >= X:
                        sp.dma_start(x[:, c], x_v3[n + X]).then_inc(x_loaded[c], 16)
                    if left == CPB - 1:
                        early.load_weights(sp, a)
                    if left < X and c < X - 1:
                        sp.wait_ge(x1_stored[c % 2], 16 * (c // 2 + 1) + 16)
                        sp.dma_start(x[:, c], x1_v3[c]).then_inc(early.x_loaded[c], 16)

                chunks(sp, body)
                for s in range(2):
                    sp.wait_ge(x1_stored[s], 16 * NCH // 2 + 16)

            @block.gpsimd
            def _(pool):
                for counts_from_one in (num_done, q_done, gate_done):
                    pool.sem_inc(counts_from_one, 1)
                pool.sem_inc(hid_low, RING)
                pool.memset(half[:], -0.5).then_inc(consts_set, 1)
                pool.memset(zero_col[:], 0.0).then_inc(consts_set, 1)
                pool.memset(eps[:], LN_EPS).then_inc(consts_set, 1)
                pool.memset(ones[:], 1.0).then_inc(consts_set, 1)
                pool.wait_ge(consts_set, 4)

                def rstd_of(n):
                    pool.wait_ge(mv_done, TPC * n + TPC)
                    nc.gpsimd.tensor_tensor(var_eps[:], mv[:, :, 1], eps[:], ALU.add).then_inc(rstd_done, 1)
                    pool.wait_ge(rstd_done, 2 * n + 1)
                    nc.gpsimd.tensor_tensor(rstd[:], var_eps[:], half[:], ALU.pow).then_inc(rstd_done, 1)

                def diff_of(n, c, first=False):
                    pool.wait_ge(xn_done, 2 * n + 2)
                    if not first:
                        pool.wait_ge(mix_done, 3 * KT * n)
                    nc.gpsimd.tensor_tensor(diff[:], xn[:, c % 2, :, 1:CH + 1], xn[:, c % 2, :, 0:CH],
                                            ALU.subtract).then_inc(diff_done, 1)

                def xn_high_of(n, c):
                    nc.gpsimd.tensor_copy(xn_half[:, c % 2, 0], xn[:, c % 2, :, 1:CH + 1]).then_inc(xn_high, 1)

                def xn_low_of(n, c):
                    pool.wait_ge(xn_high, n + 1)
                    nc.gpsimd.tensor_tensor(xn_half[:, c % 2, 1], xn[:, c % 2, :, 1:CH + 1], xn_half[:, c % 2, 0],
                                            ALU.subtract).then_inc(xn_low, 1)

                def hidden_low(n):
                    for m in range(MT):
                        pool.wait_ge(hid_high, MT * n + m + 1)
                        nc.gpsimd.tensor_tensor(hid_half[:, 1, m], hid[:, m % RING], hid_half[:, 0, m], ALU.subtract).then_inc(hid_low, 1)

                def numerator(n):
                    pool.wait_ge(bonus_done, n + 1 + 1)
                    nc.gpsimd.tensor_tensor(out_num[:], out_num[:], num[:, :, 0:CH], ALU.add).then_inc(num_done, 1)
                    pool.wait_ge(num_done, n + 1 + 1)
                    pool.wait_ge(sig_done, n + 1)
                    nc.gpsimd.tensor_tensor(out_num[:], out_num[:], sig_r[:], ALU.mult).then_inc(q_done, 1)

                def rwkv_low_of(n):
                    pool.wait_ge(rwkv_high, n + 1)
                    nc.gpsimd.tensor_tensor(rwkv_half[:, 1], rwkv[:], rwkv_half[:, 0], ALU.subtract).then_inc(rwkv_low, 1)

                def silu(n):
                    pool.wait_ge(gate_sig_done, n + 1)
                    pool.wait_ge(prod_done, n + 1)
                    nc.gpsimd.tensor_tensor(gate[:], gate_in, gate_sig, ALU.mult).then_inc(gate_done, 1)

                rstd_of(0)
                diff_of(0, 0, first=True)
                xn_high_of(0, 0)
                xn_low_of(0, 0)
                rstd_of(1)
                diff_of(1, 1)
                rstd_of(2)
                hidden_low(0)
                numerator(0)
                xn_high_of(1, 1)
                xn_low_of(1, 1)

                def body(b, c, left):
                    n = count(b, c)
                    if left >= 1:
                        silu(n)
                    if left >= 3:
                        rstd_of(n + 3)
                    rwkv_low_of(n)
                    if left == 0:
                        silu(n)
                    if left >= 2:
                        diff_of(n + 2, c + 2)
                        xn_high_of(n + 2, c + 2)
                    if left >= 1:
                        hidden_low(n + 1)
                    if left >= 2:
                        xn_low_of(n + 2, c + 2)
                    if left >= 1:
                        numerator(n + 1)

                chunks(pool, body)

            @block.scalar
            def _(act):
                act.sem_inc(hid_done, 1)
                act.dma_start(mixes[:], a["mixes"].rearrange("p (m k) -> p m k", m=3)).then_inc(mixes_loaded, 16)
                act.dma_start(decay[:], a["time_decay"]).then_inc(small_loaded, 16)
                act.dma_start(first[:], a["time_first"]).then_inc(small_loaded, 16)
                act.dma_start(b_1[:], a["b1"]).then_inc(small_loaded, 16)
                act.dma_start(b_2[:], a["b2"].rearrange("(o d) -> o d", o=1).to_broadcast([P, DIM])).then_inc(small_loaded, 16)
                act.wait_ge(rkv_loaded, 48)
                act.dma_start(raw_1, a["W1"].rearrange("(k p) d -> p k d", p=P)).then_inc(ffn_loaded[0], 16)
                act.dma_start(raw_2, a["W2"].rearrange("(m p) d -> p m d", p=P)).then_inc(ffn_loaded[1], 16)
                act.wait_ge(sums_done, 1)
                nc.scalar.activation(roots[:, 0:VAL], ps_a[:, 0, 0:VAL], ACT.Sqrt).then_inc(roots_done, 1)

                def load(name, source):
                    register = act.alloc_register(name)
                    act.load(register, source[0:1].bitcast(I32))
                    return register

                act.wait_ge(scale_done, 1)
                x_scale = load("a_x_scale", scale[:, XM:XM + 1])

                def weight_high(i):
                    nc.scalar.activation(split[i][:, 0], raw[i], ACT.Copy, scale=scale[:, columns[i]:columns[i] + 1]).then_inc(w_high, 1)

                def xn_of(n, c):
                    s = c % 2
                    if c % CPB == 0:
                        act.wait_ge(consts_set, 2)
                        before = zero_col[:]
                    else:
                        act.wait_ge(xn_done, 2 * n)
                        before = xn[:, 1 - s, :, CH:CH + 1]
                    act.wait_ge(xt_done, n + 1)
                    nc.scalar.activation(xn[:, s, :, 0:1], before, ACT.Copy).then_inc(xn_done, 1)
                    nc.scalar.activation(xn[:, s, :, 1:CH + 1], ps_t[:], ACT.Copy, scale=x_scale).then_inc(xn_done, 1)

                def mixed_high(n, first=False):
                    if not first:
                        act.wait_ge(v_done, n)
                    for i in range(3):
                        act.wait_ge(mix_done, 3 * KT * n + KT * (i + 1))
                        nc.scalar.activation(mixed_half[:, i, 0], mixed[:, i], ACT.Copy).then_inc(mix_high, 1)

                def receptance(n):
                    act.wait_ge(r_done, n + 1)
                    act.wait_ge(q_done, n + 1)
                    nc.scalar.activation(sig_r[:], ps_a[:], ACT.Sigmoid, scale=r_unscale).then_inc(sig_done, 1)
                    act.preload_act_table_set("natural_log_exp_and_others")

                def exponential(n, i):
                    e = (e_new, e_old, e_bonus)[i]
                    act.wait_ge(arg_done, 3 * KT * n + KT * (i + 1))
                    nc.scalar.activation(e[:], e[:], ACT.Exp, scale=k_negated if e is e_old else k_unscale).then_inc(exp_done, 1)

                def hidden(n, m):
                    act.wait_ge(hid_mm, MT * n + m + 1)
                    act.wait_ge(hid_low, MT * n + m + 1)
                    nc.scalar.activation(hid[:, m % RING, :], ps_a[:, m % 2, :], ACT.Relu, bias=b_1[:, m:m + 1],
                                         scale=hid_scale).then_inc(hid_done, 1)

                def hidden_high(n, m):
                    act.wait_ge(hid_done, MT * n + m + 1 + 1)
                    nc.scalar.activation(hid_half[:, 0, m], hid[:, m % RING], ACT.Copy).then_inc(hid_high, 1)

                def reciprocal(n):
                    act.wait_ge(den_done, n + 1)
                    nc.scalar.activation(out_den[:], out_den[:], ACT.Ln).then_inc(rden_done, 1)
                    act.wait_ge(rden_done, 2 * n + 1)
                    nc.scalar.activation(out_den[:], out_den[:], ACT.Exp, scale=-1.0).then_inc(rden_done, 1)

                def gate_sigmoid(n):
                    act.wait_ge(gate_in_done, n + 1 + 1)
                    nc.scalar.activation(gate_sig, gate_in, ACT.Sigmoid).then_inc(gate_sig_done, 1)

                def chunk(n, c, following, first=False):
                    receptance(n)
                    if following:
                        xn_of(n + 1, c + 1)
                    highs = 0
                    for m in range(MT):
                        if m in (0, 1, 3):
                            exponential(n, (0, 1, 3).index(m))
                        if first and m == MT // 2:
                            act.wait_ge(w_low, 5)
                        hidden(n, m)
                        if m in (2, 4, 5, 6):
                            hidden_high(n, highs)
                            highs += 1
                    for m in range(highs, MT):
                        hidden_high(n, m)

                xn_of(0, 0)
                for i in range(3):
                    weight_high(i)
                act.wait_ge(small_loaded, 16 * 5)
                for i, (t, column, loaded) in enumerate(((raw_1, W1, ffn_loaded[0]), (raw_2, W2, ffn_loaded[1]), (b_1[:], HID, small_loaded),
                                                         (raw_o, WO, raw_o_loaded))):
                    if i == 1:
                        mixed_high(0, first=True)
                    act.wait_ge(loaded, 16)
                    if i:
                        act.wait_ge(act_squared, i)
                    sq = act_squares[:, 0:t.free_size()]
                    if len(t.shape) == 3:
                        sq = sq.rearrange("p (k n) -> p k n", k=t.shape[1])
                    nc.scalar.activation(sq, t, ACT.Square, accum_out=sums[:, column:column + 1]).then_inc(act_squared, 1)
                act.wait_ge(sums_done, 2)
                nc.scalar.activation(roots[:, W1:], ps_t[:, 0, 0:COLUMNS - W1], ACT.Sqrt).then_inc(roots_done, 1)
                nc.scalar.activation(decay[:], decay[:], ACT.Exp).then_inc(decay_exp, 1)
                act.wait_ge(scale_done, 2)
                for i in (3, 4, 5):
                    weight_high(i)
                act.wait_ge(consts_done, 1)
                r_unscale = load("a_r_unscale", unscale[:, WR:WR + 1])
                k_unscale = load("a_k_unscale", unscale[:, WK:WK + 1])
                k_negated = load("a_k_negated", neg_k[:])
                hid_scale = load("a_hid_scale", unscale[:, W1:W1 + 1])
                chunk(0, 0, True, first=True)
                reciprocal(0)
                mixed_high(1)

                def body(b, c, left):
                    n = count(b, c)
                    if left >= 1:
                        gate_sigmoid(n)
                    act.wait_ge(rwkv_done, n + 1 + 1)
                    act.wait_ge(out_done, n + 1)
                    nc.scalar.activation(rwkv_half[:, 0], rwkv[:], ACT.Copy).then_inc(rwkv_high, 1)
                    if left == 0:
                        gate_sigmoid(n)
                    if left >= 1:
                        chunk(n + 1, c + 1, left >= 2)
                        reciprocal(n + 1)
                    if left >= 2:
                        mixed_high(n + 2)

                chunks(act, body)

            @block.vector
            def _(dve):
                for counts_from_one in (bonus_done, rwkv_done, gate_in_done, prod_done):
                    dve.sem_inc(counts_from_one, 1)

                def layernorm(n, c, turn):
                    dve.wait_ge(x_loaded[c % X], 16 * (turn + 1))
                    for j in range(TPC):
                        nc.vector.bn_stats(stats[:, j, :], x[:, c % X, j, :]).then_inc(stats_done, 1)

                def aggregate():
                    for j in range(TPC):
                        nc.vector.bn_aggr(mv[:, j, :], stats[:, j, :]).then_inc(mv_done, 1)

                def normalise(n, c, first=False):
                    dve.wait_ge(rstd_done, 2 * n + 2)
                    if not first:
                        dve.wait_ge(xt_done, n)
                    for j in range(TPC):
                        nc.vector.tensor_scalar(xhat[:, j, :], x[:, c % X, j, :], mv[:, j, 0:1], rstd[:, j:j + 1],
                                                ALU.subtract, ALU.mult).then_inc(xhat_done, 1)

                def mix(n, c, first=False):
                    dve.wait_ge(diff_done, n + 1)
                    for i in range(3):
                        for k in range(KT):
                            nc.vector.scalar_tensor_tensor(mixed[:, i, k, :], diff[:, k, :], mixes[:, i, k:k + 1],
                                                           xn[:, c % 2, k, 0:CH], ALU.mult, ALU.add).then_inc(mix_done, 1)
                        if first and i == 1:
                            mixed_low(n, 0)
                    if not first:
                        dve.wait_ge(v_done, n)
                    for i in range(1 if first else 0, 3):
                        mixed_low(n, i)

                def mixed_low(n, i):
                    dve.wait_ge(mix_high, 3 * n + i + 1)
                    nc.vector.tensor_tensor(mixed_half[:, i, 1], mixed[:, i], mixed_half[:, i, 0], ALU.subtract).then_inc(mix_low, 1)

                def weight_low(i):
                    dve.wait_ge(w_high, i + 1)
                    nc.vector.scalar_tensor_tensor(split[i][:, 1], raw[i], scale[:, columns[i]:columns[i] + 1], split[i][:, 0],
                                                   ALU.mult, ALU.subtract).then_inc(w_low, 1)

                def old_states(n, c):
                    dve.wait_ge(num_done, n + 1)
                    if c % CPB == 0:
                        nc.vector.memset(mx[:, :, 0:1], MAX_INIT).then_inc(state_set, 1)
                        nc.vector.memset(num[:, :, 0:1], 0.0).then_inc(state_set, 1)
                        nc.vector.memset(den[:, :, 0:1], 0.0).then_inc(state_set, 1)
                    else:
                        for t in (mx, num, den):
                            nc.vector.tensor_copy(t[:, :, 0:1], t[:, :, CH:CH + 1]).then_inc(state_set, 1)

                def keys(n):
                    dve.wait_ge(state_set, 3 * n + 3)
                    dve.wait_ge(k_done, n + 1)
                    for k in range(KT):
                        nc.vector.tensor_tensor_scan(mx[:, k, 1:CH + 1], decay[:, k:k + 1].to_broadcast([P, CH]),
                                                     ps_b[:, k, :], mx[:, k, 0:1], ALU.add, ALU.max).then_inc(mx_done, 1)
                    dve.wait_ge(mx_done, KT * n + KT)
                    nc.vector.tensor_tensor(dist[:], ps_b[:], mx[:, :, 0:CH], ALU.subtract).then_inc(dist_done, 1)
                    dve.wait_ge(dist_done, n + 1)
                    for k in range(KT):
                        nc.vector.tensor_scalar(e_new[:, k, :], dist[:, k, :], decay[:, k:k + 1], 0.0,
                                                ALU.subtract, ALU.min).then_inc(arg_done, 1)
                    for k in range(KT):
                        nc.vector.tensor_scalar(e_old[:, k, :], dist[:, k, :], decay[:, k:k + 1], 0.0,
                                                ALU.subtract, ALU.max).then_inc(arg_done, 1)
                    for k in range(KT):
                        nc.vector.tensor_scalar(e_bonus[:, k, :], dist[:, k, :], first[:, k:k + 1], cap[:],
                                                ALU.add, ALU.min).then_inc(arg_done, 1)

                def states(n):
                    dve.wait_ge(exp_done, 3 * n + 1)
                    dve.wait_ge(v_done, n + 1)
                    nc.vector.scalar_tensor_tensor(new_v[:], ps_c[:], unscale[:, WV:WV + 1], e_new[:], ALU.mult, ALU.mult).then_inc(new_done, 1)
                    dve.wait_ge(exp_done, 3 * n + 2)
                    for k in range(KT):
                        nc.vector.tensor_tensor_scan(den[:, k, 1:CH + 1], e_old[:, k, :], e_new[:, k, :],
                                                     den[:, k, 0:1], ALU.mult, ALU.add).then_inc(scan_done, 1)
                    dve.wait_ge(new_done, n + 1)
                    for k in range(KT):
                        nc.vector.tensor_tensor_scan(num[:, k, 1:CH + 1], e_old[:, k, :], new_v[:, k, :],
                                                     num[:, k, 0:1], ALU.mult, ALU.add).then_inc(scan_done, 1)
                    dve.wait_ge(exp_done, 3 * n + 3)
                    dve.wait_ge(rwkv_done, n + 1)
                    dve.wait_ge(scan_done, 2 * KT * n + 2 * KT)
                    nc.vector.scalar_tensor_tensor(out_num[:], ps_c[:], unscale[:, WV:WV + 1], e_bonus[:], ALU.mult, ALU.mult).then_inc(bonus_done, 1)
                    nc.vector.tensor_tensor(out_den[:], e_bonus[:], den[:, :, 0:CH], ALU.add).then_inc(den_done, 1)

                def gate_input(n):
                    dve.wait_ge(ffn_done, n + 1)
                    dve.wait_ge(gate_done, n + 1)
                    nc.vector.scalar_tensor_tensor(gate_in, ps_ffn, unscale[:, W2:W2 + 1],
                                                   b_2[:].rearrange("p (o d) -> p o d", o=1).to_broadcast([P, TPC, DIM]),
                                                   ALU.mult, ALU.add).then_inc(gate_in_done, 1)

                def sum_squares(t, column):
                    if column:
                        dve.wait_ge(squares_done, column)
                    sq = squares[:, 0:t.free_size()]
                    if len(t.shape) == 3:
                        sq = sq.rearrange("p (k n) -> p k n", k=t.shape[1])
                    nc.vector.tensor_tensor_reduce(out=sq, in0=t, in1=t, scale=1.0, scalar=0.0, op0=ALU.mult, op1=ALU.add,
                                                   accum_out=sums[:, column:column + 1]).then_inc(squares_done, 1)

                def scales(group, steps):
                    nc.vector.tensor_scalar(power[:, group].bitcast(I32), bound[:, group].bitcast(I32), 0x7F800000, None,
                                            ALU.bitwise_and).then_inc(bound_done, 1)
                    dve.wait_ge(bound_done, steps + 1)
                    nc.vector.reciprocal(scale[:, group], power[:, group]).then_inc(bound_done, 1)
                    dve.wait_ge(bound_done, steps + 2)
                    nc.vector.tensor_scalar(scale[:, group], scale[:, group], F16_TARGET, None, ALU.mult).then_inc(scale_done, 1)

                xn_max, room = float(np.sqrt(DIM)), F16_TARGET / X_TARGET
                layernorm(0, 0, 0)
                dve.wait_ge(stats_done, TPC)
                dve.wait_ge(rkv_loaded, 48)
                aggregate()
                for column in (WR, WK, WV):
                    sum_squares(raw[column], column)
                dve.wait_ge(mixes_loaded, 16)
                sum_squares(mixes[:], XM)
                normalise(0, 0, first=True)
                dve.wait_ge(roots_done, 1)
                nc.vector.tensor_scalar(bound[:, WR:XM], roots[:, WR:XM], 1e-20, None, ALU.max).then_inc(bound_done, 1)
                nc.vector.tensor_scalar(bound[:, XM:VAL], roots[:, XM:VAL], 2.0 * xn_max * room, xn_max * room, ALU.mult, ALU.add).then_inc(bound_done, 1)
                dve.wait_ge(bound_done, 2)
                nc.vector.tensor_scalar(bound[:, VAL:W1], bound[:, XM:VAL], bound[:, WV:XM], 1.0 / room, ALU.mult, ALU.mult).then_inc(bound_done, 1)
                dve.wait_ge(bound_done, 3)
                scales(slice(WR, W1), 3)
                for i in range(3):
                    weight_low(i)
                nc.vector.tensor_scalar(unscale[:, WR:XM], power[:, WR:XM], power[:, XM:VAL], F16_TARGET ** -2,
                                        ALU.mult, ALU.mult).then_inc(bound_done, 1)
                nc.vector.tensor_tensor(key_scale[:], scale[:, WK:WV], scale[:, XM:VAL], ALU.mult).then_inc(bound_done, 1)
                dve.wait_ge(bound_done, 6)
                nc.vector.tensor_tensor(unscale[:, WV:XM], unscale[:, WV:XM], scale[:, VAL:W1], ALU.mult)
                dve.wait_ge(squares_done, XM + 1)
                mix(0, 0, first=True)
                layernorm(1, 1, 0)
                dve.wait_ge(stats_done, 2 * TPC)
                aggregate()
                dve.wait_ge(roots_done, 2)
                nc.vector.tensor_scalar(bound[:, W1:HID], roots[:, W1:HID], 1e-20, None, ALU.max).then_inc(bound_done, 1)
                dve.wait_ge(bound_done, 8)
                nc.vector.scalar_tensor_tensor(bound[:, HID:COLUMNS], bound[:, W1:W2], xn_max, roots[:, HID:COLUMNS],
                                               ALU.mult, ALU.add).then_inc(bound_done, 1)
                dve.wait_ge(bound_done, 9)
                scales(slice(W1, COLUMNS), 9)
                dve.wait_ge(scale_done, 2)
                nc.vector.tensor_scalar(unscale[:, W1:W2], power[:, W1:W2], power[:, XM:VAL], F16_TARGET ** -2,
                                        ALU.mult, ALU.mult).then_inc(bound_done, 1)
                nc.vector.tensor_scalar(unscale[:, W2:WO], power[:, W2:WO], power[:, HID:COLUMNS], F16_TARGET ** -2, ALU.mult, ALU.mult)
                nc.vector.tensor_scalar(unscale[:, WO:HID], power[:, WO:HID], power[:, VAL:W1], F16_TARGET ** -2, ALU.mult, ALU.mult)
                nc.vector.tensor_scalar(neg_k[:], unscale[:, WK:WV], -1.0, None, ALU.mult)
                nc.vector.tensor_scalar(b_1[:], b_1[:], scale[:, HID:COLUMNS], None, ALU.mult)
                dve.wait_ge(decay_exp, 1)
                nc.vector.tensor_scalar(decay[:], decay[:], key_scale[:], -1.0, ALU.mult, ALU.mult)
                nc.vector.tensor_scalar(first[:], first[:], key_scale[:], None, ALU.mult)
                nc.vector.tensor_scalar(cap[:], key_scale[:], EXP_CAP, None, ALU.mult)
                dve.wait_ge(bound_done, 12)
                nc.vector.tensor_tensor(unscale[:, W1:W2], unscale[:, W1:W2], scale[:, HID:COLUMNS], ALU.mult).then_inc(consts_done, 1)
                normalise(1, 1)
                weight_low(3)
                old_states(0, 0)
                dve.wait_ge(consts_done, 1)
                keys(0)
                layernorm(2, 2, 0)
                dve.wait_ge(stats_done, 3 * TPC)
                aggregate()
                for i in (4, 5):
                    weight_low(i)
                states(0)
                normalise(2, 2)
                mix(1, 1)

                def body(b, c, left):
                    n = count(b, c)
                    if left >= 1:
                        gate_input(n)
                    dve.wait_ge(q_done, n + 1 + 1)
                    dve.wait_ge(rden_done, 2 * n + 2)
                    nc.vector.tensor_tensor(rwkv[:], out_num[:], out_den[:], ALU.mult).then_inc(rwkv_done, 1)
                    if left == 0:
                        gate_input(n)
                    if left >= 3:
                        layernorm(n + 3, c + 3, b + (c + 3) // X)
                        dve.wait_ge(stats_done, TPC * (n + 3) + TPC)
                    if left >= 1:
                        old_states(n + 1, c + 1)
                    if left >= 3:
                        aggregate()
                    if left >= 1:
                        keys(n + 1)
                    if left >= 1:
                        states(n + 1)
                    if left >= 3:
                        normalise(n + 3, c + 3)
                    if left >= 2:
                        mix(n + 2, c + 2)
                    dve.wait_ge(out_done, n + 1 + 1)
                    dve.wait_ge(gate_done, n + 1 + 1)
                    dve.wait_ge(x1_stored[c % 2], 16 * (b * (CPB // 2) + c // 2) + 16)
                    nc.vector.scalar_tensor_tensor(x1[:, c % 2], ps_out, unscale[:, WO:HID], gate[:], ALU.mult, ALU.mult).then_inc(prod_done, 1)
                    dve.wait_ge(prod_done, n + 1 + 1)
                    nc.vector.tensor_tensor(x1[:, c % 2], x1[:, c % 2], x[:, c], ALU.add).then_inc(x1_done, 1)

                chunks(dve, body)

            @block.tensor
            def _(pe):
                pe.sem_inc(out_done, 1)

                def products(ps, pairs, first=True, last=True):
                    steps = [(l[h], r[g]) for l, r in pairs for h, g in ((0, 0), (0, 1), (1, 0))]
                    for i, (l, r) in enumerate(steps):
                        mm = nc.tensor.matmul(ps, l, r, start=(first and i == 0), stop=(last and i == len(steps) - 1))
                    return mm

                def halves(t, *at):
                    return [t[(slice(None), h) + at] for h in range(2)]

                def transposes(n):
                    pe.wait_ge(xhat_done, TPC * n + TPC)
                    for k in range(KT):
                        for j in range(TPC):
                            last = nc.tensor.transpose(ps_t[:, k, j * P:(j + 1) * P], xhat[:, j, k * P:(k + 1) * P], ident[:])
                    last.then_inc(xt_done, 1)

                def project(ps, w, i):
                    for m in range(KT):
                        last = products(ps[:, m, :], [(halves(w, k, slice(m * P, (m + 1) * P)),
                                                       [mixed_half[:, i, h, k, :] for h in range(2)]) for k in range(KT)])
                    return last

                def projections(n, between=None):
                    pe.wait_ge(hid_done, MT * n + 1)
                    pe.wait_ge(mix_low, 3 * n + 1)
                    project(ps_a, w_r, 0).then_inc(r_done, 1)
                    if between:
                        between()
                    pe.wait_ge(gate_in_done, n + 1)
                    pe.wait_ge(mix_low, 3 * n + 2)
                    project(ps_b, w_k, 1).then_inc(k_done, 1)
                    pe.wait_ge(bonus_done, n + 1)
                    pe.wait_ge(mix_low, 3 * n + 3)
                    project(ps_c, w_v, 2).then_inc(v_done, 1)

                def hidden(n, c):
                    pe.wait_ge(xn_low, n + 1)
                    for m in range(MT):
                        if m < 2:
                            pe.wait_ge(sig_done, n + 1)
                        else:
                            pe.wait_ge(hid_done, MT * n + m - 1 + 1)
                        products(ps_a[:, m % 2, :], [(halves(w_1, k, slice(m * P, (m + 1) * P)),
                                                      [xn_half[:, c % 2, h, k, :] for h in range(2)])
                                                     for k in range(KT)]).then_inc(hid_mm, 1)

                def ffn(n):
                    pe.wait_ge(dist_done, n + 1)
                    for m in range(MT):
                        pe.wait_ge(hid_low, MT * n + m + 1 + RING)
                        for j in range(TPC):
                            mm = products(ps_ffn[:, j, :], [(halves(hid_half, m, slice(j * P, (j + 1) * P)), halves(w_2, m))],
                                          first=(m == 0 and j % 2 == 0), last=(m == MT - 1 and j % 2 == 1))
                    mm.then_inc(ffn_done, 1)

                pe.wait_ge(consts_set, 4)
                pe.wait_ge(squares_done, VAL)
                nc.tensor.matmul(ps_a[:, 0, 0:VAL], ones[:], sums[:, 0:VAL], start=True, stop=True).then_inc(sums_done, 1)
                pe.wait_ge(small_loaded, 16 * 5)
                transposes(0)

                def second_sums():
                    pe.wait_ge(act_squared, COLUMNS - W1)
                    nc.tensor.matmul(ps_t[:, 0, 0:COLUMNS - W1], ones[:], sums[:, W1:], start=True, stop=True).then_inc(sums_done, 1)

                pe.wait_ge(roots_done, 1)
                pe.wait_ge(w_low, 3)
                projections(0, second_sums)
                pe.wait_ge(roots_done, 2)
                transposes(1)
                pe.wait_ge(w_low, 4)
                hidden(0, 0)
                pe.wait_ge(w_low, 5)
                ffn(0)
                pe.wait_ge(w_low, 6)

                def body(b, c, left):
                    n = count(b, c)
                    if left >= 1:
                        projections(n + 1)
                    if left >= 2:
                        pe.wait_ge(prod_done, n + 1)
                        pe.wait_ge(xn_done, 2 * n + 4)
                        transposes(n + 2)
                    if left >= 1:
                        hidden(n + 1, c + 1)
                    pe.wait_ge(rwkv_low, n + 1)
                    if left >= 2:
                        pe.wait_ge(xn_done, 2 * n + 6)
                    pe.wait_ge(prod_done, n + 1)
                    for j in range(TPC):
                        mm = products(ps_out[:, j, :], [(halves(rwkv_half, k, slice(j * P, (j + 1) * P)), halves(w_o, k)) for k in range(KT)])
                    mm.then_inc(out_done, 1)
                    if left >= 1:
                        ffn(n + 1)

                chunks(pe, body)


def scratch(nc):
    def dram(name, shape, dt=F32):
        return nc.dram_tensor(name, shape, dt, kind="Internal").ap()

    return {
        "x1": dram("x1_d", [TOKENS, DIM]),
        "qc": dram("qc_d", [BATCH, 2, DIM, SEQ], F16),
        "qr": dram("qr_d", [BATCH, 2, HEADS * D_R, SEQ], F16),
        "kc": dram("kc_d", [BATCH, 2, DIM, SEQ], F16),
        "kr": dram("kr_d", [BATCH, 2, D_R, SEQ], F16),
        "v": dram("v_d", [TOKENS, HEADS * VW]),
        "gate": dram("gate_d", [TOKENS, DIM]),
        "attn": dram("attn_d", [TOKENS, DIM]),
    }


class Early:

    def __init__(self, ctx, nc):
        def sb(name, shape):
            return ctx.enter_context(nc.sbuf_tensor(name, shape, F32, side="right"))

        def sem(name):
            return ctx.enter_context(nc.semaphore(name))

        self.x = sb("rows", [P, CPB, TPC, DIM])
        self.gate_in = sb("b_gi", [P, TPC, DIM])
        self.gate_sig = sb("b_gs", [P, TPC, DIM])
        self.raw_c = self.gate_in[:, 0:KT]
        self.raw_r = self.gate_in[:, KT:2 * KT]
        self.raw_q = self.gate_sig[:, 0:KT].rearrange("p k n -> p (k n)")
        self.raw_k = self.gate_sig[:, KT:2 * KT]
        self.raw_uk = sb("b_rawuk", [P, DIM])
        self.raw_kr = sb("b_rawkr", [P, KT, VW + D_R])
        self.raw_uv = sb("b_rawuv", [P, DIM])
        self.mixes = sb("b_mixes", [P, 2, KT])
        self.weights = ((self.raw_c, "Wc"), (self.raw_q, "Wq"), (self.raw_uk[:], "Wuk"), (self.raw_kr[:], "Wkr"),
                        (self.raw_uv[:], "Wuv"), (self.raw_r, "W1rT"), (self.raw_k, "W1kT"))
        self.x_loaded = [sem(f"b_x_loaded{i}") for i in range(CPB)]
        self.weights_loaded = sem("b_weights_loaded")
        self.loads = len(self.weights) + 1

    def load_weights(self, sp, a):
        for t, name in self.weights:
            source = a[name]
            if len(t.shape) == 3:
                source = source.rearrange("(k p) n -> p k n", p=P)
            sp.dma_start(t, source).then_inc(self.weights_loaded, 16)
        sp.dma_start(self.mixes[:], a["mixes1"].rearrange("p (m k) -> p m k", m=2)).then_inc(self.weights_loaded, 16)


STORES = 8


def layer1_projections(nc, a, d, ident, early, score_scale, first):
    with ExitStack() as ctx:
        def sb(name, shape, dt=F32):
            return ctx.enter_context(nc.sbuf_tensor(name, shape, dt))

        def sem(name):
            return ctx.enter_context(nc.semaphore(name))

        QW = DIM + 2 * HEADS * D_R
        XS = CPB
        x, x_loaded = early.x, early.x_loaded
        ones = sb("b_ones", [P, P])
        relu = sb("b_relu", [P, KT, CH])
        act_k = sb("b_actk", [P, KT, CH])
        gate_in, gate_sig = early.gate_in, early.gate_sig
        raw_c, raw_q, raw_uk, raw_kr, raw_uv, raw_r, raw_k = (t for t, _ in early.weights)
        mixes, weights_loaded = early.mixes, early.weights_loaded
        w_v = sb("b_wv", [P, KT, DIM])
        w_c = sb("b_wc", [P, 2, KT, 4 * LATENT], F16)
        w_q = sb("b_wq", [P, 2, QW], F16)
        w_uk = sb("b_wuk", [P, 2, DIM], F16)
        w_kr = sb("b_wkr", [P, 2, KT, VW + D_R], F16)
        w_uv = sb("b_wuv", [P, 2, DIM], F16)
        w_r = sb("b_wr", [P, 2, KT, DIM], F16)
        w_k = sb("b_wk", [P, 2, KT, DIM], F16)
        cos = sb("b_cos", [P, SEQ])
        sin = sb("b_sin", [P, SEQ])
        DQ, DKV, WQ, WUK, WKR, WUV, WR, WK, X, CQ, CKV, Q, K = range(13)
        NORMS = X + 1
        sums = sb("b_sums", [P, NORMS])
        roots = sb("b_roots", [P, NORMS])
        bound = sb("b_bound", [P, K + 1])
        kr_bound = sb("b_kr_bound", [P, 1])
        power = sb("b_power", [P, K + 1])
        scale = sb("b_scale", [P, K + 1])
        inverse = sb("b_inverse", [P, K + 1])
        factor = sb("b_factor", [P, WK + 1])
        eps = sb("b_eps", [P, TPC])
        half = sb("b_half", [P, TPC])
        zero_col = sb("b_zero", [P, KT, 1])
        stats = sb("b_stats", [P, TPC, 6])
        mv = sb("b_mv", [P, TPC, 2])
        var_eps = sb("b_var", [P, TPC])
        rstd = sb("b_rstd", [P, TPC])
        xhat = sb("b_xhat", [P, TPC, DIM])
        xn = sb("b_xn", [P, 2, KT, CH + 1])
        xn_half = sb("b_xnh", [P, 2, KT, CH], F16)
        diff = sb("b_diff", [P, KT, CH])
        x_r, x_k = (sb(f"b_x{n}", [P, KT, CH]) for n in "rk")
        xr_half, xk_half = (sb(f"b_x{n}h", [P, 2, KT, CH], F16) for n in "rk")
        lat = sb("b_lat", [P, 2, CH], F16)
        q_cos = sb("b_qcos", [P, CH])
        q_sin = sb("b_qsin", [P, CH])
        k_cos = sb("b_kcos", [D_R, CH])
        k_sin = sb("b_ksin", [D_R, CH])
        qc = sb("b_qc", [P, 2, 2, KT, CH], F16)
        kc = sb("b_kc", [P, 2, 2, KT, CH], F16)
        qr = sb("b_qr", [P, 2, 2, CH], F16)
        kr = sb("b_kr", [D_R, 2, 2, CH], F16)
        val = sb("b_val", [P, 2, TPC, HEADS, VW])
        sig_r = sb("b_sigr", [P, TPC, DIM])
        gate = sb("b_gate", [P, 2, TPC, DIM])

        ps_a = ctx.enter_context(nc.psum_tensor("b_ps0", [P, 2, CH], F32))
        ps_b = ctx.enter_context(nc.psum_tensor("b_ps1", [P, 2, CH], F32))
        ps_c = ctx.enter_context(nc.psum_tensor("b_ps2", [P, 2, CH], F32))
        ps_t = ctx.enter_context(nc.psum_tensor("b_ps3", [P, 2, CH], F32))
        ps_val = ps_a[:].rearrange("p a (j d) -> p (a j) d", d=DIM)
        ps_r = ps_b[:].rearrange("p a (j d) -> p (a j) d", d=DIM)
        ps_kv = ps_c[:].rearrange("p a (j d) -> p (a j) d", d=DIM)

        late_loaded = sem("b_late_loaded")
        stored = [sem(f"b_stored{i}") for i in range(2)]
        consts_set = sem("b_consts_set")
        squares_done = sem("b_squares_done")
        sums_done = sem("b_sums_done")
        roots_done = sem("b_roots_done")
        bound_done = sem("b_bound_done")
        scale_done = sem("b_scale_done")
        w_high = sem("b_w_high")
        w_low = sem("b_w_low")
        stats_done = sem("b_stats_done")
        mv_done = sem("b_mv_done")
        rstd_done = sem("b_rstd_done")
        xhat_done = sem("b_xhat_done")
        xt_done = sem("b_xt_done")
        xn_done = sem("b_xn_done")
        xn_high = sem("b_xn_high")
        xn_low = sem("b_xn_low")
        diff_done = sem("b_diff_done")
        mix_done = sem("b_mix_done")
        xk_high = sem("b_xk_high")
        xk_low = sem("b_xk_low")
        xr_high = sem("b_xr_high")
        xr_low = sem("b_xr_low")
        lat_mm = sem("b_lat_mm")
        lat_high = sem("b_lat_high")
        lat_low = sem("b_lat_low")
        kr_mm = sem("b_kr_mm")
        k_mm = sem("b_k_mm")
        qc_mm = sem("b_qc_mm")
        qr_mm = sem("b_qr_mm")
        kc_mm = sem("b_kc_mm")
        r_mm = sem("b_r_mm")
        val_mm = sem("b_val_mm")
        kv_mm = sem("b_kv_mm")
        relu_done = sem("b_relu_done")
        act_done = sem("b_act_done")
        qc_high = sem("b_qc_high")
        qc_low = sem("b_qc_low")
        kc_high = sem("b_kc_high")
        kc_low = sem("b_kc_low")
        kr_parts = sem("b_kr_parts")
        kr_sum = sem("b_kr_sum")
        kr_high = sem("b_kr_high")
        kr_low = sem("b_kr_low")
        qr_parts = sem("b_qr_parts")
        qr_high = sem("b_qr_high")
        qr_low = sem("b_qr_low")
        sig_done = sem("b_sig_done")
        val_done = sem("b_val_done")
        gate_in_done = sem("b_gate_in_done")
        gate_sig_done = sem("b_gate_sig_done")
        gate_done = sem("b_gate_done")

        x_v3 = d["x1"].rearrange("(n j p) c -> n p j c", j=TPC, p=P)
        gate_v3 = d["gate"].rearrange("(n j p) c -> n p j c", j=TPC, p=P)
        val_v3 = d["v"].rearrange("(n j p) c -> n p j c", j=TPC, p=P)
        LEFT, RIGHT = slice(0, 2 * LATENT), slice(2 * LATENT, 4 * LATENT)
        def flat(t):
            return t[:].rearrange("p k n -> p (k n)")

        W_C = KT * 2 * LATENT
        normed = ((raw_c[:, :, LEFT], DQ, flat(act_k)[:, 0:W_C].rearrange("p (k n) -> p k n", k=KT)),
                  (raw_c[:, :, RIGHT], DKV, flat(act_k)[:, W_C:2 * W_C].rearrange("p (k n) -> p k n", k=KT)),
                  (raw_uk, WUK, flat(x_k)[:, 0:DIM]), (raw_uv, WUV, flat(x_k)[:, DIM:2 * DIM]),
                  (raw_kr, WKR, x_r[:, :, 0:VW + D_R]), (mixes[:], X, diff[:, :, 0:KT]))
        act_normed = ((raw_q, WQ, x_k[:, KT - 1, 0:QW]), (raw_r, WR, sig_r[:, 0:KT]), (raw_k, WK, sig_r[:, KT:2 * KT]))
        parts = [(raw_c[:, :, LEFT], w_c[:, :, :, LEFT], DQ), (raw_c[:, :, RIGHT], w_c[:, :, :, RIGHT], DKV),
                 (raw_kr, w_kr[:], WKR), (raw_k, w_k[:], WK), (raw_q, w_q[:], WQ),
                 (raw_uk, w_uk[:], WUK), (raw_uv, w_uv[:], WUV), (raw_r, w_r[:], WR)]

        def chunks(eng, body):
            with eng.Fori(0, BATCH - 1) as b:
                for c in range(CPB):
                    body(b, c, CPB)
            for c in range(CPB):
                body(BATCH - 1, c, CPB - 1 - c)

        def count(b, c):
            return b * CPB + c

        def turns(b, c):
            return b * (CPB // 2) + c // 2

        with nc.Block() as block:
            @block.sync
            def _(sp):
                for s in range(2):
                    sp.sem_inc(stored[s], 16)
                sp.dma_start(x[:, XS - 1], x_v3[XS - 1]).then_inc(x_loaded[XS - 1], 16)
                sp.dma_start(cos[:], a["cos"]).then_inc(late_loaded, 16)
                sp.dma_start(sin[:], a["sin"]).then_inc(late_loaded, 16)
                sp.dma_start(w_v[:], a["W1vT"].rearrange("(k p) n -> p k n", p=P)).then_inc(late_loaded, 16)

                def store(b, c):
                    n, s, t = count(b, c), c % 2, slice(c * CH, (c + 1) * CH)
                    sp.wait_ge(qc_low, n + 1)
                    for h in range(2):
                        sp.dma_start(d["qc"][b, h, :, t].rearrange("(m p) t -> p m t", p=P), qc[:, s, h]).then_inc(stored[s], 16)
                    sp.wait_ge(kr_low, n + 1 + 1)
                    sp.dma_start(d["kr"][b, :, :, t].rearrange("h p t -> p h t"), kr[:, s]).then_inc(stored[s], 16)
                    sp.wait_ge(kc_low, n + 1)
                    for h in range(2):
                        sp.dma_start(d["kc"][b, h, :, t].rearrange("(m p) t -> p m t", p=P), kc[:, s, h]).then_inc(stored[s], 16)
                    sp.wait_ge(qr_low, n + 1)
                    sp.dma_start(d["qr"][b, :, :, t].rearrange("h p t -> p h t"), qr[:, s]).then_inc(stored[s], 16)
                    sp.wait_ge(val_done, n + 1 + 1)
                    sp.dma_start(val_v3[n], val[:, s].rearrange("p j h e -> p j (h e)")).then_inc(stored[s], 16)
                    sp.wait_ge(gate_done, n + 1 + 1)
                    sp.dma_start(gate_v3[n], gate[:, s]).then_inc(stored[s], 16)

                def body(b, c, left):
                    n = count(b, c)
                    if left >= XS:
                        sp.wait_ge(xhat_done, TPC * n + TPC)
                        sp.dma_start(x[:, c], x_v3[n + XS]).then_inc(x_loaded[c], 16)
                    store(b, c)
                    if left == CPB - 1:
                        for s in range(2):
                            sp.wait_ge(stored[s], 16 * STORES * CPB // 2 + 16)
                        load_group(sp, d, first, 0, 0)

                chunks(sp, body)
                for s in range(2):
                    sp.wait_ge(stored[s], 16 * STORES * NCH // 2 + 16)

            @block.gpsimd
            def _(pool):
                for counts_from_one in (kr_low, gate_done):
                    pool.sem_inc(counts_from_one, 1)
                pool.memset(half[:], -0.5).then_inc(consts_set, 1)
                pool.memset(zero_col[:], 0.0).then_inc(consts_set, 1)
                pool.memset(ones[:], 1.0).then_inc(consts_set, 1)
                pool.memset(eps[:], LN_EPS).then_inc(consts_set, 1)
                pool.wait_ge(consts_set, 4)

                def rstd_of(n):
                    pool.wait_ge(mv_done, TPC * n + TPC)
                    nc.gpsimd.tensor_tensor(var_eps[:], mv[:, :, 1], eps[:], ALU.add).then_inc(rstd_done, 1)
                    pool.wait_ge(rstd_done, 2 * n + 1)
                    nc.gpsimd.tensor_tensor(rstd[:], var_eps[:], half[:], ALU.pow).then_inc(rstd_done, 1)

                def diff_of(n, c, first=False):
                    pool.wait_ge(xn_done, 2 * n + 2)
                    if not first:
                        pool.wait_ge(mix_done, 2 * KT * n)
                    nc.gpsimd.tensor_tensor(diff[:], xn[:, c % 2, :, 1:CH + 1], xn[:, c % 2, :, 0:CH],
                                            ALU.subtract).then_inc(diff_done, 1)

                def xn_low_of(n, c):
                    pool.wait_ge(xn_high, n + 1)
                    nc.gpsimd.tensor_tensor(xn_half[:, 1], xn[:, c % 2, :, 1:CH + 1], xn_half[:, 0], ALU.subtract).then_inc(xn_low, 1)

                def xr_low_of(n):
                    pool.wait_ge(xr_high, n + 1)
                    nc.gpsimd.tensor_tensor(xr_half[:, 1], x_r[:], xr_half[:, 0], ALU.subtract).then_inc(xr_low, 1)

                rstd_of(0)
                pool.memset(val[:], 0.0).then_inc(consts_set, 1)
                pool.wait_ge(consts_set, 5)
                for s in range(2):
                    pool.memset(val[:, s, :, :, D_H:D_H + 1], 1.0).then_inc(consts_set, 1)
                xn_low_of(0, 0)
                diff_of(0, 0, first=True)
                rstd_of(1)
                xr_low_of(0)

                def body(b, c, left):
                    n, s = count(b, c), c % 2
                    pool.wait_ge(kr_parts, 2 * n + 2)
                    nc.gpsimd.tensor_tensor(k_cos[:], k_cos[:], k_sin[:], ALU.add).then_inc(kr_sum, 1)
                    pool.wait_ge(relu_done, n + 1)
                    nc.gpsimd.tensor_tensor(act_k[:], relu[:], relu[:], ALU.mult).then_inc(act_done, 1)
                    if left >= 1:
                        diff_of(n + 1, c + 1)
                        xn_low_of(n + 1, c + 1)
                    pool.wait_ge(kr_high, n + 1)
                    nc.gpsimd.tensor_tensor(kr[:, s, 1, :], k_cos[:], kr[:, s, 0, :], ALU.subtract).then_inc(kr_low, 1)
                    if left >= 2:
                        rstd_of(n + 2)
                    if left >= 1:
                        xr_low_of(n + 1)
                    pool.wait_ge(gate_sig_done, n + 1)
                    pool.wait_ge(stored[s], 16 * STORES * turns(b, c) + 16)
                    nc.gpsimd.tensor_tensor(gate[:, s], gate_in[:], gate_sig[:], ALU.mult).then_inc(gate_done, 1)

                chunks(pool, body)

            @block.scalar
            def _(act):
                for counts_from_one in (val_done, sig_done):
                    act.sem_inc(counts_from_one, 1)
                act.wait_ge(weights_loaded, 16 * early.loads)
                for t, column, sq in act_normed:
                    nc.scalar.activation(sq, t, ACT.Square, accum_out=sums[:, column:column + 1]).then_inc(squares_done, 1)
                act.wait_ge(sums_done, 1)
                nc.scalar.activation(roots[:], ps_a[:, 0, 0:NORMS], ACT.Sqrt).then_inc(roots_done, 1)

                def load(name, source):
                    register = act.alloc_register(name)
                    act.load(register, source[0:1].bitcast(I32))
                    return register

                act.wait_ge(bound_done, 11)
                x_scale = load("b_x_scale", scale[:, X:X + 1])

                def xn_of(n, c):
                    s = c % 2
                    if c % CPB == 0:
                        act.wait_ge(consts_set, 2)
                        before = zero_col[:]
                    else:
                        act.wait_ge(xn_done, 2 * n)
                        before = xn[:, 1 - s, :, CH:CH + 1]
                    act.wait_ge(xt_done, n + 1)
                    nc.scalar.activation(xn[:, s, :, 0:1], before, ACT.Copy).then_inc(xn_done, 1)
                    nc.scalar.activation(xn[:, s, :, 1:CH + 1], ps_t[:], ACT.Copy, scale=x_scale).then_inc(xn_done, 1)
                    nc.scalar.activation(xn_half[:, 0], ps_t[:], ACT.Copy, scale=x_scale).then_inc(xn_high, 1)

                def mixed_high(n, first=False):
                    act.wait_ge(mix_done, 2 * KT * n + KT)
                    if not first:
                        act.wait_ge(k_mm, n)
                    nc.scalar.activation(xk_half[:, 0], x_k[:], ACT.Copy).then_inc(xk_high, 1)
                    act.wait_ge(mix_done, 2 * KT * n + 2 * KT)
                    if not first:
                        act.wait_ge(r_mm, n)
                    nc.scalar.activation(xr_half[:, 0], x_r[:], ACT.Copy).then_inc(xr_high, 1)

                xn_of(0, 0)
                for w, halves, i in parts:
                    nc.scalar.activation(halves[:, 0], w, ACT.Copy, scale=scale[:, i:i + 1]).then_inc(w_high, 1)
                act.wait_ge(scale_done, 1)
                c_factor, q_factor, k_factor, v_factor, r_factor, mix_k_factor = (
                    load(f"b_factor{i}", factor[:, i:i + 1]) for i in (DQ, WQ, WUK, WUV, WR, WK))
                ckv_factor = load("b_factor_ckv", factor[:, DKV:DKV + 1])
                mixed_high(0, first=True)

                def latents_high(n):
                    for i, f in enumerate((c_factor, ckv_factor)):
                        act.wait_ge(lat_mm, 2 * n + i + 1)
                        nc.scalar.activation(lat[:, i], ps_a[:, i, :], ACT.Copy, scale=f).then_inc(lat_high, 1)

                latents_high(0)

                def body(b, c, left):
                    n, s = count(b, c), c % 2
                    act.wait_ge(k_mm, n + 1)
                    nc.scalar.activation(relu[:], ps_b[:], ACT.Relu, scale=mix_k_factor).then_inc(relu_done, 1)
                    act.wait_ge(stored[s], 16 * STORES * turns(b, c) + 16)
                    act.wait_ge(qc_mm, n + 1)
                    nc.scalar.activation(qc[:, s, 0], ps_c[:], ACT.Copy, scale=q_factor).then_inc(qc_high, 1)
                    if left >= 1:
                        xn_of(n + 1, c + 1)
                    act.wait_ge(kc_mm, n + 1)
                    nc.scalar.activation(kc[:, s, 0], ps_c[:], ACT.Copy, scale=k_factor).then_inc(kc_high, 1)
                    act.wait_ge(kr_sum, n + 1)
                    nc.scalar.activation(kr[:, s, 0, :], k_cos[:], ACT.Copy).then_inc(kr_high, 1)
                    act.wait_ge(qr_parts, 3 * n + 3)
                    nc.scalar.activation(qr[:, s, 0, :], q_cos[:], ACT.Copy).then_inc(qr_high, 1)
                    act.wait_ge(r_mm, n + 1)
                    nc.scalar.activation(sig_r[:], ps_r, ACT.Sigmoid, scale=r_factor).then_inc(sig_done, 1)
                    act.wait_ge(val_mm, n + 1)
                    act.wait_ge(consts_set, 7)
                    nc.scalar.activation(val[:, s, :, :, 0:D_H].rearrange("p j h e -> p (j h) e"),
                                         ps_a[:].rearrange("p a (h e) -> p (a h) e", e=D_H), ACT.Copy, scale=v_factor).then_inc(val_done, 1)
                    if left >= 1:
                        mixed_high(n + 1)
                        latents_high(n + 1)
                    act.wait_ge(gate_in_done, n + 1 + 1)
                    nc.scalar.activation(gate_sig[:], gate_in[:], ACT.Sigmoid).then_inc(gate_sig_done, 1)

                chunks(act, body)

            @block.vector
            def _(dve):
                dve.sem_inc(gate_in_done, 1)

                def layernorm(n, c, turn):
                    dve.wait_ge(x_loaded[c % XS], 16 * (turn + 1))
                    for j in range(TPC):
                        nc.vector.bn_stats(stats[:, j, :], x[:, c % XS, j, :]).then_inc(stats_done, 1)

                def aggregate():
                    for j in range(TPC):
                        nc.vector.bn_aggr(mv[:, j, :], stats[:, j, :]).then_inc(mv_done, 1)

                def normalise(n, c, first=False):
                    dve.wait_ge(rstd_done, 2 * n + 2)
                    if not first:
                        dve.wait_ge(xt_done, n)
                    for j in range(TPC):
                        nc.vector.tensor_scalar(xhat[:, j, :], x[:, c % XS, j, :], mv[:, j, 0:1], rstd[:, j:j + 1],
                                                ALU.subtract, ALU.mult).then_inc(xhat_done, 1)

                def mix(n, c, between=None, first=False):
                    dve.wait_ge(diff_done, n + 1)
                    if not first:
                        dve.wait_ge(xr_low, n)
                    for i, t in ((1, x_k), (0, x_r)):
                        for k in range(KT):
                            nc.vector.scalar_tensor_tensor(t[:, k, :], diff[:, k, :], mixes[:, i, k:k + 1],
                                                           xn[:, c % 2, k, 0:CH], ALU.mult, ALU.add).then_inc(mix_done, 1)
                        if i and between:
                            between()

                def xk_low_of(n):
                    dve.wait_ge(xk_high, n + 1)
                    nc.vector.tensor_tensor(xk_half[:, 1], x_k[:], xk_half[:, 0], ALU.subtract).then_inc(xk_low, 1)

                layernorm(0, 0, 0)
                dve.wait_ge(stats_done, TPC)
                aggregate()
                dve.wait_ge(weights_loaded, 16 * early.loads)
                for t, column, sq in normed:
                    nc.vector.tensor_tensor_reduce(out=sq, in0=t, in1=t, scale=1.0, scalar=0.0, op0=ALU.mult, op1=ALU.add,
                                                   accum_out=sums[:, column:column + 1]).then_inc(squares_done, 1)
                normalise(0, 0, first=True)
                dve.wait_ge(roots_done, 1)
                xn_max, room = float(np.sqrt(DIM)), F16_TARGET / X_TARGET
                nc.vector.tensor_scalar(bound[:, 0:X], roots[:, 0:X], 1e-12, None, ALU.max).then_inc(bound_done, 1)
                nc.vector.tensor_scalar(bound[:, X:X + 1], roots[:, X:X + 1], 2.0 * xn_max * room, xn_max * room, ALU.mult, ALU.add).then_inc(bound_done, 1)
                dve.wait_ge(bound_done, 2)
                nc.vector.tensor_scalar(bound[:, CQ:CKV + 1], bound[:, DQ:DKV + 1], xn_max, None, ALU.mult).then_inc(bound_done, 1)
                nc.vector.tensor_scalar(kr_bound[:], bound[:, WKR:WKR + 1], 2.0 * xn_max, None, ALU.mult).then_inc(bound_done, 1)
                dve.wait_ge(bound_done, 4)
                nc.vector.tensor_scalar(bound[:, Q:Q + 1], bound[:, CQ:CQ + 1], bound[:, WQ:WQ + 1], 2.0, ALU.mult, ALU.mult).then_inc(bound_done, 1)
                nc.vector.tensor_scalar(bound[:, K:K + 1], bound[:, CKV:CKV + 1], bound[:, WUK:WUK + 1], 2.0, ALU.mult, ALU.mult).then_inc(bound_done, 1)
                dve.wait_ge(bound_done, 6)
                nc.vector.tensor_tensor(bound[:, K:K + 1], bound[:, K:K + 1], kr_bound[:], ALU.max).then_inc(bound_done, 1)
                dve.wait_ge(bound_done, 7)
                nc.vector.tensor_scalar(power[:].bitcast(I32), bound[:].bitcast(I32), 0x7F800000, None,
                                        ALU.bitwise_and).then_inc(bound_done, 1)
                dve.wait_ge(bound_done, 8)
                nc.vector.reciprocal(scale[:], power[:]).then_inc(bound_done, 1)
                nc.vector.tensor_scalar(inverse[:], power[:], 1.0 / F16_TARGET, None, ALU.mult).then_inc(bound_done, 1)
                dve.wait_ge(bound_done, 10)
                nc.vector.tensor_scalar(scale[:], scale[:], F16_TARGET, None, ALU.mult).then_inc(bound_done, 1)
                dve.wait_ge(bound_done, 11)
                for weight, operand, result in ((DQ, X, CQ), (DKV, X, CKV), (WQ, CQ, Q), (WUK, CKV, K), (WKR, X, K)):
                    nc.vector.tensor_scalar(factor[:, weight:weight + 1], inverse[:, weight:weight + 1], inverse[:, operand:operand + 1],
                                            scale[:, result:result + 1], ALU.mult, ALU.mult).then_inc(bound_done, 1)
                for weight, operand in ((WUV, CKV), (WR, X), (WK, X)):
                    nc.vector.tensor_scalar(factor[:, weight:weight + 1], inverse[:, weight:weight + 1], inverse[:, operand:operand + 1],
                                            None, ALU.mult).then_inc(bound_done, 1)
                nc.vector.tensor_scalar(score_scale[:], inverse[:, Q:Q + 1], inverse[:, K:K + 1], INV_SQRT, ALU.mult, ALU.mult).then_inc(scale_done, 1)
                layernorm(1, 1, 0)
                dve.wait_ge(stats_done, 2 * TPC)
                dve.wait_ge(scale_done, 1)
                aggregate()
                for j, (w, halves, i) in enumerate(parts):
                    dve.wait_ge(w_high, j + 1)
                    nc.vector.scalar_tensor_tensor(halves[:, 1], w, scale[:, i:i + 1], halves[:, 0], ALU.mult, ALU.subtract).then_inc(w_low, 1)
                mix(0, 0, first=True)
                xk_low_of(0)
                normalise(1, 1)
                dve.wait_ge(late_loaded, 48)

                def body(b, c, left):
                    n, s, t = count(b, c), c % 2, slice(c * CH, (c + 1) * CH)
                    low = slice(LATENT, 2 * LATENT)
                    for i, column in enumerate((DQ, DKV)):
                        dve.wait_ge(lat_high, 2 * n + i + 1)
                        nc.vector.scalar_tensor_tensor(lat[low, i], ps_a[low, i, :], factor[low, column:column + 1], lat[low, i],
                                                       ALU.mult, ALU.subtract).then_inc(lat_low, 1)
                    dve.wait_ge(kr_low, n + 1)
                    dve.wait_ge(kr_mm, n + 1)
                    for t_k, rows, table in ((k_cos, slice(0, D_R), cos), (k_sin, slice(VW, VW + D_R), sin)):
                        nc.vector.scalar_tensor_tensor(t_k[:], ps_t[rows, 0, :], factor[rows, WKR:WKR + 1], table[rows, t],
                                                       ALU.mult, ALU.mult).then_inc(kr_parts, 1)
                    dve.wait_ge(qc_high, n + 1)
                    nc.vector.scalar_tensor_tensor(qc[:, s, 1], ps_c[:], factor[:, WQ:WQ + 1], qc[:, s, 0],
                                                   ALU.mult, ALU.subtract).then_inc(qc_low, 1)
                    for i, (t_q, table) in enumerate(((q_cos, cos), (q_sin, sin))):
                        dve.wait_ge(qr_mm, 2 * n + i + 1)
                        nc.vector.scalar_tensor_tensor(t_q[:], ps_a[:, i, :], factor[:, WQ:WQ + 1], table[:, t],
                                                       ALU.mult, ALU.mult).then_inc(qr_parts, 1)
                    dve.wait_ge(qr_parts, 3 * n + 2)
                    nc.vector.tensor_tensor(q_cos[:], q_cos[:], q_sin[:], ALU.add).then_inc(qr_parts, 1)
                    dve.wait_ge(kc_high, n + 1)
                    nc.vector.scalar_tensor_tensor(kc[:, s, 1], ps_c[:], factor[:, WUK:WUK + 1], kc[:, s, 0],
                                                   ALU.mult, ALU.subtract).then_inc(kc_low, 1)
                    dve.wait_ge(qr_high, n + 1)
                    nc.vector.tensor_tensor(qr[:, s, 1, :], q_cos[:], qr[:, s, 0, :], ALU.subtract).then_inc(qr_low, 1)
                    if left >= 2:
                        layernorm(n + 2, c + 2, b + (c + 2) // XS)
                        dve.wait_ge(stats_done, TPC * (n + 2) + TPC)
                    if left >= 1:
                        mix(n + 1, c + 1, aggregate if left >= 2 else None)
                        xk_low_of(n + 1)
                    if left >= 2:
                        normalise(n + 2, c + 2)
                    dve.wait_ge(kv_mm, n + 1)
                    dve.wait_ge(sig_done, n + 1 + 1)
                    dve.wait_ge(gate_done, n + 1)
                    nc.vector.tensor_tensor(gate_in[:], ps_kv, sig_r[:], ALU.mult).then_inc(gate_in_done, 1)

                chunks(dve, body)

            @block.tensor
            def _(pe):
                pe.wait_ge(consts_set, 3)
                pe.wait_ge(squares_done, NORMS)
                nc.tensor.matmul(ps_a[:, 0, 0:NORMS], ones[:], sums[:], start=True, stop=True).then_inc(sums_done, 1)

                def transposes(n):
                    pe.wait_ge(xhat_done, TPC * n + TPC)
                    for k in range(KT):
                        for j in range(TPC):
                            last = nc.tensor.transpose(ps_t[:, k, j * P:(j + 1) * P], xhat[:, j, k * P:(k + 1) * P], ident[:])
                    last.then_inc(xt_done, 1)

                def products(ps, pairs, terms=((0, 0), (0, 1), (1, 0))):
                    steps = [(l(h), r(g)) for l, r in pairs for h, g in terms]
                    for i, (l, r) in enumerate(steps):
                        mm = nc.tensor.matmul(ps, l, r, start=(i == 0), stop=(i == len(steps) - 1))
                    return mm

                def channels(ps, w, t, columns):
                    return products(ps, [(lambda h, k=k: w[:, h, k, columns], lambda h, k=k: t[:, h, k, :]) for k in range(KT)])

                def tokens(ps, t, w, j):
                    return products(ps, [(lambda h, k=k: t[:, h, k, j * P:(j + 1) * P], lambda h, k=k: w[:, h, k, :]) for k in range(KT)])

                transposes(0)
                pe.wait_ge(roots_done, 1)
                pe.wait_ge(w_low, 3)

                def body(b, c, left):
                    n, s = count(b, c), c % 2
                    pe.wait_ge(val_done, n + 1)
                    pe.wait_ge(xn_low, n + 1)
                    for i, columns in enumerate((LEFT, RIGHT)):
                        channels(ps_a[:, i, :], w_c, xn_half, columns).then_inc(lat_mm, 1)
                    channels(ps_t[0:VW + D_R, 0, :], w_kr, xn_half, slice(None)).then_inc(kr_mm, 1)
                    pe.wait_ge(sig_done, n + 1)
                    pe.wait_ge(xk_low, n + 1)
                    pe.wait_ge(w_low, len(parts))
                    for m in range(KT):
                        mm = channels(ps_b[:, m, :], w_k, xk_half, slice(m * P, (m + 1) * P))
                    mm.then_inc(k_mm, 1)
                    pe.wait_ge(gate_in_done, n + 1)
                    pe.wait_ge(lat_low, 2 * n + 2)
                    both = ((0, 0), (1, 0))
                    for m in range(KT):
                        mm = products(ps_c[:, m, :], [(lambda h: w_q[:, h, m * P:(m + 1) * P], lambda h: lat[:, 0])], both)
                    mm.then_inc(qc_mm, 1)
                    for m in range(2):
                        products(ps_a[:, m, :], [(lambda h: w_q[:, h, DIM + m * P:DIM + (m + 1) * P], lambda h: lat[:, 0])],
                                 both).then_inc(qr_mm, 1)
                    if left >= 1:
                        pe.wait_ge(kr_parts, 2 * n + 2)
                        transposes(n + 1)
                    pe.wait_ge(relu_done, n + 1)
                    pe.wait_ge(xr_low, n + 1)
                    for j in range(TPC):
                        if j == TPC // 2:
                            pe.wait_ge(qc_low, n + 1)
                            for m in range(KT):
                                mm = products(ps_c[:, m, :], [(lambda h: w_uk[:, h, m * P:(m + 1) * P], lambda h: lat[:, 1])], both)
                            mm.then_inc(kc_mm, 1)
                        mm = tokens(ps_r[:, j, :], xr_half, w_r, j)
                    mm.then_inc(r_mm, 1)
                    pe.wait_ge(qr_parts, 3 * n + 2)
                    for j in range(TPC):
                        mm = products(ps_val[:, j, :], [(lambda h: lat[:, 1, j * P:(j + 1) * P], lambda h: w_uv[:, h])], ((0, 0), (0, 1)))
                    mm.then_inc(val_mm, 1)
                    pe.wait_ge(kc_low, n + 1)
                    pe.wait_ge(act_done, n + 1)
                    pe.wait_ge(late_loaded, 48)
                    for j in range(TPC):
                        for k in range(KT):
                            mm = nc.tensor.matmul(ps_kv[:, j, :], act_k[:, k, j * P:(j + 1) * P], w_v[:, k, :],
                                                  start=(k == 0), stop=(k == KT - 1))
                    mm.then_inc(kv_mm, 1)

                chunks(pe, body)


class Operands:
    LOADS = 17

    def __init__(self, ctx, nc, slot):
        self.q = ctx.enter_context(nc.sbuf_tensor(f"c_q{slot}", [KROWS, GH, SEQ], F16))
        self.k = ctx.enter_context(nc.sbuf_tensor(f"c_k{slot}", [KROWS, GH, SEQ], F16))
        self.v = ctx.enter_context(nc.sbuf_tensor(f"c_v{slot}", [P, KEYT, GH * VW], F32))
        self.loaded = ctx.enter_context(nc.semaphore(f"c_loaded{slot}"))


def load_group(sp, d, into, b, g):
    at = 0
    for hq, hk in ((0, 0), (0, 1), (1, 0), (1, 1)):
        for t, name, half in ((into.q, "q", hq), (into.k, "k", hk)):
            src = d[name + "c"][b, half].rearrange("(g h r) t -> g r h t", g=GROUPS, h=GH)[g]
            sp.dma_start(t[at:at + D_H], src).then_inc(into.loaded, 16)
            if name == "q":
                src = d["qr"][b, half].rearrange("(g h r) t -> g r h t", g=GROUPS, h=GH)[g]
            else:
                src = d["kr"][b, half].rearrange("r (o t) -> r o t", o=1).to_broadcast([D_R, GH, SEQ])
            sp.dma_start(t[at + D_H:at + D_QK], src).then_inc(into.loaded, 16)
        at += D_QK
    src = d["v"].rearrange("(b m p) (g e) -> b g p m e", b=BATCH, p=P, g=GROUPS)[b, g]
    sp.dma_start(into.v[:], src).then_inc(into.loaded, 16)


def token_view(t):
    return t.rearrange("(n j p) c -> n p j c", j=TPC, p=P)


def attention(nc, a, d, ident, score_scale, first, ahead):
    tiles = [[kt for j in range(TPC) for kt in [TPC * c + j] + [c * j + f for f in range(c)]] for c in range(CPB)]
    steps = [(s, c, kt) for s in range(2) for c in range(CPB) for kt in tiles[c]]
    N = len(steps)
    starts = [i for i, (s, c, kt) in enumerate(steps) if kt == tiles[c][0]]
    ends = [i for i, (s, c, kt) in enumerate(steps) if kt == tiles[c][-1]]
    AHEAD = 3
    LEAD = 3
    NC = len(ends)
    PAIRS = BATCH * GROUPS // 2
    HALF = GH // 2
    NBUF, NPROB = 3, 4
    bufs = [h % NBUF for h in range(2 * N)]
    if bufs[-1] == 0:
        bufs[-2], bufs[-1] = bufs[-1], bufs[-2]
    before = []
    for h in range(2 * N):
        back = [g for g in range(h - 2 * N, h) if bufs[g] == bufs[h]]
        before.append(back[-1])
    diags = [i for i, (s, c, kt) in enumerate(steps) if kt >= TPC * c]

    def offset(i):
        _, c, kt = steps[i]
        return max(0, kt - TPC * c) * P

    with ExitStack() as ctx:
        def sb(name, shape, dt=F32):
            return ctx.enter_context(nc.sbuf_tensor(name, shape, dt))

        def sem(name):
            return ctx.enter_context(nc.semaphore(name))

        slots = (first, Operands(ctx, nc, 1))
        probs = sb("c_probs", [P, NPROB, GH, CH])
        causal = sb("c_causal", [P, HALF, P])
        o_t = sb("c_ot", [P, 2, CH])
        recip = sb("c_recip", [P, 2, TPC, GH])
        attn = sb("c_attn", [P, 2, TPC, GH, D_H])
        ps_s = ctx.enter_context(nc.psum_tensor("c_ps_s", [P, NBUF, HALF, CH], F32))
        ps_o = ctx.enter_context(nc.psum_tensor("c_ps_o", [P, 2, CH], F32))
        ps_tok = ps_o[:].rearrange("p a (j h e) -> p a j h e", j=TPC, h=GH)

        causal_set = sem("c_causal_set")
        stored = [sem(f"c_stored{i}") for i in range(2)]
        qk_done = sem("c_qk_done")
        exp_done = sem("c_exp_done")
        clip_done = sem("c_clip_done")
        mask_done = sem("c_mask_done")
        pv_done = sem("c_pv_done")
        ot_done = sem("c_ot_done")
        tok_done = sem("c_tok_done")
        recip_done = sem("c_recip_done")
        norm_done = sem("c_norm_done")

        def pairs(eng, body):
            with eng.Fori(0, PAIRS - 1) as i:
                body(i, False)
            body(PAIRS - 1, True)

        attn_v = d["attn"].rearrange("(b c j p) (g e) -> b c g p j e", c=CPB, j=TPC, p=P, g=GROUPS)

        with nc.Block() as block:
            @block.sync
            def _(sp):
                for s in range(2):
                    sp.sem_inc(stored[s], 16)

                load_group(sp, d, slots[1], 0, 1)
                for n in range(NCH):
                    sp.dma_start(ahead.gate[:, n], token_view(d["gate"])[n]).then_inc(ahead.rest_loaded, 16)
                sp.dma_start(ahead.w_o[:], a["W_O"].rearrange("(k p) n -> p k n", p=P)).then_inc(ahead.rest_loaded, 16)

                def body(i, last):
                    for s in range(2):
                        b, g = (i * 2 + s) // GROUPS, (i * 2 + s) % GROUPS
                        for c in range(CPB):
                            e = s * CPB + c
                            sp.wait_ge(norm_done, NC * i + e + 1 + 2)
                            sp.dma_start(attn_v[b, c, g], attn[:, c % 2].rearrange("p j h e -> p j (h e)")).then_inc(stored[c % 2], 16)
                        if not last:
                            sp.wait_ge(pv_done, N * i + (s + 1) * N // 2 + NPROB)
                            load_group(sp, d, slots[s], ((i + 1) * 2 + s) // GROUPS, ((i + 1) * 2 + s) % GROUPS)
                    if last:
                        for s in range(2):
                            sp.wait_ge(stored[s], 16 * (GROUPS * CPB // 2) + 16)
                        for n in range(ahead.SLOTS):
                            sp.dma_start(ahead.attn[:, n], token_view(d["attn"])[n]).then_inc(ahead.attn_loaded[n], 16)

                pairs(sp, body)
                for s in range(2):
                    sp.wait_ge(stored[s], 16 * BATCH * GROUPS * CPB // 2 + 16)

            @block.scalar
            def _(act):
                act.sem_inc(exp_done, NBUF)
                unscale = act.alloc_register("c_unscale")
                act.load(unscale, score_scale[0:1, 0:1].bitcast(I32))

                def body(i, last):
                    for st in range(N):
                        o = offset(st)
                        for h in range(2):
                            hs = 2 * st + h
                            if h == 0:
                                act.wait_ge(pv_done, N * i + st + 1)
                            act.wait_ge(qk_done, 2 * N * i + hs + 1)
                            nc.scalar.activation(probs[:, st % NPROB, h * HALF:(h + 1) * HALF, o:CH], ps_s[:, bufs[hs], :, o:CH],
                                                 ACT.Exp, scale=unscale).then_inc(exp_done, 1)

                pairs(act, body)

            @block.vector
            def _(dve):
                dve.sem_inc(norm_done, 2)

                def rows_out(i, e):
                    dve.wait_ge(pv_done, N * i + ends[e] + 1 + NPROB)
                    nc.vector.tensor_copy(o_t[:, e % 2, :], ps_o[:, e % 2, :]).then_inc(ot_done, 1)

                def normalise(i, e):
                    a = e % 2
                    dve.wait_ge(tok_done, NC * i + e + 1)
                    nc.vector.reciprocal(recip[:, a], ps_tok[:, a, :, :, D_H]).then_inc(recip_done, 1)
                    dve.wait_ge(stored[a], 16 * (NC // 2 * i + e // 2) + 16)
                    dve.wait_ge(recip_done, NC * i + e + 1)
                    nc.vector.tensor_tensor(attn[:, a], ps_tok[:, a, :, :, 0:D_H],
                                            recip[:, a].rearrange("p j (h o) -> p j h o", o=1).to_broadcast([P, TPC, GH, D_H]),
                                            ALU.mult).then_inc(norm_done, 1)

                def clip(i, st):
                    o = offset(st)
                    for h in range(2):
                        hs = 2 * st + h
                        dve.wait_ge(exp_done, 2 * N * i + hs + 1 + NBUF)
                        tile = probs[:, st % NPROB, h * HALF:(h + 1) * HALF, o:CH]
                        nc.vector.tensor_scalar(tile, tile, P_MAX, P_MIN, ALU.min, ALU.max).then_inc(clip_done, 1)

                for st in range(AHEAD):
                    clip(0, st)
                for st in range(LEAD):
                    clip(0, st + AHEAD)

                def body(i, last):
                    todo = {}
                    for e, st in enumerate(ends):
                        todo.setdefault(st, []).append((rows_out, e))
                        todo.setdefault(st + 3, []).append((normalise, e))
                    for st in range(LEAD, N + LEAD):
                        if st + AHEAD < N:
                            clip(i, st + AHEAD)
                        elif not last:
                            clip(i + 1, st + AHEAD - N)
                        for task, e in todo.get(st, []):
                            task(i, e)

                pairs(dve, body)

            @block.gpsimd
            def _(pool):
                pool.memset(causal[:], 1.0).then_inc(causal_set, 1)
                pool.wait_ge(causal_set, 1)
                pool.affine_select(out=causal[:], in_=causal[:], compare_op=ALU.is_ge, fill=0.0, base=0,
                                   pattern=[[0, HALF], [1, P]], channel_multiplier=-1).then_inc(causal_set, 1)
                pool.wait_ge(causal_set, 2)

                def body(i, last):
                    for st in diags:
                        o = offset(st)
                        for h in range(2):
                            pool.wait_ge(clip_done, 2 * N * i + 2 * st + h + 1)
                            tile = probs[:, st % NPROB, h * HALF:(h + 1) * HALF, o:o + P]
                            nc.gpsimd.tensor_tensor(tile, tile, causal[:], ALU.mult).then_inc(mask_done, 1)

                pairs(pool, body)

            @block.tensor
            def _(pe):
                pe.sem_inc(pv_done, NPROB)

                def scores(i, st):
                    s, c, kt = steps[st]
                    o = offset(st)
                    if st in starts and c == 0:
                        pe.wait_ge(slots[s].loaded, 16 * Operands.LOADS * (i + 1))
                    for h in range(2):
                        hs = 2 * st + h
                        pe.wait_ge(exp_done, 2 * N * i + before[hs] + 1 + NBUF)
                        for j in range(HALF):
                            mm = nc.tensor.matmul(ps_s[:, bufs[hs], j, o:CH], slots[s].k[:, h * HALF + j, kt * P:(kt + 1) * P],
                                                  slots[s].q[:, h * HALF + j, c * CH + o:(c + 1) * CH], start=True, stop=True)
                        mm.then_inc(qk_done, 1)

                def values(i, st):
                    s, c, kt = steps[st]
                    o = offset(st)
                    e = s * CPB + c
                    if st in starts:
                        pe.wait_ge(norm_done, NC * i + e - 2 + 1 + 2)
                    if st in diags:
                        pe.wait_ge(mask_done, 2 * len(diags) * i + 2 * diags.index(st) + 2)
                    else:
                        pe.wait_ge(clip_done, 2 * N * i + 2 * st + 2)
                    for j in range(GH):
                        mm = nc.tensor.matmul(ps_o[j * VW:(j + 1) * VW, c % 2, o:CH], slots[s].v[:, kt, j * VW:(j + 1) * VW],
                                              probs[:, st % NPROB, j, o:CH], start=(st in starts), stop=(st in ends),
                                              tile_position=(0, j * VW))
                    mm.then_inc(pv_done, 1)

                def tokens(i, e):
                    pe.wait_ge(ot_done, NC * i + e + 1)
                    for j in range(TPC):
                        mm = nc.tensor.transpose(ps_o[:, e % 2, j * P:(j + 1) * P], o_t[:, e % 2, j * P:(j + 1) * P], ident[:])
                    mm.then_inc(tok_done, 1)

                for st in range(AHEAD):
                    scores(0, st)
                for st in range(LEAD):
                    scores(0, st + AHEAD)
                    values(0, st)

                def body(i, last):
                    todo = {}
                    for e, st in enumerate(ends):
                        todo.setdefault(st + 2, []).append(e)
                    for st in range(LEAD, N + LEAD):
                        if st + AHEAD < N:
                            scores(i, st + AHEAD)
                        elif not last:
                            scores(i + 1, st + AHEAD - N)
                        if st < N:
                            values(i, st)
                        elif not last:
                            values(i + 1, st - N)
                        for e in todo.get(st, []):
                            tokens(i, e)

                pairs(pe, body)


class Ahead:
    SLOTS = 4

    def __init__(self, ctx, nc):
        def sb(name, shape):
            return ctx.enter_context(nc.sbuf_tensor(name, shape, F32))

        def sem(name):
            return ctx.enter_context(nc.semaphore(name))

        self.w_o = sb("d_wo", [P, KT, DIM])
        self.gate = sb("d_gate", [P, NCH, TPC, DIM])
        self.attn = sb("d_attn", [P, self.SLOTS, TPC, DIM])
        self.rest_loaded = sem("d_rest_loaded")
        self.attn_loaded = [sem(f"d_attn_loaded{i}") for i in range(self.SLOTS)]


def layer1_output(nc, d, ident, ahead, out):
    with ExitStack() as ctx:
        def sb(name, shape, dt=F32):
            return ctx.enter_context(nc.sbuf_tensor(name, shape, dt))

        def sem(name):
            return ctx.enter_context(nc.semaphore(name))

        SLOTS = ahead.SLOTS
        w_o, gate, attn, attn_loaded = ahead.w_o, ahead.gate, ahead.attn, ahead.attn_loaded
        x1 = sb("d_x1", [P, SLOTS, TPC, DIM])
        attn_t = sb("d_attn_t", [P, 2, KT, CH])
        prod = sb("d_prod", [P, SLOTS, TPC, DIM])
        ps_t = ctx.enter_context(nc.psum_tensor("d_ps_t", [P, 2, KT, CH], F32))
        ps_o = ctx.enter_context(nc.psum_tensor("d_ps_o", [P, 2, TPC, DIM], F32))

        x1_loaded = [sem(f"d_x1_loaded{i}") for i in range(SLOTS)]
        stored = [sem(f"d_stored{i}") for i in range(SLOTS)]
        t_mm = sem("d_t_mm")
        t_done = sem("d_t_done")
        out_mm = sem("d_out_mm")
        prod_done = sem("d_prod_done")
        sum_done = sem("d_sum_done")

        attn_v, x1_v, out_v = token_view(d["attn"]), token_view(d["x1"]), token_view(out)
        ROUNDS = NCH // SLOTS

        def rounds(eng, body):
            with eng.Fori(0, ROUNDS - 1) as i:
                body(i, False)
            body(ROUNDS - 1, True)

        with nc.Block() as block:
            @block.sync
            def _(sp):
                for s in range(SLOTS):
                    sp.sem_inc(stored[s], 16)

                def load_x1(n, s):
                    sp.dma_start(x1[:, s], x1_v[n]).then_inc(x1_loaded[s], 16)

                for s in range(SLOTS):
                    load_x1(s, s)

                def body(i, last):
                    for s in range(SLOTS):
                        n = SLOTS * i + s
                        sp.wait_ge(sum_done, n + 1)
                        sp.dma_start(out_v[n], prod[:, s]).then_inc(stored[s], 16)
                        if not last:
                            sp.dma_start(attn[:, s], attn_v[n + SLOTS]).then_inc(attn_loaded[s], 16)
                            load_x1(n + SLOTS, s)

                rounds(sp, body)
                for s in range(SLOTS):
                    sp.wait_ge(stored[s], 16 * ROUNDS + 16)

            @block.tensor
            def _(pe):
                pe.sem_inc(out_mm, 2)
                pe.wait_ge(ahead.rest_loaded, 16 * NCH + 16)

                def transposes(i, s):
                    pe.wait_ge(attn_loaded[s], 16 * i + 16)
                    for k in range(KT):
                        for j in range(TPC):
                            mm = nc.tensor.transpose(ps_t[:, s % 2, k, j * P:(j + 1) * P], attn[:, s, j, k * P:(k + 1) * P], ident[:])
                    mm.then_inc(t_mm, 1)

                def product(i, s):
                    n = SLOTS * i + s
                    pe.wait_ge(t_done, n + 1)
                    pe.wait_ge(prod_done, n + 1)
                    for j in range(TPC):
                        for k in range(KT):
                            mm = nc.tensor.matmul(ps_o[:, s % 2, j, :], attn_t[:, s % 2, k, j * P:(j + 1) * P], w_o[:, k, :],
                                                  start=(k == 0), stop=(k == KT - 1))
                    mm.then_inc(out_mm, 1)

                transposes(0, 0)

                def body(i, last):
                    for s in range(SLOTS):
                        if s + 1 < SLOTS:
                            transposes(i, s + 1)
                        elif not last:
                            transposes(i + 1, 0)
                        product(i, s)

                rounds(pe, body)

            @block.scalar
            def _(act):
                def body(i, last):
                    for s in range(SLOTS):
                        n = SLOTS * i + s
                        act.wait_ge(t_mm, n + 1)
                        act.wait_ge(out_mm, n + 1)
                        nc.scalar.activation(attn_t[:, s % 2], ps_t[:, s % 2], ACT.Copy).then_inc(t_done, 1)

                rounds(act, body)

            @block.vector
            def _(dve):
                dve.sem_inc(prod_done, 2)
                dve.wait_ge(ahead.rest_loaded, 16 * NCH + 16)

                def body(i, last):
                    for s in range(SLOTS):
                        n = SLOTS * i + s
                        dve.wait_ge(x1_loaded[s], 16 * i + 16)
                        dve.wait_ge(out_mm, n + 1 + 2)
                        dve.wait_ge(stored[s], 16 * i + 16)
                        nc.vector.tensor_tensor(prod[:, s], ps_o[:, s % 2], gate[:, n], ALU.mult).then_inc(prod_done, 1)
                        dve.wait_ge(prod_done, n + 1 + 2)
                        nc.vector.tensor_tensor(prod[:, s], prod[:, s], x1[:, s], ALU.add).then_inc(sum_done, 1)

                rounds(dve, body)


def build(nc, a, out):
    d = scratch(nc)
    with ExitStack() as ctx:
        ident = ctx.enter_context(nc.sbuf_tensor("ident", [P, P], F32))
        early_ctx = ctx.enter_context(ExitStack())
        early = Early(early_ctx, nc)
        layer0(nc, a, d["x1"], ident, early)
        score_scale = ctx.enter_context(nc.sbuf_tensor("score_scale", [P, 1], F32))
        first = Operands(ctx, nc, 0)
        layer1_projections(nc, a, d, ident, early, score_scale, first)
        early_ctx.close()
        ahead = Ahead(ctx, nc)
        attention(nc, a, d, ident, score_scale, first, ahead)
        layer1_output(nc, d, ident, ahead, out)


def rotary_tables():
    inv = np.float32(10000.0) ** (-np.arange(0, D_R, 2, dtype=np.float32) / np.float32(D_R))
    ang = np.arange(SEQ, dtype=np.float32)[None, :] * inv.astype(np.float32)[:, None]
    cos = np.repeat(np.cos(ang), 2, axis=0)
    sin = np.repeat(np.sin(ang), 2, axis=0)
    sin[0::2] *= -1
    return (np.ascontiguousarray(np.tile(t, (HEADS, 1)).astype(np.float32)) for t in (cos, sin))


def layout(inputs):
    i = {k: np.asarray(v) for k, v in inputs.items()}
    cols = lambda v: np.reshape(v, (-1, P)).T
    swap = lambda w: np.reshape(np.reshape(w, (w.shape[0], -1, 2))[:, :, ::-1], w.shape)
    w_qr, w_kr = i["L1_attn_W_QR"], i["L1_attn_W_KR"]
    cos, sin = rotary_tables()
    arrays = {
        "x": np.reshape(i["L0_attn_x"], (TOKENS, DIM)),
        "ident": np.eye(P, dtype=np.float32),
        "WrT": i["L0_attn_Wr"].T, "WkT": i["L0_attn_Wk"].T, "WvT": i["L0_attn_Wv"].T, "WoT": i["L0_attn_Wo"].T,
        "W1": i["L0_ffn_W1"], "W2": i["L0_ffn_W2"], "b1": cols(i["L0_ffn_b1"]), "b2": i["L0_ffn_b2"],
        "time_decay": cols(i["L0_attn_time_decay"]), "time_first": cols(i["L0_attn_time_first"]),
        "mixes": np.concatenate([cols(i["L0_attn_mix_" + n]) for n in "rkv"], axis=1),
        "Wc": np.concatenate([i["L1_attn_W_DQ"]] * 2 + [i["L1_attn_W_DKV"]] * 2, axis=1),
        "Wkr": np.concatenate([w_kr] * (VW // D_R) + [swap(w_kr)], axis=1),
        "Wq": np.concatenate([np.concatenate([i["L1_attn_W_UQ"], w_qr, swap(w_qr)], axis=1)] * 2, axis=0),
        "Wuk": np.concatenate([i["L1_attn_W_UK"]] * 2, axis=0),
        "Wuv": np.concatenate([i["L1_attn_W_UV"]] * 2, axis=0),
        "W_O": i["L1_attn_W_O"],
        "W1rT": i["L1_ffn_W_r"].T, "W1kT": i["L1_ffn_W_k"].T, "W1vT": i["L1_ffn_W_v"].T,
        "mixes1": np.concatenate([cols(i["L1_ffn_mu_r"]), cols(i["L1_ffn_mu_k"])], axis=1),
        "cos": cos, "sin": sin,
    }
    return {k: np.ascontiguousarray(v) for k, v in arrays.items()}


def kernel(**inputs):
    import concourse.bacc as bacc
    from concourse.bass_utils import run_bass_kernel_spmd

    nc = bacc.Bacc("TRN2", target_bir_lowering=False, num_devices=1)
    arrays = layout(inputs)
    a = {k: nc.dram_tensor(f"in_{k}", list(v.shape), mybir.dt.from_np(v.dtype), kind="ExternalInput").ap() for k, v in arrays.items()}
    out = nc.dram_tensor("out", [TOKENS, DIM], F32, kind="ExternalOutput").ap()
    build(nc, a, out)
    r = run_bass_kernel_spmd(nc, [{f"in_{k}": v for k, v in arrays.items()}], core_ids=[0])
    return r.results[0]["out"].reshape(BATCH, SEQ, DIM)
```
